# Optimizing a Trainium2 kernel written in Bass

```python
import numpy as np
import jax
import jax.numpy as jnp

def _softmax(x, axis=-1):
    return jax.nn.softmax(x, axis=axis)

def _gelu(x):
    return jax.nn.gelu(x, approximate=True)

def _silu(x):
    return jax.nn.silu(x)

def _sigmoid(x):
    return jax.nn.sigmoid(x)

def _layernorm(x, axis=-1, eps=1e-05):
    m = jnp.mean(x, axis=axis, keepdims=True)
    v = jnp.var(x, axis=axis, keepdims=True)
    return (x - m) / jnp.sqrt(v + eps)

def _scatter_add(tgt, idx, src, axis=0):
    return tgt.at[idx].add(src)

def _segment_sum(src, seg, n):
    return jax.ops.segment_sum(src, seg, n)
kernel_name = 'mk_adj_resnorm_d4_adj_r2_db924e'

def setup_inputs(seed: int=0):
    np.random.seed(seed)
    _w = jnp.asarray

    def _rec_inputs():
        import jax
        import jax.numpy as jnp
        _gk = jax.random.key(seed)
        x = 0.5 + 0.2887 * jax.random.normal(jax.random.fold_in(_gk, 1), (1354, 512), jnp.float32)
        _a = jax.random.bernoulli(jax.random.fold_in(_gk, 2), 0.00590842, (1354, 1354))
        _a = jnp.logical_or(_a, jnp.eye(1354, dtype=bool))
        _af = _a.astype(jnp.float32)
        _af = _af * jax.random.uniform(jax.random.fold_in(_gk, 3), (1354, 1354), jnp.float32, 0.05, 1)
        adj = _af
        return (x, adj)
    x, adj = _rec_inputs()

    def _L0_gnn_setup():
        import jax, jax.numpy as jnp
        import numpy as np
        NBITS = 4
        N_NODES = 4096
        IN_F = 512
        OUT_F = 512

        def _act_quant(x, alpha, b):
            n = float(2 ** b - 1)
            xd = x / alpha
            xc = jnp.minimum(xd, 1.0)
            xq = jnp.round(xc * n) / n
            return xq * alpha

        def _weight_quant(w, alpha, b):
            n = float(2 ** b - 1)
            wd = w / alpha
            wc = jnp.clip(wd, -1.0, 1.0)
            wq = jnp.round(jnp.abs(wc) * n) / n * jnp.sign(wc)
            return wq * alpha
        key = jax.random.key(seed)
        k1, k2, k3 = jax.random.split(key, 3)
        stdv = 1.0 / np.sqrt(OUT_F)
        inp = {'input': jax.random.uniform(k1, (N_NODES, IN_F), dtype=jnp.float32), 'adj': jax.random.uniform(k2, (N_NODES, N_NODES), dtype=jnp.float32), 'adj_scaling_factor': jnp.float32(2.0), 'weight': jax.random.uniform(k3, (IN_F, OUT_F), minval=-stdv, maxval=stdv, dtype=jnp.float32), 'wgt_alpha': jnp.float32(3.0), 'act_alpha': jnp.float32(1.0), 'act_alpha2': jnp.float32(1.0)}
        return inp
    _L0_gnn_all = _L0_gnn_setup()
    _L0_gnn_in = {k: v for k, v in _L0_gnn_all.items() if k in ('adj_scaling_factor', 'weight', 'wgt_alpha', 'act_alpha', 'act_alpha2')}
    del _L0_gnn_all

    def _L1_gnn_setup():
        import jax, jax.numpy as jnp
        import numpy as np
        N = 4096
        D = 512

        def adjacent_mat(adj):
            adj = adj + jnp.eye(adj.shape[0], dtype=adj.dtype)
            deg = jnp.sum(adj, axis=1)
            dinv = jnp.where(deg > 0, deg ** (-0.5), 0.0).astype(adj.dtype)
            return dinv[:, None] * adj * dinv[None, :]
        key = jax.random.key(seed)
        k1, k2 = jax.random.split(key)
        x = jax.random.normal(k1, (N, D), dtype=jnp.float32)
        Coefficient2 = 1e-08 * jnp.ones((N, N), dtype=jnp.float32)
        A = jax.random.uniform(k2, (N, N), dtype=jnp.float32)
        return {'x': x, 'Coefficient2': Coefficient2, 'A': A}
    _L1_gnn_all = _L1_gnn_setup()
    _L1_gnn_in = {k: v for k, v in _L1_gnn_all.items() if k in ()}
    del _L1_gnn_all

    def _L2_gnn_setup():
        import jax, jax.numpy as jnp
        import numpy as np
        ALPHA = 0.2
        NEG = -9000000000000000.0
        N, NFEAT, NHID, NHEADS = (2048, 512, 64, 8)
        EMB = NHID * NHEADS
        key = jax.random.key(seed)
        ks = jax.random.split(key, 16)
        x = jax.random.normal(ks[0], (N, NFEAT), dtype=jnp.float32)
        adj = (jax.random.uniform(ks[1], (N, N)) < 0.01).astype(jnp.float32)
        adj = jnp.maximum(adj, jnp.eye(N, dtype=jnp.float32))
        s = 0.05
        W = jax.random.normal(ks[2], (NHEADS, NFEAT, NHID), dtype=jnp.float32) * s
        a1 = jax.random.normal(ks[3], (NHEADS, NHID), dtype=jnp.float32) * s
        a2 = jax.random.normal(ks[4], (NHEADS, NHID), dtype=jnp.float32) * s
        W1 = jax.random.normal(ks[5], (EMB // 2, EMB), dtype=jnp.float32) * s
        b1 = jnp.zeros((EMB // 2,), dtype=jnp.float32)
        W2 = jax.random.normal(ks[6], (NFEAT // 4, EMB // 2), dtype=jnp.float32) * s
        b2 = jnp.zeros((NFEAT // 4,), dtype=jnp.float32)
        W3 = jax.random.normal(ks[7], (NFEAT // 2, NFEAT // 4), dtype=jnp.float32) * s
        b3 = jnp.zeros((NFEAT // 2,), dtype=jnp.float32)
        W4 = jax.random.normal(ks[8], (NFEAT, NFEAT // 2), dtype=jnp.float32) * s
        b4 = jnp.zeros((NFEAT,), dtype=jnp.float32)
        return {'x': x, 'adj': adj, 'W': W, 'a1': a1, 'a2': a2, 'W1': W1, 'b1': b1, 'W2': W2, 'b2': b2, 'W3': W3, 'b3': b3, 'W4': W4, 'b4': b4}
    _L2_gnn_all = _L2_gnn_setup()
    _L2_gnn_in = {k: v for k, v in _L2_gnn_all.items() if k in ('W', 'a1', 'a2', 'W1', 'b1', 'W2', 'b2', 'W3', 'b3', 'W4', 'b4')}
    del _L2_gnn_all

    def _L3_gnn_setup():
        import jax, jax.numpy as jnp
        import numpy as np
        import math
        SENT_DIM = 512
        N_SENT = 2048
        key = jax.random.key(seed)
        ks = jax.random.split(key, 8)
        D = SENT_DIM
        s = 1.0 / math.sqrt(D)
        return {'sent_embed': jax.random.normal(ks[0], (N_SENT, D), dtype=jnp.float32), 'adj_tensor': jax.random.randint(ks[1], (N_SENT, N_SENT), 0, 2).astype(jnp.float32), 'W_q': jax.random.uniform(ks[2], (D, D), jnp.float32, -s, s), 'b_q': jax.random.uniform(ks[3], (D,), jnp.float32, -s, s), 'W_k': jax.random.uniform(ks[4], (D, D), jnp.float32, -s, s), 'b_k': jax.random.uniform(ks[5], (D,), jnp.float32, -s, s), 'W_v': jax.random.uniform(ks[6], (D, D), jnp.float32, -s, s), 'b_v': jax.random.uniform(ks[7], (D,), jnp.float32, -s, s)}
    _L3_gnn_all = _L3_gnn_setup()
    _L3_gnn_in = {k: v for k, v in _L3_gnn_all.items() if k in ('W_q', 'b_q', 'W_k', 'b_k', 'W_v', 'b_v')}
    del _L3_gnn_all
    return {'x': x, 'adj': adj, 'L0_gnn_adj_scaling_factor': _L0_gnn_in['adj_scaling_factor'], 'L0_gnn_weight': _L0_gnn_in['weight'], 'L0_gnn_wgt_alpha': _L0_gnn_in['wgt_alpha'], 'L0_gnn_act_alpha': _L0_gnn_in['act_alpha'], 'L0_gnn_act_alpha2': _L0_gnn_in['act_alpha2'], 'L2_gnn_W': _L2_gnn_in['W'], 'L2_gnn_a1': _L2_gnn_in['a1'], 'L2_gnn_a2': _L2_gnn_in['a2'], 'L2_gnn_W1': _L2_gnn_in['W1'], 'L2_gnn_b1': _L2_gnn_in['b1'], 'L2_gnn_W2': _L2_gnn_in['W2'], 'L2_gnn_b2': _L2_gnn_in['b2'], 'L2_gnn_W3': _L2_gnn_in['W3'], 'L2_gnn_b3': _L2_gnn_in['b3'], 'L2_gnn_W4': _L2_gnn_in['W4'], 'L2_gnn_b4': _L2_gnn_in['b4'], 'L3_gnn_W_q': _L3_gnn_in['W_q'], 'L3_gnn_b_q': _L3_gnn_in['b_q'], 'L3_gnn_W_k': _L3_gnn_in['W_k'], 'L3_gnn_b_k': _L3_gnn_in['b_k'], 'L3_gnn_W_v': _L3_gnn_in['W_v'], 'L3_gnn_b_v': _L3_gnn_in['b_v']}

def reference(x, adj, L0_gnn_adj_scaling_factor, L0_gnn_weight, L0_gnn_wgt_alpha, L0_gnn_act_alpha, L0_gnn_act_alpha2, L2_gnn_W, L2_gnn_a1, L2_gnn_a2, L2_gnn_W1, L2_gnn_b1, L2_gnn_W2, L2_gnn_b2, L2_gnn_W3, L2_gnn_b3, L2_gnn_W4, L2_gnn_b4, L3_gnn_W_q, L3_gnn_b_q, L3_gnn_W_k, L3_gnn_b_k, L3_gnn_W_v, L3_gnn_b_v):
    import jax
    import jax.numpy as jnp

    def _L0_gnn_ref(input, adj, adj_scaling_factor, weight, wgt_alpha, act_alpha, act_alpha2):
        import jax, jax.numpy as jnp
        import numpy as np
        NBITS = 4
        N_NODES = 4096
        IN_F = 512
        OUT_F = 512

        def _act_quant(x, alpha, b):
            n = float(2 ** b - 1)
            xd = x / alpha
            xc = jnp.minimum(xd, 1.0)
            xq = jnp.round(xc * n) / n
            return xq * alpha

        def _weight_quant(w, alpha, b):
            n = float(2 ** b - 1)
            wd = w / alpha
            wc = jnp.clip(wd, -1.0, 1.0)
            wq = jnp.round(jnp.abs(wc) * n) / n * jnp.sign(wc)
            return wq * alpha
        bit = NBITS
        wb = bit - 1
        mean = jax.lax.stop_gradient(jnp.mean(weight))
        std = jax.lax.stop_gradient(jnp.std(weight, ddof=1))
        w_norm = (weight - mean) / std
        weight_q = _weight_quant(w_norm, wgt_alpha, wb)
        x = _act_quant(input, act_alpha, bit)
        wgt_delta = wgt_alpha / (2 ** (bit - 1) - 1)
        act_delta = act_alpha / (2 ** bit - 1)
        support = jnp.matmul(x / act_delta, weight_q / wgt_delta)
        support = support * act_delta * wgt_delta
        support = jax.nn.relu(support)
        support_q = _act_quant(support, act_alpha2, bit)
        support_delta = act_alpha2 / (2 ** bit - 1)
        output = jnp.matmul(adj / adj_scaling_factor, support_q / support_delta)
        return output * adj_scaling_factor * support_delta

    def _L1_gnn_ref(x, Coefficient2, A):
        import jax, jax.numpy as jnp
        import numpy as np
        N = 4096
        D = 512

        def adjacent_mat(adj):
            adj = adj + jnp.eye(adj.shape[0], dtype=adj.dtype)
            deg = jnp.sum(adj, axis=1)
            dinv = jnp.where(deg > 0, deg ** (-0.5), 0.0).astype(adj.dtype)
            return dinv[:, None] * adj * dinv[None, :]
        A_c = jax.lax.stop_gradient(A)
        adj = adjacent_mat((A_c + A_c.T) * 0.5)
        y = Coefficient2 @ adj
        y = y @ x
        return y

    def _L2_gnn_ref(x, adj, W, a1, a2, W1, b1, W2, b2, W3, b3, W4, b4):
        import jax, jax.numpy as jnp
        import numpy as np
        ALPHA = 0.2
        NEG = -9000000000000000.0
        N, NFEAT, NHID, NHEADS = (2048, 512, 64, 8)
        EMB = NHID * NHEADS
        Wh = jnp.einsum('nf,hfd->hnd', x, W)
        e_src = jnp.einsum('hnd,hd->hn', Wh, a1)
        e_dst = jnp.einsum('hnd,hd->hn', Wh, a2)
        e = jax.nn.leaky_relu(e_src[:, :, None] + e_dst[:, None, :], ALPHA)
        e = jnp.where(adj[None] > 0, e, NEG)
        att = jax.nn.softmax(e, axis=-1)
        h = jnp.einsum('hnm,hmd->hnd', att, Wh)
        h = jax.nn.elu(h)
        enc = jnp.transpose(h, (1, 0, 2)).reshape(x.shape[0], -1)
        out = jax.nn.relu(enc @ W1.T + b1)
        out = jax.nn.relu(out @ W2.T + b2)
        out = jax.nn.relu(out @ W3.T + b3)
        out = out @ W4.T + b4
        return out

    def _L3_gnn_ref(sent_embed, adj_tensor, W_q, b_q, W_k, b_k, W_v, b_v):
        import jax, jax.numpy as jnp
        import numpy as np
        import math
        SENT_DIM = 512
        N_SENT = 2048
        q = sent_embed @ W_q.T + b_q
        k = sent_embed @ W_k.T + b_k
        v = sent_embed @ W_v.T + b_v
        scale = 1.0 / math.sqrt(sent_embed.shape[-1])
        z = scale * (q @ k.T)
        spare_z = z * adj_tensor
        spare_z = jnp.where(spare_z == 0.0, jnp.asarray(-10000.0, spare_z.dtype), spare_z)
        attn = jax.nn.softmax(spare_z, axis=1)
        out = attn @ v
        return jax.nn.relu(out)
    x = _layernorm(x + _L0_gnn_ref(x, adj, L0_gnn_adj_scaling_factor, L0_gnn_weight, L0_gnn_wgt_alpha, L0_gnn_act_alpha, L0_gnn_act_alpha2), axis=-1)
    x = _layernorm(x + _L1_gnn_ref(x, adj, adj), axis=-1)
    x = _layernorm(x + _L2_gnn_ref(x, adj, L2_gnn_W, L2_gnn_a1, L2_gnn_a2, L2_gnn_W1, L2_gnn_b1, L2_gnn_W2, L2_gnn_b2, L2_gnn_W3, L2_gnn_b3, L2_gnn_W4, L2_gnn_b4), axis=-1)
    x = _layernorm(x + _L3_gnn_ref(x, adj, L3_gnn_W_q, L3_gnn_b_q, L3_gnn_W_k, L3_gnn_b_k, L3_gnn_W_v, L3_gnn_b_v), axis=-1)
    return x

_drawn_inputs = setup_inputs


def setup_inputs(seed=0):
    import zlib

    import numpy as np

    out = dict(_drawn_inputs(seed))
    spreads = {'L2_gnn_b1': (0.0, 0.587),
     'L2_gnn_b2': (0.0, 0.365),
     'L2_gnn_b3': (0.0, 0.1),
     'L2_gnn_b4': (0.0, 0.1)}
    factors = {'L2_gnn_a1': 200.0,
     'L2_gnn_a2': 200.0,
     'L3_gnn_W_q': 8.0,
     'L3_gnn_b_q': 200.0,
     'L3_gnn_W_k': 8.0,
     'L3_gnn_b_k': 200.0,
     'L3_gnn_b_v': 3.34}
    for name, (base, spread) in spreads.items():
        noise = np.random.default_rng([zlib.crc32(name.encode()), seed]).standard_normal(out[name].shape)
        drawn = base * np.exp(spread * noise) if base else spread * noise
        out[name] = jnp.asarray(drawn.astype(out[name].dtype))
    for name, factor in factors.items():
        out[name] = (out[name] * factor).astype(out[name].dtype)
    return out
```

```python
from contextlib import ExitStack

import concourse.bass as bass
from concourse import mybir

F32 = mybir.dt.float32
F16 = mybir.dt.float16
BF16 = mybir.dt.bfloat16
I32 = mybir.dt.int32
ALU = mybir.AluOpType
ACT = mybir.ActivationFunctionType
AX_X = mybir.AxisListType.X
RMAX = bass.bass_isa.ReduceOp.max

P = 128
N = 1354
T = (N + P - 1) // P
NP = T * P
LAST = N - (T - 1) * P
D = 512
KD = D // P
PAIRS = (T - 1) // 2
assert T == 2 * PAIRS + 1

LN_EPS = 1e-5
ROUND = 1.5 * 2.0 ** 23
RSQRT_SEED = 0x5F3759DF
W_LEVELS = 7.0
X_LEVELS = 15.0
X_SCALE = 2.0 ** 11
Y_SCALE = 2.0 ** 6
TA = 6
H = 8
HD = D // H
HW = HD + 1
LEAK = 0.2
NEG = -9e15
NEG3 = -10000.0
M1, M2, M3 = 256, 128, 256
BIG = 3e38
A_TOP = 2.0 ** 14


class Chain:

    def __init__(self, eng, sem, base=0):
        self.eng, self.sem, self.base, self.n = eng, sem, base, 0

    def __call__(self, ins):
        self.n += 1
        ins.then_inc(self.sem, 1)
        self.eng.wait_ge(self.sem, self.base + self.n)


def build(nc, adjT, adj, xT, x, scal, w0, gat_w, gat_a, w1T, w2T, w3T, w4T, b1, b2, b3, b4, wqT, wkT, wvT, bq, bk, bv, out):
    ctx = ExitStack()
    with ctx:
        def sb(name, shape, dt=F32):
            return ctx.enter_context(nc.sbuf_tensor(name, shape, dt))

        def sem(name):
            return ctx.enter_context(nc.semaphore(name))

        r_at = sb("r_at", [P, 2, T, NP], F16)
        r_s = sb("r_s", [P, T, 2, NP], F16)
        r_x = sb("r_x", [P, T, D])
        r_xs = sb("r_xs", [P, 2, T, D], F16)
        r_y = sb("r_y", [P, 2, T, D], F16)
        r_st = sb("r_st", [P, 2, NP])
        pre = sb("pre", [P, 2, D])
        ident = sb("ident", [P, P])
        ident2 = sb("ident2", [P, P])
        ones = sb("ones", [P, P])
        scs = sb("scs", [P, 4])
        cs = sb("cs", [P, 16])
        dcol = sb("dcol", [P, T])
        ycol = sb("ycol", [P, T])
        bns = sb("bns", [P, 6])
        mv = sb("mv", [P, 2])
        rv = sb("rv", [P, 8])
        amax = sb("amax", [P, 6])
        junk = sb("junk", [P, 1])
        wa = sb("wa", [P, KD, 2 * H])
        es = sb("es", [P, H, T])
        es_pair = sb("es_pair", [P, 2 * T])
        ed = sb("ed", [P, 2, H])
        nmax = sb("nmax", [P, 2])
        rsum = sb("rsum", [P, 8])
        brow = sb("brow", [P, D])
        bcol = sb("bcol", [P, 16])
        rs3 = sb("rs3", [P, 4])
        ps = ctx.enter_context(nc.psum_tensor("ps", [P, 8, D], F32))

        at_raw = r_s[:].rearrange("p t c i -> p t (c i)").bitcast(F32)
        q = r_xs[:, 0]
        wk = r_xs[:, 1].rearrange("p t d -> p (t d)").bitcast(F32)[:, 0:KD * D]
        wk3 = wk.rearrange("p (k d) -> p k d", k=KD)
        xTf = r_y[:].rearrange("p c t d -> p (c t d)").bitcast(F32)[:, 0:KD * NP]
        xT3 = xTf.rearrange("p (k i) -> p k i", k=KD)
        wtmp = r_at[:].rearrange("p c t i -> p (c t i)").bitcast(F32)[:, 0:KD * D]

        at32 = r_at[:].rearrange("p c t i -> p (c t i)").bitcast(F32)
        o = T * H * HW
        Wh = at32[:, 0:o].rearrange("p (t h d) -> p t h d", t=T, h=H)
        drow = at32[:, o:o + 4 * N].rearrange("p (b c i) -> p b c i", b=2, c=2)
        o += 4 * N
        G = at32[:, o:o + 2 * NP].rearrange("p (b i) -> p b i", b=2)
        xs32 = r_xs[:].rearrange("p c t d -> p (c t d)").bitcast(F32)
        W2 = xs32[:, 0:KD * D].rearrange("p (k d) -> p k d", k=KD)
        o = KD * D
        w1 = xs32[:, o:o + KD * M1].rearrange("p (k d) -> p k d", k=KD)
        o += KD * M1
        w2 = xs32[:, o:o + 2 * M2].rearrange("p (k d) -> p k d", k=2)
        o += 2 * M2
        w3 = xs32[:, o:o + M3]
        o += M3
        w4 = xs32[:, o:o + 2 * D].rearrange("p (k d) -> p k d", k=2)
        o += 2 * D
        x2T = xs32[:, o:o + 2 * D].rearrange("p (b k i) -> p b k i", b=2, k=KD)
        a_bc = xs32[:, o:o + 2 * D].rearrange("p (a h d) -> p a h d", a=2, h=H)
        prod = r_st[:, 1, 0:D]
        s32 = r_s[:].rearrange("p t c i -> p (t c i)").bitcast(F32)
        mask = s32[:, 0:T * N // 2].bitcast(BF16).rearrange("p (t i) -> p t i", t=T)
        o = T * N // 2
        wq, wk_, wv = (s32[:, o + m * KD * D:o + (m + 1) * KD * D].rearrange("p (k d) -> p k d", k=KD) for m in range(3))
        o += 3 * KD * D
        edrow = s32[0:H, o:o + NP]
        o += NP
        enc = r_y[:].rearrange("p c t d -> p (c t d)").bitcast(F32).rearrange("p (t d) -> p t d", t=T)
        PT = r_st
        encT = at32[:, 0:KD * NP].rearrange("p (k i) -> p k i", k=KD)
        o1T = at32[:, KD * NP:(KD + 2) * NP].rearrange("p (k i) -> p k i", k=2)
        o2T = at32[:, (KD + 2) * NP:(KD + 3) * NP]
        o3T = at32[:, (KD + 3) * NP:(KD + 5) * NP].rearrange("p (k i) -> p k i", k=2)
        x3T = xT3
        kT = at32[:, 0:KD * NP].rearrange("p (k i) -> p k i", k=KD)
        vv = at32[:, KD * NP:KD * NP + T * D].rearrange("p (t d) -> p t d", t=T)
        o = KD * NP + T * D
        PT3 = at32[:, o:o + 2 * NP].rearrange("p (b i) -> p b i", b=2)
        S3 = s32[:, 0:2 * NP].rearrange("p (b i) -> p b i", b=2)
        Z3 = s32[:, 2 * NP:3 * NP]
        qT = xs32[:, 0:2 * D].rearrange("p (b k i) -> p b k i", b=2, k=KD)

        MEAN, RSTD, C_Q, SIG, SIGH, RSIG, F0, F1, RALPHA, RWA, TMP, CY = range(12)

        def c(k):
            return cs[:, k:k + 1]

        ld_w, ld_xT, ld_sc = sem("ld_w"), sem("ld_xT"), sem("ld_sc")
        ld_x = sem("ld_x")
        GROUPS = [(0, 3), (3, 6), (6, 9), (9, T)]
        ld_at = [sem(f"ld_at{g}") for g in range(len(GROUPS))]
        ld_nat = [sem(f"ld_nat{b}") for b in range(2)]
        const_ready = sem("const_ready")
        wsum_in, wsum_out = sem("wsum_in"), sem("wsum_out")
        amax_in, amax_out = sem("amax_in"), sem("amax_out")
        sig_ready = sem("sig_ready")
        wq_ready, xq_ready = sem("wq_ready"), sem("xq_ready")
        sup_done, q_ready = sem("sup_done"), sem("q_ready")
        at_hi, at_lo = sem("at_hi"), sem("at_lo")
        sym_ready, s_hi, s_lo = sem("sym_ready"), sem("s_hi"), sem("s_lo")
        aq_done, aq_read, x1_ready = sem("aq_done"), sem("aq_read"), sem("x1_ready")
        xs_hi, xs_lo = sem("xs_hi"), sem("xs_lo")
        sx_done, y_hi, y_lo = sem("sx_done"), sem("y_hi"), sem("y_lo")
        ay_done, ay_read, x2_ready = sem("ay_done"), sem("ay_read"), sem("x2_ready")
        pool_add = sem("pool_add")
        dve_a, dve_b, dve_ln0, dve_ln1 = sem("dve_a"), sem("dve_b"), sem("dve_ln0"), sem("dve_ln1")
        stored = sem("stored")
        scratch = nc.dram_tensor("e_dst_rows", [2, H, NP], F32, kind="Internal").ap()
        ld_w2, ld_a, ld_mlp, ld_qkv, ld_b = sem("ld_w2"), sem("ld_a"), sem("ld_mlp"), sem("ld_qkv"), sem("ld_b")
        ld_bv = sem("ld_bv")
        ld_m = [sem(f"ld_m{b}") for b in range(2)]
        wa_ready, mask_ready = sem("wa_ready"), sem("mask_ready")
        x2T_ps, x2T_ready, wh_ps, wh_ready, e_ready, ed_ps, ed_ready = (
            sem(n) for n in ("x2T_ps", "x2T_ready", "wh_ps", "wh_ready", "e_ready", "ed_ps", "ed_ready"))
        ed_stored = sem("ed_stored")
        ld_d = [sem(f"ld_d{b}") for b in range(2)]
        pad_ready, g_free, g_ready, p_ready, pt_ps, pt_ready = (
            sem(n) for n in ("pad_ready", "g_free", "g_ready", "p_ready", "pt_ps", "pt_ready"))
        o_done, enc_a, enc_b, d_used = sem("o_done"), sem("enc_a"), sem("enc_b"), sem("d_used")
        dve_w, dve_p, dve_g, dve_m, dve_3 = sem("dve_w"), sem("dve_p"), sem("dve_g"), sem("dve_m"), sem("dve_3")
        elu_e, elu_done, encT_ps, encT_ready = sem("elu_e"), sem("elu_done"), sem("encT_ps"), sem("encT_ready")
        m1_ps, m1_ready, m2_ps, m2_ready, m3_ps, m3_ready, m4_ps, m4_read = (
            sem(n) for n in ("m1_ps", "m1_ready", "m2_ps", "m2_ready", "m3_ps", "m3_ready", "m4_ps", "m4_read"))
        x3_ready, x3T_ps, x3T_ready = sem("x3_ready"), sem("x3T_ps"), sem("x3T_ready")
        k_ps, k_ready, v_ps, v_ready, q_ps, qT_ready = (
            sem(n) for n in ("k_ps", "k_ready", "v_ps", "v_ready", "q_ps", "qT_ready"))
        sc_ps, sc_read, s3_ready, p3_ready, pt3_ps, pt3_ready, o3_ps, o3_read, x4_ready = (
            sem(n) for n in ("sc_ps", "sc_read", "s3_ready", "p3_ready", "pt3_ps", "pt3_ready", "o3_ps", "o3_read", "x4_ready"))
        ld_a3 = [sem(f"ld_a3{b}") for b in range(2)]
        CH = [(0, 512), (512, 512), (1024, NP - 1024)]
        CHN = [(0, 512), (512, 512), (1024, N - 1024)]

        block = ctx.enter_context(nc.Block())

        def later(t):
            return not (isinstance(t, int) and t < 2)

        def tiles(eng, body):
            body(0, 0)
            body(1, 1)
            with eng.Fori(1, PAIRS) as k:
                body(2 * k, 0)
                body(2 * k + 1, 1)
            body(T - 1, 0)

        @block.sync
        def _(sp):
            sp.dma_start(wk3, w0.rearrange("(k p) d -> p k d", p=P)).then_inc(ld_w, 16)
            sp.dma_start(scs[:], scal).then_inc(ld_sc, 16)
            sp.dma_start(xT3, xT.rearrange("(k p) i -> p k i", p=P)).then_inc(ld_xT, 16)
            for g, (a, b) in enumerate(GROUPS):
                sp.dma_start(at_raw[:, a:b, :], adjT.rearrange("(t p) i -> p t i", p=P)[:, a:b, :]).then_inc(ld_at[g], 16)
            sp.dma_start(r_x[:], x.rearrange("(t p) d -> p t d", p=P)).then_inc(ld_x, 16)

            def nat(t, b, first):
                if not first:
                    sp.wait_ge(s_lo, t - 1)
                sp.dma_start(r_st[:, b, :], adj[bass.ts(t, P), :]).then_inc(ld_nat[b], 16)

            nat(0, 0, True)
            nat(1, 1, True)
            with sp.Fori(1, PAIRS) as k:
                nat(2 * k, 0, False)
                nat(2 * k + 1, 1, False)
            nat(T - 1, 0, False)

            sp.wait_ge(sx_done, T)
            sp.dma_start(W2, gat_w.rearrange("(k p) d -> p k d", p=P)).then_inc(ld_w2, 16)
            sp.dma_start(a_bc.rearrange("p a h d -> p (a h d)"), gat_a[0].partition_broadcast(P)).then_inc(ld_a, 16)
            sp.dma_start(w1, w1T.rearrange("(k p) d -> p k d", p=P)).then_inc(ld_mlp, 16)
            sp.dma_start(w2, w2T.rearrange("(k p) d -> p k d", p=P)).then_inc(ld_mlp, 16)
            sp.dma_start(w3, w3T).then_inc(ld_mlp, 16)
            sp.dma_start(w4, w4T.rearrange("(k p) d -> p k d", p=P)).then_inc(ld_mlp, 16)
            sp.dma_start(brow[:], b4[0].partition_broadcast(P)).then_inc(ld_mlp, 16)
            for col, bias, n in ((0, b1, 2), (2, b2, 1), (3, b3, 2), (5, bq, KD), (9, bk, KD)):
                sp.dma_start(bcol[:, col:col + n], bias).then_inc(ld_b, 16)
            for dst, src in ((wk_, wkT), (wv, wvT), (wq, wqT)):
                sp.dma_start(dst, src.rearrange("(k p) d -> p k d", p=P)).then_inc(ld_qkv, 16)
            sp.wait_ge(wa_ready, 1)
            for t in range(T):
                if t >= 2:
                    sp.wait_ge(mask_ready, t - 1)
                sp.dma_start(r_st[:, t % 2, 0:N], adj[bass.ts(t, P), 0:N]).then_inc(ld_m[t % 2], 16)
            sp.wait_ge(ed_ready, T)
            sp.dma_start(scratch[0], edrow).then_inc(ed_stored, 16)
            sp.wait_ge(ed_stored, 16)

            def load_d(h, b):
                sp.dma_start(drow[:, b, 0, :], scratch[0, bass.ts(h, 1), 0:N][0].partition_broadcast(P)).then_inc(ld_d[b], 16)

            sp.wait_ge(ay_done, T)
            load_d(0, 0)
            load_d(1, 1)
            with sp.Fori(1, H // 2) as hp:
                sp.wait_ge(d_used, 2 * hp - 1)
                load_d(2 * hp, 0)
                sp.wait_ge(d_used, 2 * hp)
                load_d(2 * hp + 1, 1)

            sp.wait_ge(m4_read, T)
            sp.dma_start(brow[:], bv[0].partition_broadcast(P)).then_inc(ld_bv, 16)
            sp.wait_ge(o_done, H * T)
            for t in range(T):
                if t >= 2:
                    sp.wait_ge(sc_read, t - 1)
                sp.dma_start(r_st[:, t % 2, 0:N], adj[bass.ts(t, P), 0:N]).then_inc(ld_a3[t % 2], 16)
                if t >= 2:
                    sp.wait_ge(x4_ready, t - 1)
                    sp.dma_start(out[bass.ts(t - 2, P), :], r_x[:, t - 2, :]).then_inc(stored, 16)
            sp.wait_ge(x4_ready, T - 1)
            sp.dma_start(out[bass.ts(T - 2, P), :], r_x[:, T - 2, :]).then_inc(stored, 16)
            sp.wait_ge(x4_ready, T)
            sp.dma_start(out[(T - 1) * P:N, :], r_x[0:LAST, T - 1, :]).then_inc(stored, 16)
            sp.wait_ge(stored, 16 * T)

        @block.gpsimd
        def _(pool):
            nc.gpsimd.memset(ident[:], 0.0).then_inc(const_ready, 1)
            nc.gpsimd.memset(ident2[:], 0.0).then_inc(const_ready, 1)
            nc.gpsimd.memset(ones[:], 1.0).then_inc(const_ready, 1)
            pool.wait_ge(const_ready, 3)
            for m, v in ((ident, 1.0), (ident2, 2.0)):
                nc.gpsimd.affine_select(out=m[:], in_=m[:], compare_op=ALU.not_equal, fill=v, base=0,
                                        pattern=[[-1, P]], channel_multiplier=1).then_inc(const_ready, 1)
            pool.wait_ge(amax_in, 1)
            nc.gpsimd.partition_all_reduce(amax[:, 5:6], amax[:, 4:5], P, RMAX).then_inc(amax_out, 1)
            pool.wait_ge(const_ready, 5)

            def sym_at(t, b, n):
                pool.wait_ge(ld_nat[b], 16 * n)
                nc.gpsimd.tensor_tensor(r_st[:, b, :], r_st[:, b, :], at_raw[:, t, :], ALU.add).then_inc(pool_add, 1)
                pool.wait_ge(pool_add, t + 1)
                d = r_st[:, b, bass.ts(t, P)]
                nc.gpsimd.tensor_tensor(d, d, ident2[:], ALU.add).then_inc(sym_ready, 1)

            sym_at(0, 0, 1)
            sym_at(1, 1, 1)
            with pool.Fori(1, PAIRS) as k:
                sym_at(2 * k, 0, k + 1)
                sym_at(2 * k + 1, 1, k + 1)
            sym_at(T - 1, 0, PAIRS + 1)

        @block.scalar
        def _(act):
            act.wait_ge(sig_ready, 1)
            for t in range(T):
                nc.scalar.activation(r_at[:, 0, t, :], at_raw[:, t, :], ACT.Copy, scale=c(SIG)).then_inc(at_hi, 1)
            act.wait_ge(at_lo, T)

            def sym_hi(t, b):
                act.wait_ge(sym_ready, t + 1)
                nc.scalar.activation(r_s[:, t, 0, :], r_st[:, b, :], ACT.Copy, scale=c(SIGH),
                                     accum_out=dcol[:, bass.ts(t, 1)]).then_inc(s_hi, 1)
            tiles(act, sym_hi)

            act.wait_ge(aq_done, T)
            def x1_hi(t, b):
                act.wait_ge(x1_ready, t + 1)
                nc.scalar.activation(r_xs[:, 0, t, :], r_x[:, t, :], ACT.Copy,
                                     scale=dcol[:, bass.ts(t, 1)]).then_inc(xs_hi, 1)
            tiles(act, x1_hi)

            def y_high(t, b):
                act.wait_ge(sx_done, t + 1)
                nc.scalar.activation(r_y[:, 0, t, :], ps[:, 4 + b, :], ACT.Copy,
                                     scale=ycol[:, bass.ts(t, 1)]).then_inc(y_hi, 1)
            tiles(act, y_high)

            act.wait_ge(wa_ready, 1)
            act.wait_ge(ay_done, T)
            for t in range(T):
                b = t % 2
                act.wait_ge(x2T_ps, t + 1)
                nc.scalar.activation(x2T[:, b], ps[:, b, :].rearrange("p (k i) -> p k i", k=KD), ACT.Copy).then_inc(x2T_ready, 1)
                act.wait_ge(wh_ps, t + 1)
                nc.scalar.activation(Wh[:, t, :, 0:HD], ps[:, 2 + b, :].rearrange("p (h d) -> p h d", h=H),
                                     ACT.Copy).then_inc(wh_ready, 1)

            def take_pt(n, s):
                act.wait_ge(pt_ps, n + 1)
                if later(n):
                    act.wait_ge(o_done, n - 1)
                b = 3 * (s % 2)
                nc.scalar.activation(PT[:, s % 2, :], ps[:, b:b + 3, :].rearrange("p b i -> p (b i)")[:, 0:NP],
                                     ACT.Copy).then_inc(pt_ready, 1)

            def exps(hp):
                first = isinstance(hp, int)
                for s in range(2 * T):
                    n = hp * 2 * T + s
                    act.wait_ge(g_ready, n + 1)
                    nc.scalar.activation(G[:, s % 2, 0:N], G[:, s % 2, 0:N], ACT.Exp, scale=-1.0,
                                         bias=nmax[:, s % 2:s % 2 + 1]).then_inc(p_ready, 1)
                    if not (first and s == 0):
                        take_pt(n - 1, (s - 1) % 2)
            exps(0)
            with act.Fori(1, H // 2) as hp:
                exps(hp)
            take_pt(H * T - 1, 1)

            act.wait_ge(enc_b, H)
            for t in range(T):
                b = t % 2
                if t >= 2:
                    act.wait_ge(elu_done, t - 1)
                nc.scalar.activation(pre[:, b, :], enc[:, t, :], ACT.Exp).then_inc(elu_e, 1)
                if t >= 1:
                    act.wait_ge(encT_ps, t)
                    nc.scalar.activation(encT[:, :, bass.ts(t - 1, P)], ps[:, (t - 1) % 2, :].rearrange("p (k i) -> p k i", k=KD),
                                         ACT.Copy).then_inc(encT_ready, 1)
            act.wait_ge(encT_ps, T)
            nc.scalar.activation(encT[:, :, bass.ts(T - 1, P)], ps[:, (T - 1) % 2, :].rearrange("p (k i) -> p k i", k=KD),
                                 ACT.Copy).then_inc(encT_ready, 1)
            act.wait_ge(ld_b, 16 * 5)
            for n, (i, w) in enumerate(CH):
                for m in range(2):
                    act.wait_ge(m1_ps, 2 * n + m + 1)
                    nc.scalar.activation(o1T[:, m, i:i + w], ps[:, 2 + m, 0:w], ACT.Relu,
                                         bias=bcol[:, m:m + 1]).then_inc(m1_ready, 1)
                act.wait_ge(m2_ps, n + 1)
                nc.scalar.activation(o2T[:, i:i + w], ps[:, 4, 0:w], ACT.Relu, bias=bcol[:, 2:3]).then_inc(m2_ready, 1)
                for m in range(2):
                    act.wait_ge(m3_ps, 2 * n + m + 1)
                    nc.scalar.activation(o3T[:, m, i:i + w], ps[:, 5 + m, 0:w], ACT.Relu,
                                         bias=bcol[:, 3 + m:4 + m]).then_inc(m3_ready, 1)
            for t in range(T):
                act.wait_ge(x3T_ps, t + 1)
                nc.scalar.activation(x3T[:, :, bass.ts(t, P)], ps[:, 2 + t % 2, :].rearrange("p (k i) -> p k i", k=KD),
                                     ACT.Copy).then_inc(x3T_ready, 1)
            for n, (i, w) in enumerate(CH):
                for m in range(KD):
                    act.wait_ge(k_ps, KD * n + m + 1)
                    nc.scalar.activation(kT[:, m, i:i + w], ps[:, (KD * n + m) % 2, 0:w], ACT.Identity,
                                         bias=bcol[:, 9 + m:10 + m]).then_inc(k_ready, 1)
            for t in range(T):
                b = t % 2
                act.wait_ge(s3_ready, t + 1)
                nc.scalar.activation(S3[:, b, 0:N], S3[:, b, 0:N], ACT.Exp, scale=-1.0, bias=nmax[:, b:b + 1],
                                     accum_out=rs3[:, b:b + 1]).then_inc(p3_ready, 1)
                act.wait_ge(pt3_ps, t + 1)
                if t >= 2:
                    act.wait_ge(o3_ps, t - 1)
                nc.scalar.activation(PT3[:, b, :], ps[:, 3:6, :].rearrange("p b i -> p (b i)")[:, 0:NP],
                                     ACT.Copy).then_inc(pt3_ready, 1)

        @block.vector
        def _(dve):
            v = nc.vector
            ch = Chain(dve, dve_a)

            def rsqrt(ch, y, val, a):
                ch(v.tensor_scalar(a.bitcast(I32), val.bitcast(I32), 1, None, ALU.logical_shift_right))
                ch(v.tensor_scalar(y.bitcast(I32), a.bitcast(I32), -1.0, float(RSQRT_SEED), ALU.mult, ALU.add))
                for _ in range(4):
                    ch(v.tensor_tensor(a, y, y, ALU.mult))
                    ch(v.tensor_tensor(a, a, val, ALU.mult))
                    ch(v.tensor_scalar(a, a, -0.5, 1.5, ALU.mult, ALU.add))
                    ch(v.tensor_tensor(y, y, a, ALU.mult))

            dve.wait_ge(ld_w, 16)
            v.tensor_reduce(rv[:, 0:1], wk, AX_X, ALU.add).then_inc(wsum_in, 1)
            dve.wait_ge(wsum_out, 1)
            ch(v.tensor_scalar(c(MEAN), ps[:, 7, 0:1], 1.0 / (D * D), None, ALU.mult))
            ch(v.tensor_scalar(wk, wk, c(MEAN), None, ALU.subtract))
            v.tensor_tensor_reduce(out=wtmp, in0=wk, in1=wk, scale=1.0, scalar=0.0, op0=ALU.mult, op1=ALU.add,
                                   accum_out=rv[:, 1:2]).then_inc(wsum_in, 1)
            dve.wait_ge(wsum_out, 2)
            ch(v.tensor_scalar(rv[:, 2:3], ps[:, 7, 1:2], 1.0 / (D * D - 1), None, ALU.mult))
            rsqrt(ch, c(RSTD), rv[:, 2:3], rv[:, 3:4])
            dve.wait_ge(ld_sc, 16)
            ch(v.reciprocal(c(RWA), scs[:, 1:2]))
            ch(v.tensor_scalar(wk, wk, c(RSTD), c(RWA), ALU.mult, ALU.mult))
            ch(v.tensor_scalar(wk, wk, 1.0, -1.0, ALU.min, ALU.max))
            ch(v.tensor_scalar(wk, wk, W_LEVELS, ROUND, ALU.mult, ALU.add))
            v.tensor_scalar(wk, wk, ROUND, None, ALU.subtract).then_inc(wq_ready, 1)

            ch(v.reciprocal(c(RALPHA), scs[:, 2:3]))
            dve.wait_ge(ld_xT, 16)
            ch(v.tensor_scalar(xTf, xTf, c(RALPHA), 1.0, ALU.mult, ALU.min))
            ch(v.tensor_scalar(xTf, xTf, X_LEVELS, ROUND, ALU.mult, ALU.add))
            v.tensor_scalar(xTf, xTf, ROUND, None, ALU.subtract).then_inc(xq_ready, 1)

            ch(v.tensor_scalar(c(C_Q), scs[:, 2:3], 1.0 / X_LEVELS, None, ALU.mult))
            ch(v.tensor_scalar(c(TMP), scs[:, 1:2], 1.0 / W_LEVELS, c(C_Q), ALU.mult, ALU.mult))
            ch(v.reciprocal(rv[:, 4:5], scs[:, 3:4]))
            ch(v.tensor_scalar(c(C_Q), c(TMP), rv[:, 4:5], None, ALU.mult))

            for g, (a, b) in enumerate(GROUPS):
                dve.wait_ge(ld_at[g], 16)
                ch(v.tensor_reduce(amax[:, g:g + 1], at_raw[:, a:b, :].rearrange("p t i -> p (t i)"), AX_X, ALU.max,
                                   apply_absolute_value=True))
            v.tensor_reduce(amax[:, 4:5], amax[:, 0:4], AX_X, ALU.max).then_inc(amax_in, 1)
            dve.wait_ge(amax_out, 1)
            ch(v.tensor_scalar(c(TMP), amax[:, 5:6], 1.0, None, ALU.add))
            ch(v.tensor_scalar(c(RSIG).bitcast(I32), c(TMP).bitcast(I32), 0x7F800000, None, ALU.bitwise_and))
            ch(v.tensor_scalar(c(RSIG), c(RSIG), 1.0 / A_TOP, None, ALU.mult))
            ch(v.reciprocal(c(SIG), c(RSIG)))
            v.tensor_scalar(c(SIGH), c(SIG), 0.5, None, ALU.mult).then_inc(sig_ready, 1)
            ch(v.reciprocal(rv[:, 5:6], scs[:, 0:1]))
            ch(v.tensor_scalar(rv[:, 6:7], rv[:, 5:6], scs[:, 0:1], 1.0 / X_LEVELS, ALU.mult, ALU.mult))
            ch(v.tensor_scalar(c(F0), rv[:, 6:7], scs[:, 3:4], c(RSIG), ALU.mult, ALU.mult))
            ch(v.tensor_scalar(c(F1), c(RSIG), 1.0 / Y_SCALE, None, ALU.mult))
            ch(v.tensor_scalar(c(CY), c(RSIG), Y_SCALE / (X_SCALE * X_SCALE), None, ALU.mult))

            for t in range(T):
                b = t % 2
                dve.wait_ge(sup_done, t + 1)
                if t >= 2:
                    dve.wait_ge(q_ready, t - 1)
                ch(v.tensor_scalar(pre[:, b, :], ps[:, b, :], c(C_Q), 0.0, ALU.mult, ALU.max))
                ch(v.tensor_scalar(pre[:, b, :], pre[:, b, :], 1.0, X_LEVELS, ALU.min, ALU.mult))
                v.tensor_scalar(q[:, t, :], pre[:, b, :], ROUND, ROUND, ALU.add, ALU.subtract).then_inc(q_ready, 1)
                dve.wait_ge(at_hi, t + 1)
                v.scalar_tensor_tensor(out=r_at[:, 1, t, :], in0=at_raw[:, t, :], scalar=c(SIG), in1=r_at[:, 0, t, :],
                                       op0=ALU.mult, op1=ALU.subtract).then_inc(at_lo, 1)
            dve.wait_ge(at_lo, T)
            dve.wait_ge(q_ready, T)

            def layer_norm(ch, t, b, also_degree):
                ch(v.bn_stats(bns[:], pre[:, b, :]))
                v.memset(junk[:], 0.0)
                ch(v.bn_aggr(mv[:], bns[:]))
                n = 1
                ch(v.tensor_scalar(rv[:, 0:1], mv[:, 1:2], LN_EPS, None, ALU.add))
                if also_degree:
                    n = 2
                    dve.wait_ge(s_hi, t + 1)
                    ch(v.tensor_scalar(rv[:, 1:2], dcol[:, bass.ts(t, 1)], c(RSIG), 1e-30, ALU.mult, ALU.max))
                rsqrt(ch, rv[:, 2:2 + n], rv[:, 0:n], rv[:, 4:4 + n])
                if also_degree:
                    ch(v.tensor_scalar(rv[:, 6:7], dcol[:, bass.ts(t, 1)], 0.0, X_SCALE, ALU.is_gt, ALU.mult))
                    ch(v.tensor_scalar(dcol[:, bass.ts(t, 1)], rv[:, 6:7], rv[:, 3:4], None, ALU.mult))
                    ch(v.tensor_scalar(ycol[:, bass.ts(t, 1)], dcol[:, bass.ts(t, 1)], c(CY), None, ALU.mult))
                return v.tensor_scalar(r_x[:, t, :], pre[:, b, :], mv[:, 0:1], rv[:, 2:3], ALU.subtract, ALU.mult)

            dve.wait_ge(ld_x, 16)
            K0 = 1 + 1 + 1 + 1 + 1 + 18 + 3

            def ln0(t, b):
                dve.wait_ge(s_hi, t + 1)
                v.scalar_tensor_tensor(out=r_s[:, t, 1, :], in0=r_st[:, b, :], scalar=c(SIGH), in1=r_s[:, t, 0, :],
                                       op0=ALU.mult, op1=ALU.subtract).then_inc(s_lo, 1)
                ch = Chain(dve, dve_ln0, t * K0)
                dve.wait_ge(aq_done, t + 1)
                v.scalar_tensor_tensor(out=pre[:, b, :], in0=ps[:, 2 + b, :], scalar=c(F0), in1=r_x[:, t, :],
                                       op0=ALU.mult, op1=ALU.add).then_inc(aq_read, 1)
                dve.wait_ge(aq_read, t + 1)
                layer_norm(ch, t, b, True).then_inc(x1_ready, 1)
                assert ch.n == K0 - 1, ch.n
                dve.wait_ge(x1_ready, t + 1)
                v.memset(junk[:], 0.0).then_inc(dve_ln0, 1)
            tiles(dve, ln0)

            def x1_lo(t, b):
                dve.wait_ge(xs_hi, t + 1)
                v.scalar_tensor_tensor(out=r_xs[:, 1, t, :], in0=r_x[:, t, :], scalar=dcol[:, bass.ts(t, 1)],
                                       in1=r_xs[:, 0, t, :], op0=ALU.mult, op1=ALU.subtract).then_inc(xs_lo, 1)
            tiles(dve, x1_lo)

            def y_low(t, b):
                dve.wait_ge(y_hi, t + 1)
                v.scalar_tensor_tensor(out=r_y[:, 1, t, :], in0=ps[:, 4 + b, :], scalar=ycol[:, bass.ts(t, 1)],
                                       in1=r_y[:, 0, t, :], op0=ALU.mult, op1=ALU.subtract).then_inc(y_lo, 1)
            tiles(dve, y_low)

            ch = Chain(dve, dve_w)
            dve.wait_ge(s_lo, T)
            dve.wait_ge(ld_w2, 16)
            dve.wait_ge(ld_a, 16)
            for k in range(KD):
                for a in range(2):
                    ch(v.tensor_tensor(prod, W2[:, k, :], a_bc[:, a].rearrange("p h d -> p (h d)"), ALU.mult))
                    ch(v.tensor_reduce(wa[:, k, a * H:(a + 1) * H], prod.rearrange("p (h d) -> p h d", h=H), AX_X, ALU.add))
            v.memset(junk[:], 0.0).then_inc(wa_ready, 1)

            def mask_tile(t):
                dve.wait_ge(ld_m[t % 2], 16 * (t // 2 + 1))
                v.tensor_scalar(mask[:, t, :], r_st[:, t % 2, 0:N], 0.0, NEG, ALU.is_le, ALU.mult).then_inc(mask_ready, 1)

            K1 = 1 + 1 + 1 + 18 + 1

            def ln1(t, b):
                ch = Chain(dve, dve_ln1, t * K1)
                dve.wait_ge(ay_done, t + 1)
                v.scalar_tensor_tensor(out=pre[:, b, :], in0=ps[:, 2 + b, :], scalar=c(F1), in1=r_x[:, t, :],
                                       op0=ALU.mult, op1=ALU.add).then_inc(ay_read, 1)
                dve.wait_ge(ay_read, t + 1)
                layer_norm(ch, t, b, False).then_inc(x2_ready, 1)
                assert ch.n == K1 - 1, ch.n
                dve.wait_ge(x2_ready, t + 1)
                v.memset(junk[:], 0.0).then_inc(dve_ln1, 1)
            tiles(dve, ln1)
            for t in range(T):
                mask_tile(t)

            ch = Chain(dve, dve_p)
            dve.wait_ge(ay_done, T)
            ch(v.memset(Wh[:, :, :, HD:HW], 1.0))
            for b in range(2):
                v.memset(G[:, b, N:NP], 0.0).then_inc(pad_ready, 1)
            for t in range(T):
                dve.wait_ge(wh_ps, t + 1)
                b = t % 2
                if t >= 2:
                    dve.wait_ge(ed_ps, t - 1)
                ch(v.tensor_copy(ed[:, b, :], ps[:, 6 + b, H:2 * H]))
                v.tensor_scalar(es[:, :, t], ps[:, 6 + b, 0:H], 1.0 - LEAK, None, ALU.mult).then_inc(e_ready, 1)
                dve.wait_ge(ed_ps, t + 1)
                v.tensor_copy(edrow[:, bass.ts(t, P)], ps[0:H, 4 + b, 0:P]).then_inc(ed_ready, 1)

            dve.wait_ge(e_ready, T)
            dve.wait_ge(mask_ready, T)
            dve.wait_ge(pad_ready, 2)
            v.memset(junk[:], 0.0).then_inc(g_free, 2)
            KG = 1 + 2 * T + 2 + 2 * 2

            def take_enc(ch, h, bank, t0, nt):
                src = ps[:, bank, 0:nt * HW].rearrange("p (t d) -> p t d", t=nt)
                ch(v.reciprocal(rsum[:, 0:nt], src[:, :, HD]))
                return v.tensor_tensor(enc[:, t0:t0 + nt, bass.ts(h, HD)], src[:, :, 0:HD],
                                       rsum[:, 0:nt].unsqueeze(2).broadcast_to([P, nt, HD]), ALU.mult)

            def scores(hp):
                first = isinstance(hp, int)
                ch = Chain(dve, dve_g, hp * KG)
                ch(v.tensor_copy(es_pair[:], es[:, bass.ts(hp, 2), :].rearrange("p h t -> p (h t)")))
                for s in range(2 * T):
                    hh, t = divmod(s, T)
                    n = hp * 2 * T + s
                    b = s % 2
                    if t == 0:
                        dve.wait_ge(ld_d[hh], 16 * (hp + 1))
                        ch(v.tensor_scalar(drow[:, hh, 1, :], drow[:, hh, 0, :], LEAK, None, ALU.mult))
                    dve.wait_ge(g_free, n + 1)
                    ch(v.scalar_tensor_tensor(out=G[:, b, 0:N], in0=drow[:, hh, 0, :], scalar=es_pair[:, s:s + 1],
                                              in1=drow[:, hh, 1, :], op0=ALU.add, op1=ALU.max))
                    v.memset(junk[:], 0.0)
                    v.tensor_tensor_reduce(out=G[:, b, 0:N], in0=G[:, b, 0:N], in1=mask[:, t, :], scale=-1.0,
                                           scalar=BIG, op0=ALU.add, op1=ALU.min,
                                           accum_out=nmax[:, b:b + 1]).then_inc(g_ready, 1)
                    if t == T - 1:
                        dve.wait_ge(g_ready, n + 1)
                        v.memset(junk[:], 0.0).then_inc(d_used, 1)
                    if t == 9:
                        dve.wait_ge(o_done, (2 * hp + hh) * T + TA)
                        take_enc(ch, 2 * hp + hh, 6, 0, TA).then_inc(enc_a, 1)
                        dve.wait_ge(enc_a, 2 * hp + hh + 1)
                    if t == 3 and not (first and hh == 0):
                        dve.wait_ge(o_done, (2 * hp + hh) * T)
                        take_enc(ch, 2 * hp + hh - 1, 7, TA, T - TA).then_inc(enc_b, 1)
                        dve.wait_ge(enc_b, 2 * hp + hh)
                if first:
                    ch(v.nop())
                assert ch.n == KG
            scores(0)
            with dve.Fori(1, H // 2) as hp:
                scores(hp)
            ch = Chain(dve, dve_m)
            dve.wait_ge(o_done, H * T)
            take_enc(ch, H - 1, 7, TA, T - TA).then_inc(enc_b, 1)
            dve.wait_ge(enc_b, H)

            for t in range(T):
                b = t % 2
                dve.wait_ge(elu_e, t + 1)
                ch(v.tensor_scalar(pre[:, b, :], pre[:, b, :], 1.0, -1.0, ALU.min, ALU.add))
                v.tensor_tensor(enc[:, t, :], enc[:, t, :], pre[:, b, :], ALU.max).then_inc(elu_done, 1)
            dve.wait_ge(elu_done, T)
            dve.wait_ge(ld_mlp, 16 * 5)
            for t in range(T):
                b = t % 2
                dve.wait_ge(m4_ps, t + 1)
                v.tensor_tensor(pre[:, b, :], ps[:, b, :], brow[:], ALU.add).then_inc(m4_read, 1)
                dve.wait_ge(m4_read, t + 1)
                ch(v.tensor_tensor(pre[:, b, :], pre[:, b, :], r_x[:, t, :], ALU.add))
                layer_norm(ch, t, b, False).then_inc(x3_ready, 1)
                dve.wait_ge(x3_ready, t + 1)
            for b in range(2):
                ch(v.memset(S3[:, b, N:NP], 0.0))
            dve.wait_ge(ld_bv, 16)
            for t in range(T):
                dve.wait_ge(v_ps, t + 1)
                v.tensor_tensor(vv[:, t, :], ps[:, 6 + t % 2, :], brow[:], ALU.add).then_inc(v_ready, 1)
            def take_q(t):
                dve.wait_ge(q_ps, t + 1)
                if t >= 2:
                    dve.wait_ge(sc_ps, t - 1)
                v.tensor_tensor(qT[:, t % 2], ps[:, 6, :].rearrange("p (k i) -> p k i", k=KD),
                                bcol[:, 5:5 + KD].unsqueeze(2).broadcast_to([P, KD, P]), ALU.add).then_inc(qT_ready, 1)

            def finish(t):
                b = t % 2
                dve.wait_ge(o3_ps, t + 1)
                ch(v.reciprocal(rsum[:, 0:1], rs3[:, b:b + 1]))
                v.tensor_scalar(pre[:, b, :], ps[:, 7, :], rsum[:, 0:1], 0.0, ALU.mult, ALU.max).then_inc(o3_read, 1)
                dve.wait_ge(o3_read, t + 1)
                ch(v.tensor_tensor(pre[:, b, :], pre[:, b, :], r_x[:, t, :], ALU.add))
                layer_norm(ch, t, b, False).then_inc(x4_ready, 1)
                dve.wait_ge(x4_ready, t + 1)

            take_q(0)
            for t in range(T):
                b = t % 2
                dve.wait_ge(sc_ps, t + 1)
                dve.wait_ge(ld_a3[b], 16 * (t // 2 + 1))
                if t >= 2:
                    dve.wait_ge(pt3_ps, t - 1)
                v.scalar_tensor_tensor(out=S3[:, b, 0:N], in0=ps[:, 0:3, :].rearrange("p b i -> p (b i)")[:, 0:N],
                                       scalar=float(D) ** -0.5, in1=r_st[:, b, 0:N], op0=ALU.mult,
                                       op1=ALU.mult).then_inc(sc_read, 1)
                dve.wait_ge(sc_read, t + 1)
                ch(v.tensor_scalar(Z3[:, 0:N], S3[:, b, 0:N], 0.0, NEG3, ALU.is_equal, ALU.mult))
                ch(v.tensor_tensor_reduce(out=S3[:, b, 0:N], in0=S3[:, b, 0:N], in1=Z3[:, 0:N], scale=-1.0,
                                          scalar=BIG, op0=ALU.add, op1=ALU.min, accum_out=nmax[:, b:b + 1]))
                v.memset(junk[:], 0.0).then_inc(s3_ready, 1)
                if t + 1 < T:
                    take_q(t + 1)
                if t >= 1:
                    finish(t - 1)
            finish(T - 1)

        @block.tensor
        def _(pe):
            mm = nc.tensor.matmul
            pe.wait_ge(const_ready, 5)
            for n in range(2):
                pe.wait_ge(wsum_in, n + 1)
                mm(ps[:, 7, n:n + 1], ones[:], rv[:, n:n + 1], start=True, stop=True).then_inc(wsum_out, 1)
            pe.wait_ge(wq_ready, 1)
            pe.wait_ge(xq_ready, 1)
            for t in range(T):
                b = t % 2
                if t >= 2:
                    pe.wait_ge(q_ready, t - 1)
                for k in range(KD):
                    last = mm(ps[:, b, :], xT3[:, k, bass.ts(t, P)], wk3[:, k, :], start=(k == 0), stop=(k == KD - 1))
                last.then_inc(sup_done, 1)
            pe.wait_ge(q_ready, T)
            pe.wait_ge(at_lo, T)

            def aq(t, b):
                if later(t):
                    pe.wait_ge(aq_read, t - 1)
                for j in range(T):
                    for part in range(2):
                        last = mm(ps[:, 2 + b, :], r_at[:, part, j, bass.ts(t, P)], q[:, j, :],
                                  start=(j == 0 and part == 0), stop=(j == T - 1 and part == 1))
                last.then_inc(aq_done, 1)
            tiles(pe, aq)

            def split_product(out_bank, left, right, wait_right=None):
                for j in range(T):
                    if wait_right:
                        wait_right(j)
                    for part, (a, bb) in enumerate(((0, 0), (0, 1), (1, 0))):
                        last = mm(out_bank, left(a, j), right[:, bb, j, :], start=(j == 0 and part == 0),
                                  stop=(j == T - 1 and part == 2))
                return last

            pe.wait_ge(s_lo, T)

            def sx(t, b):
                first = isinstance(t, int) and t == 0
                if later(t):
                    pe.wait_ge(y_lo, t - 1)
                def wait_right(j):
                    pe.wait_ge(xs_lo, j + 1)
                split_product(ps[:, 4 + b, :], lambda a, j: r_s[:, j, a, bass.ts(t, P)], r_xs,
                              wait_right if first else None).then_inc(sx_done, 1)
            tiles(pe, sx)

            pe.wait_ge(x1_ready, T)

            def ay(t, b):
                first = isinstance(t, int) and t == 0
                if later(t):
                    pe.wait_ge(ay_read, t - 1)
                def wait_right(j):
                    pe.wait_ge(y_lo, j + 1)
                split_product(ps[:, 2 + b, :], lambda a, j: r_at[:, a, j, bass.ts(t, P)], r_y,
                              wait_right if first else None).then_inc(ay_done, 1)
            tiles(pe, ay)

            tr = nc.tensor.transpose

            pe.wait_ge(ld_w2, 16)
            pe.wait_ge(wa_ready, 1)
            for t in range(T):
                b = t % 2
                pe.wait_ge(x2_ready, t + 1)
                if t >= 2:
                    pe.wait_ge(x2T_ready, t - 1)
                for k in range(KD):
                    last = tr(ps[:, b, bass.ts(k, P)], r_x[:, t, bass.ts(k, P)], ident[:])
                last.then_inc(x2T_ps, 1)
                pe.wait_ge(x2T_ready, t + 1)
                if t == 0:
                    pe.wait_ge(ay_read, T)
                if t >= 2:
                    pe.wait_ge(wh_ready, t - 1)
                    pe.wait_ge(e_ready, t - 1)
                for k in range(KD):
                    mm(ps[:, 2 + b, :], x2T[:, b, k, :], W2[:, k, :], start=(k == 0), stop=(k == KD - 1))
                for k in range(KD):
                    last = mm(ps[:, 6 + b, 0:2 * H], x2T[:, b, k, :], wa[:, k, :], start=(k == 0), stop=(k == KD - 1))
                last.then_inc(wh_ps, 1)
                pe.wait_ge(e_ready, t + 1)
                if t >= 2:
                    pe.wait_ge(ed_ready, t - 1)
                tr(ps[0:H, 4 + b, 0:P], ed[:, b, :], ident[:]).then_inc(ed_ps, 1)
            pe.wait_ge(wh_ready, T)
            pe.wait_ge(e_ready, T)
            pe.wait_ge(ed_ready, T)

            def weigh(n, s, h, hh, t):
                pe.wait_ge(pt_ready, n + 1)
                if t == 0 and later(h + 1):
                    pe.wait_ge(enc_a, h)
                if t == TA and later(h + 1):
                    pe.wait_ge(enc_b, h)
                bank, c0 = (6, t * HW) if t < TA else (7, (t - TA) * HW)
                for j in range(T):
                    last = mm(ps[:, bank, c0:c0 + HW], PT[:, s % 2, bass.ts(j, P)],
                              Wh[:, j, bass.ts(h, 1), :].rearrange("p h d -> p (h d)"), start=(j == 0), stop=(j == T - 1))
                last.then_inc(o_done, 1)

            def heads(hp):
                first = isinstance(hp, int)
                for s in range(2 * T):
                    hh, t = divmod(s, T)
                    n = hp * 2 * T + s
                    pe.wait_ge(p_ready, n + 1)
                    if not (first and s < 2):
                        pe.wait_ge(pt_ready, n - 1)
                    for j in range(T):
                        last = tr(ps[:, 3 * (s % 2) + j // KD, bass.ts(j % KD, P)], G[:, s % 2, bass.ts(j, P)], ident[:])
                    last.then_inc(pt_ps, 1)
                    pe.wait_ge(pt_ps, n + 1)
                    pe.nop().then_inc(g_free, 1)
                    if not (first and s == 0):
                        hb, tb = divmod((s - 1) % (2 * T), T)
                        h = 2 * hp + hb if s else 2 * hp - 1
                        weigh(n - 1, (s - 1) % 2, h, hb, tb)
            heads(0)
            with pe.Fori(1, H // 2) as hp:
                heads(hp)
            weigh(H * T - 1, 1, H - 1, 1, T - 1)

            pe.wait_ge(ld_mlp, 16 * 5)
            for t in range(T):
                b = t % 2
                pe.wait_ge(elu_done, t + 1)
                if t >= 2:
                    pe.wait_ge(encT_ready, t - 1)
                for k in range(KD):
                    last = tr(ps[:, b, bass.ts(k, P)], enc[:, t, bass.ts(k, P)], ident[:])
                last.then_inc(encT_ps, 1)
            pe.wait_ge(encT_ready, T)
            for n, (i, w) in enumerate(CH):
                for m in range(2):
                    if n:
                        pe.wait_ge(m1_ready, 2 * (n - 1) + m + 1)
                    for k in range(KD):
                        last = mm(ps[:, 2 + m, 0:w], w1[:, k, bass.ts(m, P)], encT[:, k, i:i + w], start=(k == 0), stop=(k == KD - 1))
                    last.then_inc(m1_ps, 1)
                pe.wait_ge(m1_ready, 2 * n + 2)
                if n:
                    pe.wait_ge(m2_ready, n)
                for k in range(2):
                    last = mm(ps[:, 4, 0:w], w2[:, k, :], o1T[:, k, i:i + w], start=(k == 0), stop=(k == 1))
                last.then_inc(m2_ps, 1)
                pe.wait_ge(m2_ready, n + 1)
                for m in range(2):
                    if n:
                        pe.wait_ge(m3_ready, 2 * (n - 1) + m + 1)
                    mm(ps[:, 5 + m, 0:w], w3[:, bass.ts(m, P)], o2T[:, i:i + w], start=True, stop=True).then_inc(m3_ps, 1)
            pe.wait_ge(m3_ready, 6)

            def x3_turn(t):
                pe.wait_ge(x3_ready, t + 1)
                if t >= 2:
                    pe.wait_ge(x3T_ready, t - 1)
                for k in range(KD):
                    last = tr(ps[:, 2 + t % 2, bass.ts(k, P)], r_x[:, t, bass.ts(k, P)], ident[:])
                last.then_inc(x3T_ps, 1)

            for t in range(T):
                if t >= 2:
                    pe.wait_ge(m4_read, t - 1)
                for k in range(2):
                    last = mm(ps[:, t % 2, :], o3T[:, k, bass.ts(t, P)], w4[:, k, :], start=(k == 0), stop=(k == 1))
                last.then_inc(m4_ps, 1)
                if t >= 2:
                    x3_turn(t - 2)
            x3_turn(T - 2)
            x3_turn(T - 1)
            pe.wait_ge(m4_read, T)
            pe.wait_ge(ld_qkv, 16 * 3)
            pe.wait_ge(x3T_ready, T)
            for n, (i, w) in enumerate(CH):
                for m in range(KD):
                    if KD * n + m >= 2:
                        pe.wait_ge(k_ready, KD * n + m - 1)
                    for k in range(KD):
                        last = mm(ps[:, (KD * n + m) % 2, 0:w], wk_[:, k, bass.ts(m, P)], x3T[:, k, i:i + w],
                                  start=(k == 0), stop=(k == KD - 1))
                    last.then_inc(k_ps, 1)
            for t in range(T):
                if t >= 2:
                    pe.wait_ge(v_ready, t - 1)
                for k in range(KD):
                    last = mm(ps[:, 6 + t % 2, :], x3T[:, k, bass.ts(t, P)], wv[:, k, :], start=(k == 0), stop=(k == KD - 1))
                last.then_inc(v_ps, 1)
            pe.wait_ge(k_ready, 3 * KD)
            pe.wait_ge(v_ready, T)

            def query(t):
                if t >= 1:
                    pe.wait_ge(qT_ready, t)
                for m in range(KD):
                    for k in range(KD):
                        last = mm(ps[:, 6, bass.ts(m, P)], wq[:, k, bass.ts(m, P)], x3T[:, k, bass.ts(t, P)],
                                  start=(k == 0), stop=(k == KD - 1))
                last.then_inc(q_ps, 1)

            def score(t):
                pe.wait_ge(qT_ready, t + 1)
                if t >= 1:
                    pe.wait_ge(sc_read, t)
                for n, (i, w) in enumerate(CHN):
                    for k in range(KD):
                        last = mm(ps[:, n, 0:w], qT[:, t % 2, k, :], kT[:, k, i:i + w], start=(k == 0), stop=(k == KD - 1))
                last.then_inc(sc_ps, 1)

            query(0)
            score(0)
            for t in range(T):
                if t + 1 < T:
                    query(t + 1)
                    score(t + 1)
                pe.wait_ge(p3_ready, t + 1)
                if t >= 1:
                    pe.wait_ge(pt3_ready, t)
                for j in range(T):
                    last = tr(ps[:, 3 + j // KD, bass.ts(j % KD, P)], S3[:, t % 2, bass.ts(j, P)], ident[:])
                last.then_inc(pt3_ps, 1)
                pe.wait_ge(pt3_ready, t + 1)
                if t >= 1:
                    pe.wait_ge(o3_read, t)
                for j in range(T):
                    last = mm(ps[:, 7, :], PT3[:, t % 2, bass.ts(j, P)], vv[:, j, :], start=(j == 0), stop=(j == T - 1))
                last.then_inc(o3_ps, 1)


_OUT = (N, D)


def kernel(**inputs):
    import numpy as _np
    import concourse.bacc as _bacc
    from concourse import mybir as _mybir
    from concourse.bass_utils import run_bass_kernel_spmd as _run

    f = {k: _np.asarray(a) for k, a in inputs.items()}
    pad = NP - N
    lay = {
        "adjT": _np.pad(f["adj"].T, ((0, pad), (0, pad))),
        "adj": _np.pad(f["adj"], ((0, pad), (0, pad))),
        "xT": _np.pad(f["x"].T, ((0, 0), (0, pad))),
        "x": _np.pad(f["x"], ((0, pad), (0, 0))),
        "scal": _np.broadcast_to(_np.stack([f["L0_gnn_adj_scaling_factor"], f["L0_gnn_wgt_alpha"], f["L0_gnn_act_alpha"],
                                            f["L0_gnn_act_alpha2"]]), (P, 4)),
        "w0": f["L0_gnn_weight"],
        "gat_w": f["L2_gnn_W"].transpose(1, 0, 2).reshape(D, D),
        "gat_a": _np.stack([f["L2_gnn_a1"], f["L2_gnn_a2"]]).reshape(1, 2 * D),
        "w1T": f["L2_gnn_W1"].T, "w2T": f["L2_gnn_W2"].T, "w3T": f["L2_gnn_W3"].T, "w4T": f["L2_gnn_W4"].T,
        "b1": f["L2_gnn_b1"].reshape(-1, P).T, "b2": f["L2_gnn_b2"].reshape(-1, P).T, "b3": f["L2_gnn_b3"].reshape(-1, P).T,
        "b4": f["L2_gnn_b4"].reshape(1, D),
        "wqT": f["L3_gnn_W_q"].T, "wkT": f["L3_gnn_W_k"].T, "wvT": f["L3_gnn_W_v"].T,
        "bq": f["L3_gnn_b_q"].reshape(-1, P).T, "bk": f["L3_gnn_b_k"].reshape(-1, P).T, "bv": f["L3_gnn_b_v"].reshape(1, D),
    }
    nc = _bacc.Bacc("TRN2", target_bir_lowering=False, num_devices=1)
    arrays, args = {}, []
    for name, a in lay.items():
        a = _np.ascontiguousarray(a)
        arrays[f"in_{name}_dram"] = a
        args.append(nc.dram_tensor(f"in_{name}_dram", a.shape, _mybir.dt.from_np(a.dtype), kind="ExternalInput").ap())
    args.append(nc.dram_tensor("out_0_dram", _OUT, F32, kind="ExternalOutput").ap())
    build(nc, *args)
    r = _run(nc, [arrays], core_ids=[0])
    return r.results[0]["out_0_dram"]
```

```python
from contextlib import ExitStack

import concourse.bass as bass
from concourse import mybir

F32 = mybir.dt.float32
F16 = mybir.dt.float16
BF16 = mybir.dt.bfloat16
I32 = mybir.dt.int32
ALU = mybir.AluOpType
ACT = mybir.ActivationFunctionType
AX_X = mybir.AxisListType.X
RMAX = bass.bass_isa.ReduceOp.max

P = 128
N = 1354
T = (N + P - 1) // P
NP = T * P
LAST = N - (T - 1) * P
D = 512
KD = D // P
PAIRS = (T - 1) // 2
assert T == 2 * PAIRS + 1

LN_EPS = 1e-5
ROUND = 1.5 * 2.0 ** 23
RSQRT_SEED = 0x5F3759DF
W_LEVELS = 7.0
X_LEVELS = 15.0
X_SCALE = 2.0 ** 11
Y_SCALE = 2.0 ** 6
TA = 6
H = 8
HD = D // H
HW = HD + 1
LEAK = 0.2
NEG = -9e15
NEG3 = -10000.0
M1, M2, M3 = 256, 128, 256
BIG = 3e38
P_SCALE = 2.0 ** 14
A_TOP = 2.0 ** 14


class Chain:

    def __init__(self, eng, sem, base=0):
        self.eng, self.sem, self.base, self.n = eng, sem, base, 0

    def __call__(self, ins):
        self.n += 1
        ins.then_inc(self.sem, 1)
        self.eng.wait_ge(self.sem, self.base + self.n)


def build(nc, adjT, adj, xT, x, scal, w0, gat_w, gat_a, w1T, w2T, w3T, w4T, b1, b2, b3, b4, wq, wk, wvT, bq, bk, bv, out):
    ctx = ExitStack()
    with ctx:
        def sb(name, shape, dt=F32):
            return ctx.enter_context(nc.sbuf_tensor(name, shape, dt))

        def sem(name):
            return ctx.enter_context(nc.semaphore(name))

        r_at = sb("r_at", [P, 2, T, NP], F16)
        r_s = sb("r_s", [P, T, 2, NP], F16)
        r_x = sb("r_x", [P, T, D])
        r_xs = sb("r_xs", [P, 2, T, D], F16)
        r_y = sb("r_y", [P, 2, T, D], F16)
        r_st = sb("r_st", [P, 2, NP])
        pre = sb("pre", [P, 2, D])
        ident = sb("ident", [P, P])
        ident2 = sb("ident2", [P, P])
        ones = sb("ones", [P, P])
        scs = sb("scs", [P, 4])
        cs = sb("cs", [P, 16])
        dcol = sb("dcol", [P, T])
        ycol = sb("ycol", [P, T])
        bns = sb("bns", [P, 6])
        mv = sb("mv", [P, 2])
        rv = sb("rv", [P, 8])
        amax = sb("amax", [P, 6])
        junk = sb("junk", [P, 1])
        wa = sb("wa", [P, KD, 2 * H])
        es = sb("es", [P, H, T])
        es_pair = sb("es_pair", [P, 2 * T])
        ed = sb("ed", [P, 2, H])
        nmax = sb("nmax", [P, 2])
        rsum = sb("rsum", [P, 8])
        brow = sb("brow", [P, D])
        bcol = sb("bcol", [P, 16])
        rs3 = sb("rs3", [P, 4])
        fold = sb("fold", [P, KD + 1])
        r_col = sb("r_col", [P, T])
        bqk = sb("bqk", [P, KD])
        bound = sb("bound", [P, 4])
        r_sig3 = sb("r_sig3", [P, 4])
        sig3 = sb("sig3", [P, 4])
        k3 = sb("k3", [P, 8])
        ps = ctx.enter_context(nc.psum_tensor("ps", [P, 8, D], F32))

        at_raw = r_s[:].rearrange("p t c i -> p t (c i)").bitcast(F32)
        q = r_xs[:, 0]
        wlev = r_xs[:, 1].rearrange("p t d -> p (t d)").bitcast(F32)[:, 0:KD * D]
        wk3 = wlev.rearrange("p (k d) -> p k d", k=KD)
        xTf = r_y[:].rearrange("p c t d -> p (c t d)").bitcast(F32)[:, 0:KD * NP]
        xT3 = xTf.rearrange("p (k i) -> p k i", k=KD)
        wq_n, wk_n = (xTf[:, m * KD * D:(m + 1) * KD * D].rearrange("p (k d) -> p k d", k=KD) for m in range(2))
        fold_row = xTf[:, 2 * KD * D:2 * KD * D + 2 * D].rearrange("p (b d) -> p b d", b=2)
        wtmp = r_at[:].rearrange("p c t i -> p (c t i)").bitcast(F32)[:, 0:KD * D]

        at32 = r_at[:].rearrange("p c t i -> p (c t i)").bitcast(F32)
        o = 0
        drow = at32[:, o:o + 4 * N].rearrange("p (b c i) -> p b c i", b=2, c=2)
        o += 4 * N
        G = at32[:, o:o + 2 * N].rearrange("p (b i) -> p b i", b=2)
        o += 2 * N
        PR0 = at32[:, o:o + NP]
        xs32 = r_xs[:].rearrange("p c t d -> p (c t d)").bitcast(F32)
        W2 = xs32[:, 0:KD * D].rearrange("p (k d) -> p k d", k=KD)
        o = KD * D
        w1 = xs32[:, o:o + KD * M1].rearrange("p (k d) -> p k d", k=KD)
        o += KD * M1
        w2 = xs32[:, o:o + 2 * M2].rearrange("p (k d) -> p k d", k=2)
        o += 2 * M2
        w3 = xs32[:, o:o + M3]
        o += M3
        w4 = xs32[:, o:o + 2 * D].rearrange("p (k d) -> p k d", k=2)
        x2 = w4
        o += 2 * D
        x2T = xs32[:, o:o + 2 * D].rearrange("p (b k i) -> p b k i", b=2, k=KD)
        M32 = W2
        w_row = xs32[:, o:o + D]
        st32 = r_st[:].rearrange("p b i -> p (b i)")
        W2_st = st32[:, 0:KD * D].rearrange("p (k d) -> p k d", k=KD)
        prod = st32[:, KD * D:KD * D + D]
        a_bc = pre[:]
        s32 = r_s[:].rearrange("p t c i -> p (t c i)").bitcast(F32)
        mask = s32[:, 0:T * N // 2].bitcast(BF16).rearrange("p (t i) -> p t i", t=T)
        o = T * N // 2
        Wh = s32[:, o:o + T * H * HW].rearrange("p (t h d) -> p t h d", t=T, h=H)
        o += T * H * HW
        edrow = s32[0:H, o:o + NP]
        PR1 = s32[:, o:o + NP]
        PR = [PR0, PR1]
        o += NP
        enc = r_y[:].rearrange("p c t d -> p (c t d)").bitcast(F32).rearrange("p (t d) -> p t d", t=T)
        PT = r_st
        encT = at32[:, 0:KD * NP].rearrange("p (k i) -> p k i", k=KD)
        o1T = at32[:, KD * NP:(KD + 2) * NP].rearrange("p (k i) -> p k i", k=2)
        o2T = at32[:, (KD + 2) * NP:(KD + 3) * NP]
        o3T = at32[:, (KD + 3) * NP:(KD + 5) * NP].rearrange("p (k i) -> p k i", k=2)
        x3T = r_y[:].rearrange("p c t d -> p (c t d)").rearrange("p (c k i) -> p c k i", c=2, k=KD)
        at16 = r_at[:].rearrange("p c t i -> p (c t i)")
        vv = at16[:, 0:2 * T * D].rearrange("p (c t d) -> p c t d", c=2, t=T)
        PT3 = at16[:, 2 * T * D:2 * T * D + 4 * NP].rearrange("p (b c i) -> p b c i", b=2, c=2)
        S3 = s32[:, 0:2 * NP].rearrange("p (b i) -> p b i", b=2)
        Z3 = s32[:, 2 * NP:3 * NP]
        o = 3 * NP
        wv = s32[:, o:o + KD * D].rearrange("p (k d) -> p k d", k=KD)
        o += KD * D
        m_parts, wv_parts = (s32[:, o + m * KD * D:o + (m + 1) * KD * D].bitcast(F16).rearrange(
            "p (c k d) -> p c k d", c=2, k=KD) for m in range(2))
        o += 2 * KD * D
        v_row = s32[:, o:o + D]
        o += D
        g32 = s32[:, o:o + 2 * D].rearrange("p (b k i) -> p b k i", b=2, k=KD)
        o += 2 * D
        g_parts = s32[:, o:o + 2 * D].bitcast(F16).rearrange("p (b c k i) -> p b c k i", b=2, c=2, k=KD)
        o += 2 * D
        v32 = s32[:, o:o + 2 * D].rearrange("p (b d) -> p b d", b=2)

        MEAN, RSTD, C_Q, SIG, SIGH, RSIG, F0, F1, RALPHA, RWA, TMP, CY = range(12)

        A_G, A_V, KAPPA, NEG_K, R_V, S_R = range(6)

        def c(k):
            return cs[:, k:k + 1]

        def kc(k):
            return k3[:, k:k + 1]

        ld_w, ld_xT, ld_sc = sem("ld_w"), sem("ld_xT"), sem("ld_sc")
        ld_x = sem("ld_x")
        GROUPS = [(0, 3), (3, 6), (6, 9), (9, T)]
        ld_at = [sem(f"ld_at{g}") for g in range(len(GROUPS))]
        ld_nat = [sem(f"ld_nat{b}") for b in range(2)]
        const_ready = sem("const_ready")
        wsum_in, wsum_out = sem("wsum_in"), sem("wsum_out")
        amax_in, amax_out = sem("amax_in"), sem("amax_out")
        sig_ready = sem("sig_ready")
        wq_ready, xq_ready = sem("wq_ready"), sem("xq_ready")
        sup_done, q_ready = sem("sup_done"), sem("q_ready")
        at_hi, at_lo = sem("at_hi"), sem("at_lo")
        sym_ready, s_hi, s_lo = sem("sym_ready"), sem("s_hi"), sem("s_lo")
        aq_done, aq_read, x1_ready = sem("aq_done"), sem("aq_read"), sem("x1_ready")
        xs_hi, xs_lo = sem("xs_hi"), sem("xs_lo")
        sx_done, y_hi, y_lo = sem("sx_done"), sem("y_hi"), sem("y_lo")
        ay_done, ay_read, x2_ready = sem("ay_done"), sem("ay_read"), sem("x2_ready")
        pool_add = sem("pool_add")
        dve_a, dve_b, dve_ln0, dve_ln1 = sem("dve_a"), sem("dve_b"), sem("dve_ln0"), sem("dve_ln1")
        stored = sem("stored")
        scratch = nc.dram_tensor("e_dst_rows", [H, NP], F32, kind="Internal").ap()
        folded = nc.dram_tensor("folded_weights", [D + 1, D], F32, kind="Internal").ap()
        ld_w2, ld_a, ld_mlp, ld_qkv, ld_b = sem("ld_w2"), sem("ld_a"), sem("ld_mlp"), sem("ld_qkv"), sem("ld_b")
        ld_bv = sem("ld_bv")
        ld_m = [sem(f"ld_m{b}") for b in range(2)]
        x2_kept, w2_kept = sem("x2_kept"), sem("w2_kept")
        wa_ready, mask_ready = sem("wa_ready"), sem("mask_ready")
        x2T_ps, x2T_ready, wh_ps, wh_ready, e_ready, ed_ps, ed_ready = (
            sem(n) for n in ("x2T_ps", "x2T_ready", "wh_ps", "wh_ready", "e_ready", "ed_ps", "ed_ready"))
        ed_stored = sem("ed_stored")
        ld_d = [sem(f"ld_d{b}") for b in range(2)]
        pad_ready, g_ready, p_ready, pt_ps, pt_ready = (
            sem(n) for n in ("pad_ready", "g_ready", "p_ready", "pt_ps", "pt_ready"))
        o_done, enc_a, enc_b, d_used = sem("o_done"), sem("enc_a"), sem("enc_b"), sem("d_used")
        dve_w, dve_p, dve_g, dve_m, dve_3 = sem("dve_w"), sem("dve_p"), sem("dve_g"), sem("dve_m"), sem("dve_3")
        elu_e, elu_done, encT_ps, encT_ready = sem("elu_e"), sem("elu_done"), sem("encT_ps"), sem("encT_ready")
        m1_ps, m1_ready, m2_ps, m2_ready, m3_ps, m3_ready, m4_ps, m4_read = (
            sem(n) for n in ("m1_ps", "m1_ready", "m2_ps", "m2_ready", "m3_ps", "m3_ready", "m4_ps", "m4_read"))
        x3_ready, x3T_ps, x3T_hi, x3T_ready = sem("x3_ready"), sem("x3T_ps"), sem("x3T_hi"), sem("x3T_ready")
        fold_stored = [sem(f"fold_stored{b}") for b in range(2)]
        ld_qk, fold_ps, fold_ready = sem("ld_qk"), sem("fold_ps"), sem("fold_ready")
        ld_fold, bqk_ready = sem("ld_fold"), sem("bqk_ready")
        bound_in, bound_out, scale3_ready = sem("bound_in"), sem("bound_out"), sem("scale3_ready")
        wv_hi, m_hi, wv_ready, m_ready = sem("wv_hi"), sem("m_hi"), sem("wv_ready"), sem("m_ready")
        v_read, v_hi, v_lo, g_ps, g_read, g_hi, g_lo = (
            sem(n) for n in ("v_read", "v_hi", "v_lo", "g_ps", "g_read", "g_hi", "g_lo"))
        pt3_hi = sem("pt3_hi")
        v_ps = sem("v_ps")
        sc_ps, sc_read, s3_ready, p3_ready, pt3_ps, pt3_lo, o3_ps, o3_read, x4_ready = (
            sem(n) for n in ("sc_ps", "sc_read", "s3_ready", "p3_ready", "pt3_ps", "pt3_lo", "o3_ps", "o3_read", "x4_ready"))
        ld_a3 = [sem(f"ld_a3{b}") for b in range(2)]
        CH = [(0, 512), (512, 512), (1024, NP - 1024)]
        CHN = [(0, 512), (512, 512), (1024, N - 1024)]

        FOLDS = KD + 2
        FOLD_BANK = (0, 1, 6, 7, 0, 1)

        block = ctx.enter_context(nc.Block())

        def later(t):
            return not (isinstance(t, int) and t < 2)

        def at_least(t, n):
            return not (isinstance(t, int) and t < n)

        def nth(t, b):
            return t // 2 + 1 if isinstance(t, int) else pair_of[0] + 1

        pair_of = [None]

        def tiles(eng, body, peel=1):
            for t in range(2 * peel):
                body(t, t % 2)
            with eng.Fori(peel, PAIRS) as k:
                pair_of[0] = k
                body(2 * k, 0)
                body(2 * k + 1, 1)
            body(T - 1, 0)

        @block.sync
        def _(sp):
            sp.dma_start(wk3, w0.rearrange("(k p) d -> p k d", p=P)).then_inc(ld_w, 16)
            sp.dma_start(scs[:], scal).then_inc(ld_sc, 16)
            sp.dma_start(xT3, xT.rearrange("(k p) i -> p k i", p=P)).then_inc(ld_xT, 16)
            for g, (a, b) in enumerate(GROUPS):
                sp.dma_start(at_raw[:, a:b, :], adjT.rearrange("(t p) i -> p t i", p=P)[:, a:b, :]).then_inc(ld_at[g], 16)
            sp.dma_start(r_x[:], x.rearrange("(t p) d -> p t d", p=P)).then_inc(ld_x, 16)

            def nat(t, b, first):
                if not first:
                    sp.wait_ge(s_lo, t - 1)
                sp.dma_start(r_st[:, b, :], adj[bass.ts(t, P), :]).then_inc(ld_nat[b], 16)

            nat(0, 0, True)
            nat(1, 1, True)
            for col, bias, n in ((0, b1, 2), (2, b2, 1), (3, b3, 2), (5, bq, KD), (9, bk, KD)):
                sp.dma_start(bcol[:, col:col + n], bias).then_inc(ld_b, 16)
            sp.wait_ge(sup_done, T)
            for dst, src in ((wq_n, wq), (wk_n, wk)):
                sp.dma_start(dst, src.rearrange("(k p) d -> p k d", p=P)).then_inc(ld_qk, 16)
            with sp.Fori(1, PAIRS) as k:
                nat(2 * k, 0, False)
                nat(2 * k + 1, 1, False)
            nat(T - 1, 0, False)

            for n in range(KD + 1):
                sp.wait_ge(fold_ready, n + 1)
                if n < KD:
                    sp.dma_start(folded[n * P:(n + 1) * P, :], fold_row[:, n % 2, :]).then_inc(fold_stored[n % 2], 16)
                else:
                    sp.dma_start(folded[D:D + 1, :], fold_row[0:1, n % 2, :]).then_inc(fold_stored[n % 2], 16)

            sp.wait_ge(s_lo, T)
            sp.dma_start(W2_st, gat_w.rearrange("(k p) d -> p k d", p=P)).then_inc(ld_w2, 16)
            sp.wait_ge(x1_ready, T)
            sp.dma_start(a_bc.rearrange("p a d -> p (a d)"), gat_a[0].partition_broadcast(P)).then_inc(ld_a, 16)
            sp.wait_ge(sx_done, T)
            sp.dma_start(w1, w1T.rearrange("(k p) d -> p k d", p=P)).then_inc(ld_mlp, 16)
            sp.dma_start(w2, w2T.rearrange("(k p) d -> p k d", p=P)).then_inc(ld_mlp, 16)
            sp.dma_start(w3, w3T).then_inc(ld_mlp, 16)
            sp.dma_start(brow[:], b4[0].partition_broadcast(P)).then_inc(ld_mlp, 16)
            sp.wait_ge(wa_ready, 1)
            sp.wait_ge(w2_kept, 1)
            def load_mask(t, b):
                if later(t):
                    sp.wait_ge(mask_ready, t - 1)
                sp.dma_start(r_st[:, b, 0:N], adj[bass.ts(t, P), 0:N]).then_inc(ld_m[b], 16)
            tiles(sp, load_mask)
            sp.wait_ge(x2T_ps, T)
            sp.wait_ge(x2_kept, T)
            sp.dma_start(w4, w4T.rearrange("(k p) d -> p k d", p=P)).then_inc(ld_mlp, 16)
            sp.wait_ge(ed_ready, T)
            sp.dma_start(scratch, edrow).then_inc(ed_stored, 16)
            sp.wait_ge(ed_stored, 16)

            def load_d(h, b):
                sp.dma_start(drow[:, b, 0, :], scratch[bass.ts(h, 1), 0:N][0].partition_broadcast(P)).then_inc(ld_d[b], 16)

            sp.wait_ge(ay_done, T)
            load_d(0, 0)
            load_d(1, 1)
            sp.wait_ge(fold_stored[0], 16 * 3)
            sp.wait_ge(fold_stored[1], 16 * 2)
            sp.wait_ge(wh_ps, T)
            sp.dma_start(M32, folded[0:D, :].rearrange("(k p) d -> p k d", p=P)).then_inc(ld_fold, 16)
            sp.dma_start(w_row, folded[D:D + 1, :][0].partition_broadcast(P)).then_inc(ld_fold, 16)
            with sp.Fori(1, H // 2) as hp:
                sp.wait_ge(d_used, 2 * hp - 1)
                load_d(2 * hp, 0)
                sp.wait_ge(d_used, 2 * hp)
                load_d(2 * hp + 1, 1)

            sp.wait_ge(o_done, H * T)
            sp.dma_start(wv, wvT.rearrange("(k p) d -> p k d", p=P)).then_inc(ld_qkv, 16)
            sp.dma_start(v_row, bv[0].partition_broadcast(P)).then_inc(ld_bv, 16)

            for t in range(T):
                if t >= 2:
                    sp.wait_ge(sc_read, t - 1)
                sp.dma_start(r_st[:, t % 2, 0:N], adj[bass.ts(t, P), 0:N]).then_inc(ld_a3[t % 2], 16)
                if t >= 2:
                    sp.wait_ge(x4_ready, t - 1)
                    sp.dma_start(out[bass.ts(t - 2, P), :], r_x[:, t - 2, :]).then_inc(stored, 16)
            sp.wait_ge(x4_ready, T - 1)
            sp.dma_start(out[bass.ts(T - 2, P), :], r_x[:, T - 2, :]).then_inc(stored, 16)
            sp.wait_ge(x4_ready, T)
            sp.dma_start(out[(T - 1) * P:N, :], r_x[0:LAST, T - 1, :]).then_inc(stored, 16)
            sp.wait_ge(stored, 16 * T)

        @block.gpsimd
        def _(pool):
            nc.gpsimd.memset(ident[:], 0.0).then_inc(const_ready, 1)
            nc.gpsimd.memset(ident2[:], 0.0).then_inc(const_ready, 1)
            nc.gpsimd.memset(ones[:], 1.0).then_inc(const_ready, 1)
            pool.wait_ge(const_ready, 3)
            for m, v in ((ident, 1.0), (ident2, 2.0)):
                nc.gpsimd.affine_select(out=m[:], in_=m[:], compare_op=ALU.not_equal, fill=v, base=0,
                                        pattern=[[-1, P]], channel_multiplier=1).then_inc(const_ready, 1)
            pool.wait_ge(amax_in, 1)
            nc.gpsimd.partition_all_reduce(amax[:, 5:6], amax[:, 4:5], P, RMAX).then_inc(amax_out, 1)
            pool.wait_ge(const_ready, 5)

            pool.wait_ge(ld_b, 16 * 5)
            nc.gpsimd.tensor_tensor(bqk[:], bcol[:, 5:5 + KD], bcol[:, 9:9 + KD], ALU.mult).then_inc(bqk_ready, 1)

            def sym_at(t, b, n):
                pool.wait_ge(ld_nat[b], 16 * n)
                nc.gpsimd.tensor_tensor(r_st[:, b, :], r_st[:, b, :], at_raw[:, t, :], ALU.add).then_inc(pool_add, 1)
                pool.wait_ge(pool_add, t + 1)
                d = r_st[:, b, bass.ts(t, P)]
                nc.gpsimd.tensor_tensor(d, d, ident2[:], ALU.add).then_inc(sym_ready, 1)

            sym_at(0, 0, 1)
            sym_at(1, 1, 1)
            with pool.Fori(1, PAIRS) as k:
                sym_at(2 * k, 0, k + 1)
                sym_at(2 * k + 1, 1, k + 1)
            sym_at(T - 1, 0, PAIRS + 1)

            pool.wait_ge(bound_in, 1)
            nc.gpsimd.partition_all_reduce(bound[:], amax[:, 0:4], P, RMAX).then_inc(bound_out, 1)

        @block.scalar
        def _(act):
            act.wait_ge(sig_ready, 1)
            for t in range(T):
                nc.scalar.activation(r_at[:, 0, t, :], at_raw[:, t, :], ACT.Copy, scale=c(SIG)).then_inc(at_hi, 1)
            act.wait_ge(at_lo, T)

            def sym_hi(t, b):
                act.wait_ge(sym_ready, t + 1)
                nc.scalar.activation(r_s[:, t, 0, :], r_st[:, b, :], ACT.Copy, scale=c(SIGH),
                                     accum_out=dcol[:, bass.ts(t, 1)]).then_inc(s_hi, 1)
            tiles(act, sym_hi)

            act.wait_ge(sup_done, T)
            for n in range(FOLDS):
                src = ps[:, FOLD_BANK[n], :]
                act.wait_ge(fold_ps, n + 1)
                if 2 <= n < KD + 1:
                    act.wait_ge(fold_stored[n % 2], 16 * (n // 2))
                if n < KD:
                    nc.scalar.activation(fold_row[:, n % 2, :], src, ACT.Copy).then_inc(fold_ready, 1)
                elif n == KD:
                    nc.scalar.activation(fold_row[0:1, n % 2, :], src[0:1, :], ACT.Copy).then_inc(fold_ready, 1)
                else:
                    nc.scalar.activation(fold[:], src[:, 0:KD + 1], ACT.Copy).then_inc(fold_ready, 1)

            act.wait_ge(aq_done, T)
            def x1_hi(t, b):
                act.wait_ge(x1_ready, t + 1)
                nc.scalar.activation(r_xs[:, 0, t, :], r_x[:, t, :], ACT.Copy,
                                     scale=dcol[:, bass.ts(t, 1)]).then_inc(xs_hi, 1)
            tiles(act, x1_hi)

            act.wait_ge(fold_stored[0], 16 * 3)
            act.wait_ge(fold_stored[1], 16 * 2)

            def y_high(t, b):
                act.wait_ge(sx_done, t + 1)
                nc.scalar.activation(r_y[:, 0, t, :], ps[:, 4 + b, :], ACT.Copy,
                                     scale=ycol[:, bass.ts(t, 1)]).then_inc(y_hi, 1)
            tiles(act, y_high)

            act.wait_ge(sx_done, T)
            act.wait_ge(ld_w2, 16)
            nc.scalar.activation(W2, W2_st, ACT.Copy).then_inc(w2_kept, 1)

            def x2T_out(t, b):
                act.wait_ge(x2T_ps, t + 1)
                if later(t):
                    act.wait_ge(wh_ps, t - 1)
                nc.scalar.activation(x2T[:, b], ps[:, b, :].rearrange("p (k i) -> p k i", k=KD), ACT.Copy).then_inc(x2T_ready, 1)

            def wh_out(t, b):
                act.wait_ge(wh_ps, t + 1)
                nc.scalar.activation(Wh[:, t, :, 0:HD], ps[:, 4 + b, :].rearrange("p (h d) -> p h d", h=H),
                                     ACT.Copy).then_inc(wh_ready, 1)

            def project_out(t, b):
                if at_least(t, 1):
                    x2T_out(t - 1, 1 - b)
                if at_least(t, 2):
                    wh_out(t - 2, b)
                act.wait_ge(x2_ready, t + 1)
                nc.scalar.activation(r_x[:, t, :], x2[:, b, :], ACT.Copy).then_inc(x2_kept, 1)

            tiles(act, project_out, 2)
            x2T_out(T - 1, 0)
            wh_out(T - 2, 1)
            wh_out(T - 1, 0)

            def take_pt(n, s):
                act.wait_ge(pt_ps, n + 1)
                if later(n):
                    act.wait_ge(o_done, n - 1)
                b = 3 * (s % 2)
                nc.scalar.activation(PT[:, s % 2, :], ps[:, b:b + 3, :].rearrange("p b i -> p (b i)")[:, 0:NP],
                                     ACT.Copy).then_inc(pt_ready, 1)

            act.wait_ge(pad_ready, 2)

            def exps(hp):
                first = isinstance(hp, int)
                for s in range(2 * T):
                    n = hp * 2 * T + s
                    act.wait_ge(g_ready, n + 1)
                    if not (first and s < 2):
                        act.wait_ge(pt_ps, n - 1)
                    nc.scalar.activation(PR[s % 2][:, 0:N], G[:, s % 2, :], ACT.Exp, scale=-1.0,
                                         bias=nmax[:, s % 2:s % 2 + 1]).then_inc(p_ready, 1)
                    if not (first and s == 0):
                        take_pt(n - 1, (s - 1) % 2)
            exps(0)
            with act.Fori(1, H // 2) as hp:
                exps(hp)
            take_pt(H * T - 1, 1)

            act.wait_ge(enc_b, H)

            def elu_exp(t):
                if t >= 2:
                    act.wait_ge(elu_done, t - 1)
                nc.scalar.activation(pre[:, t % 2, :], enc[:, t, :], ACT.Exp).then_inc(elu_e, 1)

            def take_encT(t):
                act.wait_ge(encT_ps, t + 1)
                nc.scalar.activation(encT[:, :, bass.ts(t, P)], ps[:, t % 2, :].rearrange("p (k i) -> p k i", k=KD),
                                     ACT.Copy).then_inc(encT_ready, 1)

            def relu1(n):
                i, w = CH[n]
                for m in range(2):
                    act.wait_ge(m1_ps, 2 * n + m + 1)
                    nc.scalar.activation(o1T[:, m, i:i + w], ps[:, 2 + m, 0:w], ACT.Relu,
                                         bias=bcol[:, m:m + 1]).then_inc(m1_ready, 1)

            def relu2(n):
                i, w = CH[n]
                act.wait_ge(m2_ps, n + 1)
                nc.scalar.activation(o2T[:, i:i + w], ps[:, 4, 0:w], ACT.Relu, bias=bcol[:, 2:3]).then_inc(m2_ready, 1)

            def relu3(n):
                i, w = CH[n]
                for m in range(2):
                    act.wait_ge(m3_ps, 2 * n + m + 1)
                    nc.scalar.activation(o3T[:, m, i:i + w], ps[:, 5 - m, 0:w], ACT.Relu,
                                         bias=bcol[:, 3 + m:4 + m]).then_inc(m3_ready, 1)

            elu_exp(0)
            elu_exp(1)
            for t in range(4):
                elu_exp(t + 2)
                take_encT(t)
            relu1(0)
            for t in range(4, 8):
                elu_exp(t + 2)
                take_encT(t)
            elu_exp(T - 1)
            relu2(0)
            relu1(1)
            relu3(0)
            for t in range(8, T):
                take_encT(t)
            relu2(1)
            relu1(2)
            relu3(1)
            act.wait_ge(scale3_ready, 1)
            nc.scalar.activation(wv_parts[:, 0], wv, ACT.Copy, scale=sig3[:, 2:3]).then_inc(wv_hi, 1)
            nc.scalar.activation(m_parts[:, 0], M32, ACT.Copy, scale=sig3[:, 0:1]).then_inc(m_hi, 1)
            relu2(2)
            relu3(2)

            def x3T_high(t):
                act.wait_ge(x3T_ps, t + 1)
                nc.scalar.activation(x3T[:, 0, :, bass.ts(t, P)], ps[:, t % 2, :].rearrange("p (k i) -> p k i", k=KD),
                                     ACT.Copy, scale=X_SCALE).then_inc(x3T_hi, 1)

            def v_high(t):
                act.wait_ge(v_read, t + 1)
                nc.scalar.activation(vv[:, 0, t, :], v32[:, t % 2, :], ACT.Copy).then_inc(v_hi, 1)

            x3T_high(0)
            x3T_high(1)
            for t in range(2, T):
                v_high(t - 2)
                x3T_high(t)
            v_high(T - 2)
            v_high(T - 1)

            def g_high(t):
                act.wait_ge(g_read, t + 1)
                if t >= 2:
                    act.wait_ge(sc_ps, t - 1)
                nc.scalar.activation(g_parts[:, t % 2, 0], g32[:, t % 2], ACT.Copy).then_inc(g_hi, 1)

            def soft(t):
                b = t % 2
                act.wait_ge(s3_ready, t + 1)
                nc.scalar.activation(S3[:, b, 0:N], S3[:, b, 0:N], ACT.Exp, scale=kc(KAPPA),
                                     bias=nmax[:, b:b + 1], accum_out=rs3[:, b:b + 1]).then_inc(p3_ready, 1)

            g_high(0)
            g_high(1)
            soft(0)
            for t in range(T):
                b = t % 2
                act.wait_ge(pt3_ps, t + 1)
                if t >= 2:
                    act.wait_ge(o3_ps, t - 1)
                nc.scalar.activation(PT3[:, b, 0, :], ps[:, 3:6, :].rearrange("p b i -> p (b i)")[:, 0:NP],
                                     ACT.Copy, scale=P_SCALE).then_inc(pt3_hi, 1)
                if t + 1 < T:
                    soft(t + 1)
                if t + 2 < T:
                    g_high(t + 2)

        @block.vector
        def _(dve):
            v = nc.vector
            ch = Chain(dve, dve_a)

            def rsqrt(ch, y, val, a):
                ch(v.tensor_scalar(a.bitcast(I32), val.bitcast(I32), 1, None, ALU.logical_shift_right))
                ch(v.tensor_scalar(y.bitcast(I32), a.bitcast(I32), -1.0, float(RSQRT_SEED), ALU.mult, ALU.add))
                for _ in range(3):
                    if y.shape[-1] == 1:
                        ch(v.scalar_tensor_tensor(out=a, in0=y, scalar=val, in1=y, op0=ALU.mult, op1=ALU.mult))
                    else:
                        ch(v.tensor_tensor(a, y, y, ALU.mult))
                        ch(v.tensor_tensor(a, a, val, ALU.mult))
                    ch(v.tensor_scalar(a, a, -0.5, 1.5, ALU.mult, ALU.add))
                    ch(v.tensor_tensor(y, y, a, ALU.mult))

            dve.wait_ge(ld_w, 16)
            v.tensor_reduce(rv[:, 0:1], wlev, AX_X, ALU.add).then_inc(wsum_in, 1)
            dve.wait_ge(wsum_out, 1)
            ch(v.tensor_scalar(c(MEAN), ps[:, 7, 0:1], 1.0 / (D * D), None, ALU.mult))
            ch(v.tensor_scalar(wlev, wlev, c(MEAN), None, ALU.subtract))
            v.tensor_tensor_reduce(out=wtmp, in0=wlev, in1=wlev, scale=1.0, scalar=0.0, op0=ALU.mult, op1=ALU.add,
                                   accum_out=rv[:, 1:2]).then_inc(wsum_in, 1)
            dve.wait_ge(wsum_out, 2)
            ch(v.tensor_scalar(rv[:, 2:3], ps[:, 7, 1:2], 1.0 / (D * D - 1), None, ALU.mult))
            rsqrt(ch, c(RSTD), rv[:, 2:3], rv[:, 3:4])
            dve.wait_ge(ld_sc, 16)
            ch(v.reciprocal(c(RWA), scs[:, 1:2]))
            ch(v.tensor_scalar(wlev, wlev, c(RSTD), c(RWA), ALU.mult, ALU.mult))
            ch(v.tensor_scalar(wlev, wlev, 1.0, -1.0, ALU.min, ALU.max))
            ch(v.tensor_scalar(wlev, wlev, W_LEVELS, ROUND, ALU.mult, ALU.add))
            v.tensor_scalar(wlev, wlev, ROUND, None, ALU.subtract).then_inc(wq_ready, 1)

            ch(v.reciprocal(c(RALPHA), scs[:, 2:3]))
            dve.wait_ge(ld_xT, 16)
            ch(v.tensor_scalar(xTf, xTf, c(RALPHA), 1.0, ALU.mult, ALU.min))
            ch(v.tensor_scalar(xTf, xTf, X_LEVELS, ROUND, ALU.mult, ALU.add))
            v.tensor_scalar(xTf, xTf, ROUND, None, ALU.subtract).then_inc(xq_ready, 1)

            ch(v.tensor_scalar(c(C_Q), scs[:, 2:3], 1.0 / X_LEVELS, None, ALU.mult))
            ch(v.tensor_scalar(c(TMP), scs[:, 1:2], 1.0 / W_LEVELS, c(C_Q), ALU.mult, ALU.mult))
            ch(v.reciprocal(rv[:, 4:5], scs[:, 3:4]))
            ch(v.tensor_scalar(c(C_Q), c(TMP), rv[:, 4:5], None, ALU.mult))

            for g, (a, b) in enumerate(GROUPS):
                dve.wait_ge(ld_at[g], 16)
                ch(v.tensor_reduce(amax[:, g:g + 1], at_raw[:, a:b, :].rearrange("p t i -> p (t i)"), AX_X, ALU.max,
                                   apply_absolute_value=True))
            v.tensor_reduce(amax[:, 4:5], amax[:, 0:4], AX_X, ALU.max).then_inc(amax_in, 1)
            dve.wait_ge(amax_out, 1)
            ch(v.tensor_scalar(c(TMP), amax[:, 5:6], 1.0, None, ALU.add))
            ch(v.tensor_scalar(c(RSIG).bitcast(I32), c(TMP).bitcast(I32), 0x7F800000, None, ALU.bitwise_and))
            ch(v.tensor_scalar(c(RSIG), c(RSIG), 1.0 / A_TOP, None, ALU.mult))
            ch(v.reciprocal(c(SIG), c(RSIG)))
            v.tensor_scalar(c(SIGH), c(SIG), 0.5, None, ALU.mult).then_inc(sig_ready, 1)
            ch(v.reciprocal(rv[:, 5:6], scs[:, 0:1]))
            ch(v.tensor_scalar(rv[:, 6:7], rv[:, 5:6], scs[:, 0:1], 1.0 / X_LEVELS, ALU.mult, ALU.mult))
            ch(v.tensor_scalar(c(F0), rv[:, 6:7], scs[:, 3:4], c(RSIG), ALU.mult, ALU.mult))
            ch(v.tensor_scalar(c(F1), c(RSIG), 1.0 / Y_SCALE, None, ALU.mult))
            ch(v.tensor_scalar(c(CY), c(RSIG), Y_SCALE / (X_SCALE * X_SCALE), None, ALU.mult))

            for t in range(T):
                b = t % 2
                dve.wait_ge(sup_done, t + 1)
                if t >= 2:
                    dve.wait_ge(q_ready, t - 1)
                ch(v.tensor_scalar(pre[:, b, :], ps[:, b, :], c(C_Q), 0.0, ALU.mult, ALU.max))
                ch(v.tensor_scalar(pre[:, b, :], pre[:, b, :], 1.0, X_LEVELS, ALU.min, ALU.mult))
                v.tensor_scalar(q[:, t, :], pre[:, b, :], ROUND, ROUND, ALU.add, ALU.subtract).then_inc(q_ready, 1)
                dve.wait_ge(at_hi, t + 1)
                v.scalar_tensor_tensor(out=r_at[:, 1, t, :], in0=at_raw[:, t, :], scalar=c(SIG), in1=r_at[:, 0, t, :],
                                       op0=ALU.mult, op1=ALU.subtract).then_inc(at_lo, 1)
            dve.wait_ge(at_lo, T)
            dve.wait_ge(q_ready, T)

            def layer_norm(ch, t, b, also_degree, dst=None):
                ch(v.bn_stats(bns[:], pre[:, b, :]))
                v.memset(junk[:], 0.0)
                ch(v.bn_aggr(mv[:], bns[:]))
                n = 1
                ch(v.tensor_scalar(rv[:, 0:1], mv[:, 1:2], LN_EPS, None, ALU.add))
                if also_degree:
                    n = 2
                    dve.wait_ge(s_hi, t + 1)
                    ch(v.tensor_scalar(rv[:, 1:2], dcol[:, bass.ts(t, 1)], c(RSIG), 1e-30, ALU.mult, ALU.max))
                rsqrt(ch, rv[:, 2:2 + n], rv[:, 0:n], rv[:, 4:4 + n])
                if also_degree:
                    ch(v.tensor_scalar(rv[:, 6:7], dcol[:, bass.ts(t, 1)], 0.0, X_SCALE, ALU.is_gt, ALU.mult))
                    ch(v.tensor_scalar(dcol[:, bass.ts(t, 1)], rv[:, 6:7], rv[:, 3:4], None, ALU.mult))
                    ch(v.tensor_scalar(ycol[:, bass.ts(t, 1)], dcol[:, bass.ts(t, 1)], c(CY), None, ALU.mult))
                return v.tensor_scalar(r_x[:, t, :] if dst is None else dst, pre[:, b, :], mv[:, 0:1], rv[:, 2:3],
                                       ALU.subtract, ALU.mult)

            dve.wait_ge(ld_x, 16)
            K0 = 1 + 1 + 1 + 1 + 1 + 14 + 3

            def ln0(t, b):
                dve.wait_ge(s_hi, t + 1)
                v.scalar_tensor_tensor(out=r_s[:, t, 1, :], in0=r_st[:, b, :], scalar=c(SIGH), in1=r_s[:, t, 0, :],
                                       op0=ALU.mult, op1=ALU.subtract).then_inc(s_lo, 1)
                ch = Chain(dve, dve_ln0, t * K0)
                dve.wait_ge(aq_done, t + 1)
                v.scalar_tensor_tensor(out=pre[:, b, :], in0=ps[:, 2 + b, :], scalar=c(F0), in1=r_x[:, t, :],
                                       op0=ALU.mult, op1=ALU.add).then_inc(aq_read, 1)
                dve.wait_ge(aq_read, t + 1)
                layer_norm(ch, t, b, True).then_inc(x1_ready, 1)
                assert ch.n == K0 - 1, ch.n
                dve.wait_ge(x1_ready, t + 1)
                v.memset(junk[:], 0.0).then_inc(dve_ln0, 1)
            tiles(dve, ln0)

            def x1_lo(t, b):
                dve.wait_ge(xs_hi, t + 1)
                v.scalar_tensor_tensor(out=r_xs[:, 1, t, :], in0=r_x[:, t, :], scalar=dcol[:, bass.ts(t, 1)],
                                       in1=r_xs[:, 0, t, :], op0=ALU.mult, op1=ALU.subtract).then_inc(xs_lo, 1)
            tiles(dve, x1_lo)

            ch = Chain(dve, dve_w)
            dve.wait_ge(ld_w2, 16)
            dve.wait_ge(ld_a, 16)
            for k in range(KD):
                for a in range(2):
                    ch(v.tensor_tensor(prod, W2_st[:, k, :], a_bc[:, a], ALU.mult))
                    ch(v.tensor_reduce(wa[:, k, a * H:(a + 1) * H], prod.rearrange("p (h d) -> p h d", h=H), AX_X, ALU.add))
            v.memset(junk[:], 0.0).then_inc(wa_ready, 1)

            def y_low(t, b):
                dve.wait_ge(y_hi, t + 1)
                v.scalar_tensor_tensor(out=r_y[:, 1, t, :], in0=ps[:, 4 + b, :], scalar=ycol[:, bass.ts(t, 1)],
                                       in1=r_y[:, 0, t, :], op0=ALU.mult, op1=ALU.subtract).then_inc(y_lo, 1)
            tiles(dve, y_low)

            ch = Chain(dve, dve_p)
            dve.wait_ge(sx_done, T)
            dve.wait_ge(wa_ready, 1)

            K1 = 1 + 1 + 1 + 11 + 1

            def ln1(t, b):
                ch = Chain(dve, dve_ln1, t * K1)
                dve.wait_ge(ay_done, t + 1)
                if later(t):
                    dve.wait_ge(x2_kept, t - 1)
                    dve.wait_ge(x2T_ps, t - 1)
                v.scalar_tensor_tensor(out=pre[:, b, :], in0=ps[:, 2 + b, :], scalar=c(F1), in1=r_x[:, t, :],
                                       op0=ALU.mult, op1=ALU.add).then_inc(ay_read, 1)
                dve.wait_ge(ay_read, t + 1)
                layer_norm(ch, t, b, False, x2[:, b, :]).then_inc(x2_ready, 1)
                assert ch.n == K1 - 1, ch.n
                dve.wait_ge(ld_m[b], 16 * nth(t, b))
                v.tensor_scalar(mask[:, t, :], r_st[:, b, 0:N], 0.0, NEG, ALU.is_le, ALU.mult).then_inc(mask_ready, 1)
                dve.wait_ge(x2_ready, t + 1)
                v.memset(junk[:], 0.0).then_inc(dve_ln1, 1)
                if at_least(t, 2):
                    logits(t - 2, b)
                if at_least(t, 3):
                    take_ed(t - 3, 1 - b)

            def logits(t, b):
                dve.wait_ge(wh_ps, t + 1)
                if later(t):
                    dve.wait_ge(ed_ps, t - 1)
                v.tensor_copy(ed[:, b, :], ps[:, 6 + b, H:2 * H]).then_inc(e_ready, 1)
                v.tensor_scalar(es[:, :, bass.ts(t, 1)], ps[:, 6 + b, 0:H].unsqueeze(2), 1.0 - LEAK, None,
                                ALU.mult).then_inc(e_ready, 1)

            def take_ed(t, b):
                dve.wait_ge(ed_ps, t + 1)
                v.tensor_copy(edrow[:, bass.ts(t, P)], ps[0:H, 6 + b, P:2 * P]).then_inc(ed_ready, 1)

            tiles(dve, ln1, 2)
            logits(T - 2, 1)
            take_ed(T - 3, 0)
            logits(T - 1, 0)
            take_ed(T - 2, 1)
            take_ed(T - 1, 0)
            dve.wait_ge(ay_done, T)
            ch(v.memset(Wh[:, :, :, HD:HW], 1.0))
            v.memset(PR0[:, N:NP], 0.0).then_inc(pad_ready, 1)

            dve.wait_ge(e_ready, 2 * T)
            dve.wait_ge(mask_ready, T)
            dve.wait_ge(ed_stored, 16)
            v.memset(PR1[:, N:NP], 0.0).then_inc(pad_ready, 1)
            dve.wait_ge(pad_ready, 2)
            KG = 1 + 2 * T + 2 + 2 * 2

            def take_enc(ch, h, bank, t0, nt):
                src = ps[:, bank, 0:nt * HW].rearrange("p (t d) -> p t d", t=nt)
                ch(v.reciprocal(rsum[:, 0:nt], src[:, :, HD]))
                return v.tensor_tensor(enc[:, t0:t0 + nt, bass.ts(h, HD)], src[:, :, 0:HD],
                                       rsum[:, 0:nt].unsqueeze(2).broadcast_to([P, nt, HD]), ALU.mult)

            def scores(hp):
                first = isinstance(hp, int)
                ch = Chain(dve, dve_g, hp * KG)
                ch(v.tensor_copy(es_pair[:], es[:, bass.ts(hp, 2), :].rearrange("p h t -> p (h t)")))
                for s in range(2 * T):
                    hh, t = divmod(s, T)
                    n = hp * 2 * T + s
                    b = s % 2
                    if t == 0:
                        dve.wait_ge(ld_d[hh], 16 * (hp + 1))
                        ch(v.tensor_scalar(drow[:, hh, 1, :], drow[:, hh, 0, :], LEAK, None, ALU.mult))
                    if not (first and s < 2):
                        dve.wait_ge(p_ready, n - 1)
                    ch(v.scalar_tensor_tensor(out=G[:, b, :], in0=drow[:, hh, 0, :], scalar=es_pair[:, s:s + 1],
                                              in1=drow[:, hh, 1, :], op0=ALU.add, op1=ALU.max))
                    v.memset(junk[:], 0.0)
                    v.tensor_tensor_reduce(out=G[:, b, :], in0=G[:, b, :], in1=mask[:, t, :], scale=-1.0,
                                           scalar=BIG, op0=ALU.add, op1=ALU.min,
                                           accum_out=nmax[:, b:b + 1]).then_inc(g_ready, 1)
                    if t == T - 1:
                        dve.wait_ge(g_ready, n + 1)
                        v.memset(junk[:], 0.0).then_inc(d_used, 1)
                    if t == 9:
                        dve.wait_ge(o_done, (2 * hp + hh) * T + TA)
                        take_enc(ch, 2 * hp + hh, 6, 0, TA).then_inc(enc_a, 1)
                        dve.wait_ge(enc_a, 2 * hp + hh + 1)
                    if t == 3 and not (first and hh == 0):
                        dve.wait_ge(o_done, (2 * hp + hh) * T)
                        take_enc(ch, 2 * hp + hh - 1, 7, TA, T - TA).then_inc(enc_b, 1)
                        dve.wait_ge(enc_b, 2 * hp + hh)
                if first:
                    ch(v.nop())
                assert ch.n == KG
            scores(0)
            with dve.Fori(1, H // 2) as hp:
                scores(hp)
            ch = Chain(dve, dve_m)
            dve.wait_ge(o_done, H * T)
            take_enc(ch, H - 1, 7, TA, T - TA).then_inc(enc_b, 1)
            dve.wait_ge(enc_b, H)

            for t in range(T):
                b = t % 2
                dve.wait_ge(elu_e, t + 1)
                ch(v.tensor_scalar(pre[:, b, :], pre[:, b, :], 1.0, -1.0, ALU.min, ALU.add))
                v.tensor_tensor(enc[:, t, :], enc[:, t, :], pre[:, b, :], ALU.max).then_inc(elu_done, 1)
            dve.wait_ge(elu_done, T)
            dve.wait_ge(fold_ready, FOLDS)
            dve.wait_ge(ld_fold, 16 * 2)
            dve.wait_ge(ld_qkv, 16)
            dve.wait_ge(ld_bv, 16)
            for n, src in enumerate((M32.rearrange("p k d -> p (k d)"), fold[:, 0:KD],
                                     wv.rearrange("p k d -> p (k d)"), v_row)):
                ch(v.tensor_reduce(amax[:, n:n + 1], src, AX_X, ALU.max, apply_absolute_value=True))
            v.memset(junk[:], 0.0).then_inc(bound_in, 1)
            dve.wait_ge(bound_out, 1)
            for n in (1, 3):
                ch(v.scalar_tensor_tensor(out=bound[:, n:n + 1], in0=bound[:, n - 1:n], scalar=float(D),
                                          in1=bound[:, n:n + 1], op0=ALU.mult, op1=ALU.add))
            ch(v.tensor_scalar(bound[:], bound[:], 1e-18, None, ALU.max))
            ch(v.tensor_scalar(r_sig3[:].bitcast(I32), bound[:].bitcast(I32), 0x7F800000, None, ALU.bitwise_and))
            ch(v.tensor_scalar(r_sig3[:], r_sig3[:], 1.0 / A_TOP, None, ALU.mult))
            ch(v.reciprocal(sig3[:], r_sig3[:]))
            v.memset(junk[:], 0.0).then_inc(scale3_ready, 1)
            for dst, src, by in ((A_G, 1, 0), (A_V, 3, 2)):
                ch(v.tensor_scalar(kc(dst), sig3[:, src:src + 1], r_sig3[:, by:by + 1], 1.0 / X_SCALE, ALU.mult, ALU.mult))
            ch(v.tensor_scalar(kc(KAPPA), r_sig3[:, 1:2], -float(D) ** -0.5 / X_SCALE, None, ALU.mult))
            ch(v.tensor_scalar(kc(NEG_K), sig3[:, 1:2], NEG3 * float(D) ** 0.5 * X_SCALE, None, ALU.mult))
            ch(v.tensor_scalar(kc(R_V), r_sig3[:, 3:4], 1.0 / P_SCALE, None, ALU.mult))
            ch(v.tensor_scalar(kc(S_R), sig3[:, 1:2], X_SCALE, None, ALU.mult))
            ch(v.tensor_scalar(w_row, w_row, kc(S_R), None, ALU.mult))
            ch(v.tensor_scalar(fold[:, KD:KD + 1], fold[:, KD:KD + 1], kc(S_R), None, ALU.mult))
            ch(v.tensor_scalar(fold[:, 0:KD], fold[:, 0:KD], sig3[:, 1:2], None, ALU.mult))
            ch(v.tensor_scalar(v_row, v_row, sig3[:, 3:4], None, ALU.mult))
            for b in range(2):
                ch(v.memset(S3[:, b, N:NP], 0.0))

            def ln2(t):
                b = t % 2
                dve.wait_ge(m4_ps, t + 1)
                v.tensor_tensor(pre[:, b, :], ps[:, 6 + b, :], brow[:], ALU.add).then_inc(m4_read, 1)
                dve.wait_ge(m4_read, t + 1)
                ch(v.tensor_tensor(pre[:, b, :], pre[:, b, :], r_x[:, t, :], ALU.add))
                layer_norm(ch, t, b, False).then_inc(x3_ready, 1)
                dve.wait_ge(x3_ready, t + 1)

            def x3T_low(t):
                dve.wait_ge(x3T_hi, t + 1)
                v.scalar_tensor_tensor(out=x3T[:, 1, :, bass.ts(t, P)],
                                       in0=ps[:, t % 2, :].rearrange("p (k i) -> p k i", k=KD), scalar=X_SCALE,
                                       in1=x3T[:, 0, :, bass.ts(t, P)], op0=ALU.mult, op1=ALU.subtract).then_inc(x3T_ready, 1)

            def take_v(t):
                dve.wait_ge(v_ps, t + 1)
                v.scalar_tensor_tensor(out=v32[:, t % 2, :], in0=ps[:, 2 + t % 2, :], scalar=kc(A_V), in1=v_row,
                                       op0=ALU.mult, op1=ALU.add).then_inc(v_read, 1)

            def v_low(t):
                dve.wait_ge(v_hi, t + 1)
                v.tensor_tensor(vv[:, 1, t, :], v32[:, t % 2, :], vv[:, 0, t, :], ALU.subtract).then_inc(v_lo, 1)
                dve.wait_ge(v_lo, t + 1)

            dve.wait_ge(ld_mlp, 16 * 5)
            for t in range(T + 3):
                if t < T:
                    ln2(t)
                if 1 <= t <= T:
                    x3T_low(t - 1)
                if t == 1:
                    dve.wait_ge(wv_hi, 1)
                    v.scalar_tensor_tensor(out=wv_parts[:, 1], in0=wv, scalar=sig3[:, 2:3], in1=wv_parts[:, 0],
                                           op0=ALU.mult, op1=ALU.subtract).then_inc(wv_ready, 1)
                if t == 3:
                    dve.wait_ge(m_hi, 1)
                    v.scalar_tensor_tensor(out=m_parts[:, 1], in0=M32, scalar=sig3[:, 0:1], in1=m_parts[:, 0],
                                           op0=ALU.mult, op1=ALU.subtract).then_inc(m_ready, 1)
                if 3 <= t:
                    v_low(t - 3)
                if 2 <= t < T + 2:
                    take_v(t - 2)

            def take_g(t):
                b = t % 2
                dve.wait_ge(g_ps, t + 1)
                v.scalar_tensor_tensor(out=g32[:, b], in0=ps[:, 6, :].rearrange("p (k i) -> p k i", k=KD), scalar=kc(A_G),
                                       in1=fold[:, 0:KD].unsqueeze(2).broadcast_to([P, KD, P]), op0=ALU.mult,
                                       op1=ALU.add).then_inc(g_read, 1)
                dve.wait_ge(g_hi, t + 1)
                v.tensor_tensor(g_parts[:, b, 1], g32[:, b], g_parts[:, b, 0], ALU.subtract).then_inc(g_lo, 1)
                dve.wait_ge(g_lo, t + 1)

            def row_part(t):
                ch(v.tensor_tensor_reduce(out=pre[:, t % 2, :], in0=r_x[:, t, :], in1=w_row, scale=1.0, scalar=0.0,
                                          op0=ALU.mult, op1=ALU.add, accum_out=r_col[:, t:t + 1]))
                ch(v.tensor_scalar(r_col[:, t:t + 1], r_col[:, t:t + 1], fold[:, KD:KD + 1], None, ALU.add))

            def masked(t):
                b = t % 2
                dve.wait_ge(sc_ps, t + 1)
                dve.wait_ge(ld_a3[b], 16 * (t // 2 + 1))
                if t >= 2:
                    dve.wait_ge(pt3_ps, t - 1)
                v.scalar_tensor_tensor(out=S3[:, b, 0:N], in0=ps[:, 0:3, :].rearrange("p b i -> p (b i)")[:, 0:N],
                                       scalar=r_col[:, t:t + 1], in1=r_st[:, b, 0:N], op0=ALU.add,
                                       op1=ALU.mult).then_inc(sc_read, 1)
                dve.wait_ge(sc_read, t + 1)
                ch(v.tensor_scalar(Z3[:, 0:N], S3[:, b, 0:N], 0.0, kc(NEG_K), ALU.is_equal, ALU.mult))
                ch(v.tensor_tensor_reduce(out=S3[:, b, 0:N], in0=S3[:, b, 0:N], in1=Z3[:, 0:N], scale=-1.0,
                                          scalar=BIG, op0=ALU.add, op1=ALU.min, accum_out=rv[:, 7:8]))
                v.tensor_scalar(nmax[:, b:b + 1], rv[:, 7:8], kc(KAPPA), -1.0, ALU.mult, ALU.mult).then_inc(s3_ready, 1)
                dve.wait_ge(s3_ready, t + 1)

            def pt_low(t):
                b = t % 2
                dve.wait_ge(pt3_hi, t + 1)
                v.scalar_tensor_tensor(out=PT3[:, b, 1, :], in0=ps[:, 3:6, :].rearrange("p b i -> p (b i)")[:, 0:NP],
                                       scalar=P_SCALE, in1=PT3[:, b, 0, :], op0=ALU.mult, op1=ALU.subtract).then_inc(pt3_lo, 1)

            def finish(t):
                b = t % 2
                dve.wait_ge(o3_ps, t + 1)
                ch(v.reciprocal(rsum[:, 0:1], rs3[:, b:b + 1]))
                ch(v.tensor_scalar(rsum[:, 1:2], rsum[:, 0:1], kc(R_V), None, ALU.mult))
                v.tensor_scalar(pre[:, b, :], ps[:, 7, :], rsum[:, 1:2], 0.0, ALU.mult, ALU.max).then_inc(o3_read, 1)
                dve.wait_ge(o3_read, t + 1)
                ch(v.tensor_tensor(pre[:, b, :], pre[:, b, :], r_x[:, t, :], ALU.add))
                layer_norm(ch, t, b, False).then_inc(x4_ready, 1)
                dve.wait_ge(x4_ready, t + 1)

            take_g(0)
            take_g(1)
            row_part(0)
            masked(0)
            for t in range(T):
                pt_low(t)
                if t + 1 < T:
                    row_part(t + 1)
                    masked(t + 1)
                if t + 2 < T:
                    take_g(t + 2)
                finish(t)

        @block.tensor
        def _(pe):
            mm = nc.tensor.matmul
            pe.wait_ge(const_ready, 5)
            for n in range(2):
                pe.wait_ge(wsum_in, n + 1)
                mm(ps[:, 7, n:n + 1], ones[:], rv[:, n:n + 1], start=True, stop=True).then_inc(wsum_out, 1)
            pe.wait_ge(wq_ready, 1)
            pe.wait_ge(xq_ready, 1)
            for t in range(T):
                b = t % 2
                if t >= 2:
                    pe.wait_ge(q_ready, t - 1)
                for k in range(KD):
                    last = mm(ps[:, b, :], xT3[:, k, bass.ts(t, P)], wk3[:, k, :], start=(k == 0), stop=(k == KD - 1))
                last.then_inc(sup_done, 1)
            pe.wait_ge(q_ready, T)
            pe.wait_ge(at_lo, T)

            def aq(t, b):
                if later(t):
                    pe.wait_ge(aq_read, t - 1)
                for j in range(T):
                    for part in range(2):
                        last = mm(ps[:, 2 + b, :], r_at[:, part, j, bass.ts(t, P)], q[:, j, :],
                                  start=(j == 0 and part == 0), stop=(j == T - 1 and part == 1))
                last.then_inc(aq_done, 1)
            tiles(pe, aq)

            def split_product(out_bank, left, right, wait_right=None):
                for j in range(T):
                    if wait_right:
                        wait_right(j)
                    for part, (a, bb) in enumerate(((0, 0), (0, 1), (1, 0))):
                        last = mm(out_bank, left(a, j), right[:, bb, j, :], start=(j == 0 and part == 0),
                                  stop=(j == T - 1 and part == 2))
                return last

            pe.wait_ge(ld_qk, 16 * 2)
            pe.wait_ge(ld_b, 16 * 5)
            pe.wait_ge(bqk_ready, 1)
            for n in range(FOLDS):
                if n == 4:
                    pe.wait_ge(fold_ready, 2)
                out_n = ps[:, FOLD_BANK[n], :]
                for k in range(KD):
                    st = dict(start=(k == 0), stop=(k == KD - 1))
                    if n < KD:
                        last = mm(out_n, wq_n[:, k, bass.ts(n, P)], wk_n[:, k, :], **st)
                    elif n == KD:
                        last = mm(out_n[0:1, :], bcol[:, 9 + k:10 + k], wq_n[:, k, :], **st)
                    else:
                        last = mm(out_n[:, KD:KD + 1], ones[:], bqk[:, k:k + 1], **st)
                if n == KD + 1:
                    for m in range(KD):
                        for k in range(KD):
                            last = mm(out_n[:, m:m + 1], wk_n[:, k, bass.ts(m, P)], bcol[:, 5 + k:6 + k],
                                      start=(k == 0), stop=(k == KD - 1))
                last.then_inc(fold_ps, 1)

            pe.wait_ge(s_lo, T)

            def sx(t, b):
                first = isinstance(t, int) and t == 0
                if later(t):
                    pe.wait_ge(y_lo, t - 1)
                def wait_right(j):
                    pe.wait_ge(xs_lo, j + 1)
                split_product(ps[:, 4 + b, :], lambda a, j: r_s[:, j, a, bass.ts(t, P)], r_xs,
                              wait_right if first else None).then_inc(sx_done, 1)
            tiles(pe, sx)

            pe.wait_ge(x1_ready, T)

            tr = nc.tensor.transpose

            def ay(t, b):
                first = isinstance(t, int) and t == 0
                if later(t):
                    pe.wait_ge(ay_read, t - 1)

                def wait_right(j):
                    pe.wait_ge(y_lo, j + 1)
                split_product(ps[:, 2 + b, :], lambda a, j: r_at[:, a, j, bass.ts(t, P)], r_y,
                              wait_right if first else None).then_inc(ay_done, 1)
                if first:
                    pe.wait_ge(w2_kept, 1)
                    pe.wait_ge(wa_ready, 1)
                if at_least(t, 1):
                    turn_x2(t - 1, 1 - b)
                if at_least(t, 2):
                    project(t - 2, b)
                if at_least(t, 3):
                    turn_ed(t - 3, 1 - b)

            def turn_x2(t, b):
                pe.wait_ge(x2_ready, t + 1)
                if later(t):
                    pe.wait_ge(x2T_ready, t - 1)
                for k in range(KD):
                    last = tr(ps[:, b, bass.ts(k, P)], x2[:, b, bass.ts(k, P)], ident[:])
                last.then_inc(x2T_ps, 1)

            def project(t, b):
                pe.wait_ge(x2T_ready, t + 1)
                if later(t):
                    pe.wait_ge(wh_ready, t - 1)
                    pe.wait_ge(ed_ready, t - 1)
                for k in range(KD):
                    mm(ps[:, 4 + b, :], x2T[:, b, k, :], W2[:, k, :], start=(k == 0), stop=(k == KD - 1))
                for k in range(KD):
                    last = mm(ps[:, 6 + b, 0:2 * H], x2T[:, b, k, :], wa[:, k, :], start=(k == 0), stop=(k == KD - 1))
                last.then_inc(wh_ps, 1)

            def turn_ed(t, b):
                pe.wait_ge(e_ready, 2 * t + 2)
                tr(ps[0:H, 6 + b, P:2 * P], ed[:, b, :], ident[:]).then_inc(ed_ps, 1)

            tiles(pe, ay, 2)
            turn_x2(T - 1, 0)
            project(T - 2, 1)
            turn_ed(T - 3, 0)
            project(T - 1, 0)
            turn_ed(T - 2, 1)
            turn_ed(T - 1, 0)
            pe.wait_ge(wh_ready, T)
            pe.wait_ge(ed_ready, T)

            def weigh(n, s, h, hh, t):
                pe.wait_ge(pt_ready, n + 1)
                if t == 0 and later(h + 1):
                    pe.wait_ge(enc_a, h)
                if t == TA and later(h + 1):
                    pe.wait_ge(enc_b, h)
                bank, c0 = (6, t * HW) if t < TA else (7, (t - TA) * HW)
                for j in range(T):
                    last = mm(ps[:, bank, c0:c0 + HW], PT[:, s % 2, bass.ts(j, P)],
                              Wh[:, j, bass.ts(h, 1), :].rearrange("p h d -> p (h d)"), start=(j == 0), stop=(j == T - 1))
                last.then_inc(o_done, 1)

            def heads(hp):
                first = isinstance(hp, int)
                for s in range(2 * T):
                    hh, t = divmod(s, T)
                    n = hp * 2 * T + s
                    pe.wait_ge(p_ready, n + 1)
                    if not (first and s < 2):
                        pe.wait_ge(pt_ready, n - 1)
                    for j in range(T):
                        last = tr(ps[:, 3 * (s % 2) + j // KD, bass.ts(j % KD, P)], PR[s % 2][:, bass.ts(j, P)], ident[:])
                    last.then_inc(pt_ps, 1)
                    if not (first and s == 0):
                        hb, tb = divmod((s - 1) % (2 * T), T)
                        h = 2 * hp + hb if s else 2 * hp - 1
                        weigh(n - 1, (s - 1) % 2, h, hb, tb)

            heads(0)
            with pe.Fori(1, H // 2) as hp:
                heads(hp)
            weigh(H * T - 1, 1, H - 1, 1, T - 1)

            pe.wait_ge(ld_mlp, 16 * 5)

            def turn_enc(t):
                pe.wait_ge(elu_done, t + 1)
                if t >= 2:
                    pe.wait_ge(encT_ready, t - 1)
                for k in range(KD):
                    last = tr(ps[:, t % 2, bass.ts(k, P)], enc[:, t, bass.ts(k, P)], ident[:])
                last.then_inc(encT_ps, 1)

            def mlp1(n):
                i, w = CH[n]
                pe.wait_ge(encT_ready, (i + w) // P)
                for m in range(2):
                    if n:
                        pe.wait_ge(m1_ready, 2 * (n - 1) + m + 1)
                    for k in range(KD):
                        last = mm(ps[:, 2 + m, 0:w], w1[:, k, bass.ts(m, P)], encT[:, k, i:i + w], start=(k == 0), stop=(k == KD - 1))
                    last.then_inc(m1_ps, 1)

            def mlp2(n):
                i, w = CH[n]
                pe.wait_ge(m1_ready, 2 * n + 2)
                if n:
                    pe.wait_ge(m3_ready, 2 * n)
                for k in range(2):
                    last = mm(ps[:, 4, 0:w], w2[:, k, :], o1T[:, k, i:i + w], start=(k == 0), stop=(k == 1))
                last.then_inc(m2_ps, 1)

            def mlp3(n):
                i, w = CH[n]
                pe.wait_ge(m2_ready, n + 1)
                for m in range(2):
                    mm(ps[:, 5 - m, 0:w], w3[:, bass.ts(m, P)], o2T[:, i:i + w], start=True, stop=True).then_inc(m3_ps, 1)

            def mlp4(t):
                pe.wait_ge(m3_ready, 2 * (t // KD + 1))
                if t >= 2:
                    pe.wait_ge(m4_read, t - 1)
                for k in range(2):
                    last = mm(ps[:, 6 + t % 2, :], o3T[:, k, bass.ts(t, P)], w4[:, k, :], start=(k == 0), stop=(k == 1))
                last.then_inc(m4_ps, 1)

            def turn_x3(t):
                pe.wait_ge(x3_ready, t + 1)
                if t >= 2:
                    pe.wait_ge(x3T_ready, t - 1)
                for k in range(KD):
                    last = tr(ps[:, t % 2, bass.ts(k, P)], r_x[:, t, bass.ts(k, P)], ident[:])
                last.then_inc(x3T_ps, 1)

            def parts(out, left, right, ks):
                for k in ks:
                    for n, (a, bb) in enumerate(((0, 0), (0, 1), (1, 0))):
                        last = mm(out, left(a, k), right(bb, k), start=(k == ks[0] and n == 0), stop=(k == ks[-1] and n == 2))
                return last

            def value(t):
                pe.wait_ge(x3T_ready, t + 1)
                if t == 0:
                    pe.wait_ge(wv_ready, 1)
                if t >= 2:
                    pe.wait_ge(v_read, t - 1)
                parts(ps[:, 2 + t % 2, :], lambda a, k: x3T[:, a, k, bass.ts(t, P)], lambda a, k: wv_parts[:, a, k, :],
                      range(KD)).then_inc(v_ps, 1)

            for t in range(4):
                turn_enc(t)
            mlp1(0)
            for t in range(4, 8):
                turn_enc(t)
            mlp2(0)
            mlp1(1)
            mlp3(0)
            mlp4(0)
            mlp4(1)
            for t in range(8, T):
                turn_enc(t)
            mlp2(1)
            mlp1(2)
            mlp3(1)
            mlp2(2)
            mlp3(2)
            pe.wait_ge(encT_ready, T)
            for t in range(2, T + 3):
                if t < T:
                    mlp4(t)
                if t - 2 < T:
                    turn_x3(t - 2)
                if t >= 3:
                    value(t - 3)
            pe.wait_ge(v_read, T)
            pe.wait_ge(x3T_ready, T)

            def make_g(t):
                if t == 0:
                    pe.wait_ge(m_ready, 1)
                    pe.wait_ge(m4_read, T)
                if t >= 1:
                    pe.wait_ge(g_read, t)
                for m in range(KD):
                    last = parts(ps[:, 6, bass.ts(m, P)], lambda a, k: m_parts[:, a, k, bass.ts(m, P)],
                                 lambda a, k: x3T[:, a, k, bass.ts(t, P)], range(KD))
                last.then_inc(g_ps, 1)

            def score(t):
                pe.wait_ge(g_lo, t + 1)
                if t >= 1:
                    pe.wait_ge(sc_read, t)
                for n, (i, w) in enumerate(CHN):
                    last = parts(ps[:, n, 0:w], lambda a, k: g_parts[:, t % 2, a, k, :], lambda a, k: x3T[:, a, k, i:i + w],
                                 range(KD))
                last.then_inc(sc_ps, 1)

            def turn_p(t):
                pe.wait_ge(p3_ready, t + 1)
                if t >= 1:
                    pe.wait_ge(pt3_lo, t)
                for j in range(T):
                    last = tr(ps[:, 3 + j // KD, bass.ts(j % KD, P)], S3[:, t % 2, bass.ts(j, P)], ident[:])
                last.then_inc(pt3_ps, 1)

            def weigh_v(t):
                if t == 0:
                    pe.wait_ge(v_lo, T)
                pe.wait_ge(pt3_lo, t + 1)
                if t >= 1:
                    pe.wait_ge(o3_read, t)
                parts(ps[:, 7, :], lambda a, j: PT3[:, t % 2, a, bass.ts(j, P)], lambda a, j: vv[:, a, j, :],
                      range(T)).then_inc(o3_ps, 1)

            make_g(0)
            make_g(1)
            score(0)
            for t in range(T):
                turn_p(t)
                if t + 1 < T:
                    score(t + 1)
                if t + 2 < T:
                    make_g(t + 2)
                weigh_v(t)


_OUT = (N, D)


def kernel(**inputs):
    import numpy as _np
    import concourse.bacc as _bacc
    from concourse import mybir as _mybir
    from concourse.bass_utils import run_bass_kernel_spmd as _run

    f = {k: _np.asarray(a) for k, a in inputs.items()}
    pad = NP - N
    lay = {
        "adjT": _np.pad(f["adj"].T, ((0, pad), (0, pad))),
        "adj": _np.pad(f["adj"], ((0, pad), (0, pad))),
        "xT": _np.pad(f["x"].T, ((0, 0), (0, pad))),
        "x": _np.pad(f["x"], ((0, pad), (0, 0))),
        "scal": _np.broadcast_to(_np.stack([f["L0_gnn_adj_scaling_factor"], f["L0_gnn_wgt_alpha"], f["L0_gnn_act_alpha"],
                                            f["L0_gnn_act_alpha2"]]), (P, 4)),
        "w0": f["L0_gnn_weight"],
        "gat_w": f["L2_gnn_W"].transpose(1, 0, 2).reshape(D, D),
        "gat_a": _np.stack([f["L2_gnn_a1"], f["L2_gnn_a2"]]).reshape(1, 2 * D),
        "w1T": f["L2_gnn_W1"].T, "w2T": f["L2_gnn_W2"].T, "w3T": f["L2_gnn_W3"].T, "w4T": f["L2_gnn_W4"].T,
        "b1": f["L2_gnn_b1"].reshape(-1, P).T, "b2": f["L2_gnn_b2"].reshape(-1, P).T, "b3": f["L2_gnn_b3"].reshape(-1, P).T,
        "b4": f["L2_gnn_b4"].reshape(1, D),
        "wq": f["L3_gnn_W_q"], "wk": f["L3_gnn_W_k"], "wvT": f["L3_gnn_W_v"].T,
        "bq": f["L3_gnn_b_q"].reshape(-1, P).T, "bk": f["L3_gnn_b_k"].reshape(-1, P).T, "bv": f["L3_gnn_b_v"].reshape(1, D),
    }
    nc = _bacc.Bacc("TRN2", target_bir_lowering=False, num_devices=1)
    arrays, args = {}, []
    for name, a in lay.items():
        a = _np.ascontiguousarray(a)
        arrays[f"in_{name}_dram"] = a
        args.append(nc.dram_tensor(f"in_{name}_dram", a.shape, _mybir.dt.from_np(a.dtype), kind="ExternalInput").ap())
    args.append(nc.dram_tensor("out_0_dram", _OUT, F32, kind="ExternalOutput").ap())
    build(nc, *args)
    r = _run(nc, [arrays], core_ids=[0])
    return r.results[0]["out_0_dram"]
```

```python
from contextlib import ExitStack

import concourse.bass as bass
from concourse import mybir

F32 = mybir.dt.float32
F16 = mybir.dt.float16
BF16 = mybir.dt.bfloat16
I32 = mybir.dt.int32
ALU = mybir.AluOpType
ACT = mybir.ActivationFunctionType
AX_X = mybir.AxisListType.X
RMAX = bass.bass_isa.ReduceOp.max

P = 128
N = 1354
T = (N + P - 1) // P
NP = T * P
LAST = N - (T - 1) * P
D = 512
KD = D // P
PAIRS = (T - 1) // 2
assert T == 2 * PAIRS + 1

LN_EPS = 1e-5
ROUND = 1.5 * 2.0 ** 23
RSQRT_SEED = 0x5F3759DF
RSQRT_GAIN = 2.0 * (8.0 / 3.0) ** 3
W_LEVELS = 7.0
X_LEVELS = 15.0
X_SCALE = 2.0 ** 11
Y_SCALE = 2.0 ** 6
TA = 6
H = 8
HD = D // H
HW = HD + 1
LEAK = 0.2
NEG = -9e15
NEG3 = -10000.0
M1, M2, M3 = 256, 128, 256
BIG = 3e38
P_SCALE = 2.0 ** 14
A_TOP = 2.0 ** 14


class Chain:

    def __init__(self, eng, sem, base=0):
        self.eng, self.sem, self.base, self.n = eng, sem, base, 0

    def __call__(self, ins):
        self.n += 1
        ins.then_inc(self.sem, 1)
        self.eng.wait_ge(self.sem, self.base + self.n)


def build(nc, adjT, adj, xT, x, scal, w0, gat_w, gat_a, w1T, w2T, w3T, w4T, b1, b2, b3, b4, wq, wk, wvT, bq, bk, bv, out):
    ctx = ExitStack()
    with ctx:
        def sb(name, shape, dt=F32):
            return ctx.enter_context(nc.sbuf_tensor(name, shape, dt))

        def sem(name):
            return ctx.enter_context(nc.semaphore(name))

        r_at = sb("r_at", [P, 2, T, NP], F16)
        r_s = sb("r_s", [P, T, 2, NP], F16)
        r_x = sb("r_x", [P, T, D])
        r_xs = sb("r_xs", [P, 2, T, D], F16)
        r_y = sb("r_y", [P, 2, T, D], F16)
        r_st = sb("r_st", [P, 2, NP])
        pre = sb("pre", [P, 2, D])
        ident = sb("ident", [P, P])
        ident2 = sb("ident2", [P, P])
        ones = sb("ones", [P, P])
        scs = sb("scs", [P, 4])
        cs = sb("cs", [P, 16])
        dcol = sb("dcol", [P, T])
        ycol = sb("ycol", [P, T])
        bns = sb("bns", [P, 6])
        mv = sb("mv", [P, 2])
        rv = sb("rv", [P, 8])
        amax = sb("amax", [P, 6])
        asum = sb("asum", [P, T])
        dtmp = sb("dtmp", [P, 4, T])
        junk = sb("junk", [P, 1])
        wa = sb("wa", [P, KD, 2 * H])
        wa_parts = sb("wa_parts", [P, 2, KD, 2 * H], F16)
        r_sig2 = sb("r_sig2", [P, 2])
        sig2 = sb("sig2", [P, 2])
        back2 = sb("back2", [P, 2])
        es = sb("es", [P, H, T])
        es_pair = sb("es_pair", [P, 2 * T])
        ed = sb("ed", [P, 2, H])
        nmax = sb("nmax", [P, 2])
        rsum = sb("rsum", [P, 8])
        brow = sb("brow", [P, D])
        bcol = sb("bcol", [P, 16])
        rs3 = sb("rs3", [P, 4])
        fold = sb("fold", [P, KD + 1])
        r_col = sb("r_col", [P, T])
        bqk = sb("bqk", [P, KD])
        bound = sb("bound", [P, 4])
        r_sig3 = sb("r_sig3", [P, 4])
        sig3 = sb("sig3", [P, 4])
        k3 = sb("k3", [P, 8])
        ps = ctx.enter_context(nc.psum_tensor("ps", [P, 8, D], F32))

        at_raw = r_s[:].rearrange("p t c i -> p t (c i)").bitcast(F32)
        q = r_xs[:, 0]
        wlev = r_xs[:, 1].rearrange("p t d -> p (t d)").bitcast(F32)[:, 0:KD * D]
        wk3 = wlev.rearrange("p (k d) -> p k d", k=KD)
        xTf = r_y[:].rearrange("p c t d -> p (c t d)").bitcast(F32)[:, 0:KD * NP]
        xT3 = xTf.rearrange("p (k i) -> p k i", k=KD)
        nat_x = r_xs[:, 1].rearrange("p t d -> p (t d)").bitcast(F32).rearrange("p (b i) -> p b i", b=2)
        nat_buf = [r_st[:, 0, :], r_st[:, 1, :], nat_x[:, 0, :], nat_x[:, 1, :]]
        wq_n, wk_n = (xTf[:, m * KD * D:(m + 1) * KD * D].rearrange("p (k d) -> p k d", k=KD) for m in range(2))
        fold_row = xTf[:, 2 * KD * D:2 * KD * D + 2 * D].rearrange("p (b d) -> p b d", b=2)
        wtmp = r_at[:].rearrange("p c t i -> p (c t i)").bitcast(F32)[:, 0:KD * D]

        at32 = r_at[:].rearrange("p c t i -> p (c t i)").bitcast(F32)
        o = 0
        drow = at32[:, o:o + 4 * N].rearrange("p (b c i) -> p b c i", b=2, c=2)
        o += 4 * N
        G = at32[:, o:o + 2 * N].rearrange("p (b i) -> p b i", b=2)
        o += 2 * N
        PR0 = at32[:, o:o + NP]
        xs32 = r_xs[:].rearrange("p c t d -> p (c t d)").bitcast(F32)
        W2 = xs32[:, 0:KD * D].bitcast(F16).rearrange("p (c k d) -> p c k d", c=2, k=KD)
        o = KD * D
        w1 = xs32[:, o:o + KD * M1].rearrange("p (k d) -> p k d", k=KD)
        o += KD * M1
        w2 = xs32[:, o:o + 2 * M2].rearrange("p (k d) -> p k d", k=2)
        o += 2 * M2
        w3 = xs32[:, o:o + M3]
        o += M3
        w4 = xs32[:, o:o + 2 * D].rearrange("p (k d) -> p k d", k=2)
        x2 = w4
        o += 2 * D
        x2T = xs32[:, o:o + 2 * D].bitcast(F16).rearrange("p (b c k i) -> p b c k i", b=2, c=2, k=KD)
        M32 = xs32[:, 0:KD * D].rearrange("p (k d) -> p k d", k=KD)
        w_row = xs32[:, o:o + D]
        st32 = r_st[:].rearrange("p b i -> p (b i)")
        W2_st = st32[:, 0:KD * D].rearrange("p (k d) -> p k d", k=KD)
        prod = st32[:, KD * D:KD * D + D]
        a_bc = pre[:]
        s32 = r_s[:].rearrange("p t c i -> p (t c i)").bitcast(F32)
        mask = s32[:, 0:T * N // 2].bitcast(BF16).rearrange("p (t i) -> p t i", t=T)
        o = T * N // 2
        Wh = s32[:, o:o + T * H * HW].rearrange("p (t h d) -> p t h d", t=T, h=H)
        o += T * H * HW
        edrow = s32[0:H, o:o + NP]
        PR1 = s32[:, o:o + NP]
        PR = [PR0, PR1]
        o += NP
        enc = r_y[:].rearrange("p c t d -> p (c t d)").bitcast(F32).rearrange("p (t d) -> p t d", t=T)
        PT = r_st
        encT = at32[:, 0:KD * NP].rearrange("p (k i) -> p k i", k=KD)
        o1T = at32[:, KD * NP:(KD + 2) * NP].rearrange("p (k i) -> p k i", k=2)
        o2T = at32[:, (KD + 2) * NP:(KD + 3) * NP]
        o3T = at32[:, (KD + 3) * NP:(KD + 5) * NP].rearrange("p (k i) -> p k i", k=2)
        x3T = r_y[:].rearrange("p c t d -> p (c t d)").rearrange("p (c k i) -> p c k i", c=2, k=KD)
        at16 = r_at[:].rearrange("p c t i -> p (c t i)")
        vv = at16[:, 0:2 * T * D].rearrange("p (c t d) -> p c t d", c=2, t=T)
        PT3 = at16[:, 2 * T * D:2 * T * D + 4 * NP].rearrange("p (b c i) -> p b c i", b=2, c=2)
        wv = at32[:, 9 * NP:9 * NP + KD * D].rearrange("p (k d) -> p k d", k=KD)
        v_row = at32[:, 9 * NP + KD * D:9 * NP + KD * D + D]
        m_parts, wv_parts = (s32[:, m * KD * D:(m + 1) * KD * D].bitcast(F16).rearrange(
            "p (c k d) -> p c k d", c=2, k=KD) for m in range(2))
        assert 2 * KD * D <= T * N // 2
        o = 2 * KD * D
        S3 = s32[:, o:o + 2 * NP].rearrange("p (b i) -> p b i", b=2)
        o += 2 * NP
        Z3 = s32[:, o:o + NP]
        o += NP
        g32 = s32[:, o:o + 2 * D].rearrange("p (b k i) -> p b k i", b=2, k=KD)
        o += 2 * D
        g_parts = s32[:, o:o + 2 * D].bitcast(F16).rearrange("p (b c k i) -> p b c k i", b=2, c=2, k=KD)

        NMEAN, RSTD, C_Q, SIG, SIGH, RSIG, F0, F1, RALPHA, RWA, TMP, CY = range(12)

        A_G, A_V, KAPPA, NEG_K, R_V, S_R = range(6)

        def c(k):
            return cs[:, k:k + 1]

        def kc(k):
            return k3[:, k:k + 1]

        ld_w, ld_sc = sem("ld_w"), sem("ld_sc")
        ld_xT = [sem(f"ld_xT{k}") for k in range(KD)]
        ld_x = sem("ld_x")
        GROUPS = [(0, 3), (3, 6), (6, 9), (9, T)]
        ld_at = [sem(f"ld_at{g}") for g in range(len(GROUPS))]
        ld_nat = [sem(f"ld_nat{b}") for b in range(4)]
        const_ready = sem("const_ready")
        wsum_in, wsum_out = sem("wsum_in"), sem("wsum_out")
        asum_ready, amax_in, amax_out = sem("asum_ready"), sem("amax_in"), sem("amax_out")
        deg_ready = sem("deg_ready")
        sig_ready = sem("sig_ready")
        mean_ready, x_rounded, wq_ready, xq_ready = (sem(n) for n in ("mean_ready", "x_rounded", "wq_ready", "xq_ready"))
        sup_done, q_ready = sem("sup_done"), sem("q_ready")
        at_hi, at_lo = sem("at_hi"), sem("at_lo")
        sym_ready, s_hi, s_lo = sem("sym_ready"), sem("s_hi"), sem("s_lo")
        aq_done, aq_read, x1_ready = sem("aq_done"), sem("aq_read"), sem("x1_ready")
        xs_hi, xs_lo = sem("xs_hi"), sem("xs_lo")
        sx_done, y_hi, y_lo = sem("sx_done"), sem("y_hi"), sem("y_lo")
        ay_done, ay_read, x2_ready = sem("ay_done"), sem("ay_read"), sem("x2_ready")
        pool_add = sem("pool_add")
        dve_d = sem("dve_d")
        dve_a, dve_ln0, dve_ln1 = sem("dve_a"), sem("dve_ln0"), sem("dve_ln1")
        stored = sem("stored")
        scratch = nc.dram_tensor("e_dst_rows", [H, NP], F32, kind="Internal").ap()
        folded = nc.dram_tensor("folded_weights", [D + 1, D], F32, kind="Internal").ap()
        ld_w2, ld_a, ld_mlp, ld_qkv, ld_b = sem("ld_w2"), sem("ld_a"), sem("ld_mlp"), sem("ld_qkv"), sem("ld_b")
        ld_bv = sem("ld_bv")
        ld_m = [sem(f"ld_m{b}") for b in range(2)]
        x2_kept, w2_hi, w2_ready, x2T_hi = sem("x2_kept"), sem("w2_hi"), sem("w2_ready"), sem("x2T_hi")
        scale2_in, scale2_out, scale2_ready = sem("scale2_in"), sem("scale2_out"), sem("scale2_ready")
        wa_ready, mask_ready = sem("wa_ready"), sem("mask_ready")
        x2T_ps, x2T_ready, wh_ps, wh_ready, e_ps, e_ready, ed_ps, ed_ready = (
            sem(n) for n in ("x2T_ps", "x2T_ready", "wh_ps", "wh_ready", "e_ps", "e_ready", "ed_ps", "ed_ready"))
        ed_stored = sem("ed_stored")
        ld_d = [sem(f"ld_d{b}") for b in range(2)]
        pad_ready, g_ready, p_ready, pt_ps, pt_ready = (
            sem(n) for n in ("pad_ready", "g_ready", "p_ready", "pt_ps", "pt_ready"))
        o_done, enc_a, enc_b, d_used = sem("o_done"), sem("enc_a"), sem("enc_b"), sem("d_used")
        dve_w, dve_p, dve_g, dve_m, dve_3 = sem("dve_w"), sem("dve_p"), sem("dve_g"), sem("dve_m"), sem("dve_3")
        elu_e, elu_done, encT_ps, encT_ready = sem("elu_e"), sem("elu_done"), sem("encT_ps"), sem("encT_ready")
        m1_ps, m1_ready, m2_ps, m2_ready, m3_ps, m3_ready, m4_ps, m4_read = (
            sem(n) for n in ("m1_ps", "m1_ready", "m2_ps", "m2_ready", "m3_ps", "m3_ready", "m4_ps", "m4_read"))
        x3_ready, x3T_ps, x3T_hi, x3T_ready = sem("x3_ready"), sem("x3T_ps"), sem("x3T_hi"), sem("x3T_ready")
        fold_stored = [sem(f"fold_stored{b}") for b in range(2)]
        ld_qk, fold_ps, fold_ready = sem("ld_qk"), sem("fold_ps"), sem("fold_ready")
        ld_fold, bqk_ready = sem("ld_fold"), sem("bqk_ready")
        bound_in, bound_out, scale3_ready = sem("bound_in"), sem("bound_out"), sem("scale3_ready")
        wv_hi, m_hi, wv_ready, m_ready = sem("wv_hi"), sem("m_hi"), sem("wv_ready"), sem("m_ready")
        b4_added = sem("b4_added")
        v_hi, v_lo, g_ps, g_read, g_hi, g_lo = (
            sem(n) for n in ("v_hi", "v_lo", "g_ps", "g_read", "g_hi", "g_lo"))
        pt3_hi, s3_pad = sem("pt3_hi"), sem("s3_pad")
        v_ps = sem("v_ps")
        sc_ps, sc_read, s3_ready, p3_ready, pt3_ps, pt3_lo, o3_ps, o3_read, x4_ready = (
            sem(n) for n in ("sc_ps", "sc_read", "s3_ready", "p3_ready", "pt3_ps", "pt3_lo", "o3_ps", "o3_read", "x4_ready"))
        ld_a3 = [sem(f"ld_a3{b}") for b in range(2)]
        CH = [(0, 512), (512, 512), (1024, NP - 1024)]
        CHN = [(0, 512), (512, 512), (1024, N - 1024)]

        V_BANK = (4, 5)
        FOLDS = KD + 2
        FOLD_BANK = (0, 1, 6, 7, 0, 1)

        block = ctx.enter_context(nc.Block())

        def later(t):
            return not (isinstance(t, int) and t < 2)

        def at_least(t, n):
            return not (isinstance(t, int) and t < n)

        def nth(t, b):
            return t // 2 + 1 if isinstance(t, int) else pair_of[0] + 1

        pair_of = [None]

        def tiles(eng, body, peel=1):
            for t in range(2 * peel):
                body(t, t % 2)
            with eng.Fori(peel, PAIRS) as k:
                pair_of[0] = k
                body(2 * k, 0)
                body(2 * k + 1, 1)
            body(T - 1, 0)

        def before_end(t, n):
            return not isinstance(t, int) or t + n < T

        def last_tiles(body):
            def run(eng):
                for t in range(2):
                    body(t, t % 2, t // 2 + 1)
                with eng.Fori(1, (T - 3) // 2) as k:
                    body(2 * k, 0, k + 1)
                    body(2 * k + 1, 1, k + 1)
                for t in range(T - 3, T):
                    body(t, t % 2, t // 2 + 1)
            return run

        def tiles4(eng, body):
            first = T % 4
            for t in range(first):
                body(t, t % 2, t, 1)
            with eng.Fori(0, T // 4) as k:
                for i in range(first, first + 4):
                    body(4 * k + i, i % 2, i % 4, k + i // 4 + 1)

        @block.sync
        def _(sp):
            sp.dma_start(wk3, w0.rearrange("(k p) d -> p k d", p=P)).then_inc(ld_w, 16)
            sp.dma_start(scs[:], scal).then_inc(ld_sc, 16)
            for k in range(KD):
                sp.dma_start(xT3[:, k, :], xT[k * P:(k + 1) * P, :]).then_inc(ld_xT[k], 16)
            for g, (a, b) in enumerate(GROUPS):
                sp.dma_start(at_raw[:, a:b, :], adjT.rearrange("(t p) i -> p t i", p=P)[:, a:b, :]).then_inc(ld_at[g], 16)
            sp.dma_start(r_x[:], x.rearrange("(t p) d -> p t d", p=P)).then_inc(ld_x, 16)

            def nat(t):
                if t >= 4:
                    sp.wait_ge(s_lo, t - 3)
                sp.dma_start(nat_buf[t % 4], adj[t * P:(t + 1) * P, :]).then_inc(ld_nat[t % 4], 16)

            nat(0)
            nat(1)
            for col, bias, n in ((0, b1, 2), (2, b2, 1), (3, b3, 2), (5, bq, KD), (9, bk, KD)):
                sp.dma_start(bcol[:, col:col + n], bias).then_inc(ld_b, 16)
            sp.wait_ge(sup_done, T)
            nat(2)
            nat(3)
            for dst, src in ((wq_n, wq), (wk_n, wk)):
                sp.dma_start(dst, src.rearrange("(k p) d -> p k d", p=P)).then_inc(ld_qk, 16)
            for t in range(4, T):
                nat(t)

            for n in range(KD + 1):
                sp.wait_ge(fold_ready, n + 1)
                if n < KD:
                    sp.dma_start(folded[n * P:(n + 1) * P, :], fold_row[:, n % 2, :]).then_inc(fold_stored[n % 2], 16)
                else:
                    sp.dma_start(folded[D:D + 1, :], fold_row[0:1, n % 2, :]).then_inc(fold_stored[n % 2], 16)

            sp.wait_ge(s_lo, T)
            sp.dma_start(W2_st, gat_w.rearrange("(k p) d -> p k d", p=P)).then_inc(ld_w2, 16)
            sp.wait_ge(x1_ready, T)
            sp.dma_start(a_bc.rearrange("p a d -> p (a d)"), gat_a[0].partition_broadcast(P)).then_inc(ld_a, 16)
            sp.wait_ge(sx_done, T)
            sp.dma_start(w1, w1T.rearrange("(k p) d -> p k d", p=P)).then_inc(ld_mlp, 16)
            sp.dma_start(w2, w2T.rearrange("(k p) d -> p k d", p=P)).then_inc(ld_mlp, 16)
            sp.dma_start(w3, w3T).then_inc(ld_mlp, 16)
            sp.dma_start(brow[:], b4[0].partition_broadcast(P)).then_inc(ld_mlp, 16)
            sp.wait_ge(wa_ready, 1)
            sp.wait_ge(w2_ready, 1)

            def load_mask(t, b):
                if later(t):
                    sp.wait_ge(mask_ready, t - 1)
                sp.dma_start(r_st[:, b, 0:N], adj[bass.ts(t, P), 0:N]).then_inc(ld_m[b], 16)
            tiles(sp, load_mask)
            sp.wait_ge(x2T_ps, T)
            sp.wait_ge(x2_kept, T)
            sp.dma_start(w4, w4T.rearrange("(k p) d -> p k d", p=P)).then_inc(ld_mlp, 16)
            sp.wait_ge(ed_ready, T)
            sp.dma_start(scratch, edrow).then_inc(ed_stored, 16)
            sp.wait_ge(ed_stored, 16)

            def load_d(h, b):
                sp.dma_start(drow[:, b, 0, :], scratch[bass.ts(h, 1), 0:N][0].partition_broadcast(P)).then_inc(ld_d[b], 16)

            sp.wait_ge(ay_done, T)
            load_d(0, 0)
            load_d(1, 1)
            sp.wait_ge(fold_stored[0], 16 * 3)
            sp.wait_ge(fold_stored[1], 16 * 2)
            sp.wait_ge(wh_ps, T)
            sp.dma_start(M32, folded[0:D, :].rearrange("(k p) d -> p k d", p=P)).then_inc(ld_fold, 16)
            sp.dma_start(w_row, folded[D:D + 1, :][0].partition_broadcast(P)).then_inc(ld_fold, 16)
            sp.dma_start(wv, wvT.rearrange("(k p) d -> p k d", p=P)).then_inc(ld_qkv, 16)
            sp.dma_start(v_row, bv[0].partition_broadcast(P)).then_inc(ld_bv, 16)
            with sp.Fori(1, H // 2) as hp:
                sp.wait_ge(d_used, 2 * hp - 1)
                load_d(2 * hp, 0)
                sp.wait_ge(d_used, 2 * hp)
                load_d(2 * hp + 1, 1)

            sp.wait_ge(o_done, H * T)

            def serve(t, b):
                if later(t):
                    sp.wait_ge(sc_read, t - 1)
                sp.dma_start(r_st[:, b, 0:N], adj[bass.ts(t, P), 0:N]).then_inc(ld_a3[b], 16)
                if later(t):
                    sp.wait_ge(x4_ready, t - 1)
                    sp.dma_start(out[bass.ts(t - 2, P), :], r_x[:, t - 2, :]).then_inc(stored, 16)
            tiles(sp, serve)
            sp.wait_ge(x4_ready, T - 1)
            sp.dma_start(out[bass.ts(T - 2, P), :], r_x[:, T - 2, :]).then_inc(stored, 16)
            sp.wait_ge(x4_ready, T)
            sp.dma_start(out[(T - 1) * P:N, :], r_x[0:LAST, T - 1, :]).then_inc(stored, 16)
            sp.wait_ge(stored, 16 * T)

        @block.gpsimd
        def _(pool):
            nc.gpsimd.memset(ident[:], 0.0).then_inc(const_ready, 1)
            nc.gpsimd.memset(ident2[:], 0.0).then_inc(const_ready, 1)
            nc.gpsimd.memset(ones[:], 1.0).then_inc(const_ready, 1)
            pool.wait_ge(const_ready, 3)
            for m, v in ((ident, 1.0), (ident2, 2.0)):
                nc.gpsimd.affine_select(out=m[:], in_=m[:], compare_op=ALU.not_equal, fill=v, base=0,
                                        pattern=[[-1, P]], channel_multiplier=1).then_inc(const_ready, 1)
            pool.wait_ge(amax_in, 1)
            nc.gpsimd.partition_all_reduce(amax[:, 5:6], amax[:, 4:5], P, RMAX).then_inc(amax_out, 1)
            pool.wait_ge(const_ready, 5)
            pool.wait_ge(ld_b, 16 * 5)
            nc.gpsimd.tensor_tensor(bqk[:], bcol[:, 5:5 + KD], bcol[:, 9:9 + KD], ALU.mult).then_inc(bqk_ready, 1)

            def sym_at(t, b, buf, n):
                pool.wait_ge(ld_nat[buf], 16 * n)
                nc.gpsimd.tensor_tensor(nat_buf[buf], nat_buf[buf], at_raw[:, t, :], ALU.add).then_inc(pool_add, 1)
                pool.wait_ge(pool_add, t + 1)
                d = nat_buf[buf][:, bass.ts(t, P)]
                nc.gpsimd.tensor_tensor(d, d, ident2[:], ALU.add).then_inc(sym_ready, 1)

            tiles4(pool, sym_at)

            pool.wait_ge(scale2_in, 1)
            nc.gpsimd.partition_all_reduce(amax[:, 2:4], amax[:, 0:2], P, RMAX).then_inc(scale2_out, 1)

            pool.wait_ge(ld_mlp, 16 * 5)
            pool.wait_ge(x2_kept, T)
            for t in range(T):
                nc.gpsimd.tensor_tensor(r_x[:, t, :], r_x[:, t, :], brow[:], ALU.add).then_inc(b4_added, 1)

            pool.wait_ge(bound_in, 1)
            nc.gpsimd.partition_all_reduce(bound[:, 0:3], amax[:, 0:3], P, RMAX).then_inc(bound_out, 1)

            def g_low(t, b):
                pool.wait_ge(g_hi, t + 1)
                nc.gpsimd.tensor_tensor(g_parts[:, b, 1], g32[:, b], g_parts[:, b, 0], ALU.subtract).then_inc(g_lo, 1)
            tiles(pool, g_low)

        @block.scalar
        def _(act):
            act.wait_ge(ld_w, 16)
            nc.scalar.activation(wtmp, wlev, ACT.Copy, accum_out=rv[:, 0:1]).then_inc(wsum_in, 1)
            act.wait_ge(mean_ready, 1)
            nc.scalar.activation(wtmp, wlev, ACT.Square, bias=c(NMEAN), accum_out=rv[:, 1:2]).then_inc(wsum_in, 1)
            for k in range(KD):
                act.wait_ge(x_rounded, k + 1)
                nc.scalar.activation(xT3[:, k, :], xT3[:, k, :], ACT.Copy, bias=-ROUND).then_inc(xq_ready, 1)

            for g, (a, b) in enumerate(GROUPS):
                act.wait_ge(ld_at[g], 16)
                for t in range(a, b):
                    nc.scalar.activation(r_at[:, 1, t, :], at_raw[:, t, :], ACT.Abs,
                                         accum_out=asum[:, t:t + 1]).then_inc(asum_ready, 1)
            act.wait_ge(sig_ready, 1)
            for t in range(T):
                nc.scalar.activation(r_at[:, 0, t, :], at_raw[:, t, :], ACT.Copy, scale=c(SIG)).then_inc(at_hi, 1)

            def sym_hi(t, b, buf, n):
                act.wait_ge(sym_ready, t + 1)
                act.wait_ge(at_lo, t + 1)
                nc.scalar.activation(r_s[:, t, 0, :], nat_buf[buf], ACT.Copy, scale=c(SIGH),
                                     accum_out=dcol[:, bass.ts(t, 1)]).then_inc(s_hi, 1)
            tiles4(act, sym_hi)

            act.wait_ge(sup_done, T)
            for n in range(FOLDS):
                src = ps[:, FOLD_BANK[n], :]
                act.wait_ge(fold_ps, n + 1)
                if 2 <= n < KD + 1:
                    act.wait_ge(fold_stored[n % 2], 16 * (n // 2))
                if n < KD:
                    nc.scalar.activation(fold_row[:, n % 2, :], src, ACT.Copy).then_inc(fold_ready, 1)
                elif n == KD:
                    nc.scalar.activation(fold_row[0:1, n % 2, :], src[0:1, :], ACT.Copy).then_inc(fold_ready, 1)
                else:
                    nc.scalar.activation(fold[:], src[:, 0:KD + 1], ACT.Copy).then_inc(fold_ready, 1)

            act.wait_ge(aq_done, T)
            act.wait_ge(deg_ready, 1)

            def x1_hi(t, b):
                act.wait_ge(x1_ready, t + 1)
                nc.scalar.activation(r_xs[:, 0, t, :], r_x[:, t, :], ACT.Copy,
                                     scale=dcol[:, bass.ts(t, 1)]).then_inc(xs_hi, 1)
            tiles(act, x1_hi)

            act.wait_ge(fold_stored[0], 16 * 3)
            act.wait_ge(fold_stored[1], 16 * 2)

            def y_high(t, b):
                act.wait_ge(sx_done, t + 1)
                nc.scalar.activation(r_y[:, 0, t, :], ps[:, 4 + b, :], ACT.Copy,
                                     scale=ycol[:, bass.ts(t, 1)]).then_inc(y_hi, 1)
            tiles(act, y_high)

            act.wait_ge(sx_done, T)
            act.wait_ge(scale2_ready, 1)
            nc.scalar.activation(W2[:, 0], W2_st, ACT.Copy, scale=sig2[:, 0:1]).then_inc(w2_hi, 1)
            nc.scalar.activation(wa_parts[:, 0], wa[:], ACT.Copy, scale=sig2[:, 1:2]).then_inc(w2_hi, 1)

            def x2T_out(t, b):
                act.wait_ge(x2T_ps, t + 1)
                if later(t):
                    act.wait_ge(wh_ps, t - 1)
                nc.scalar.activation(x2T[:, b, 0], ps[:, b, :].rearrange("p (k i) -> p k i", k=KD), ACT.Copy,
                                     scale=X_SCALE).then_inc(x2T_hi, 1)

            def wh_out(t, b):
                act.wait_ge(wh_ps, t + 1)
                nc.scalar.activation(Wh[:, t, :, 0:HD], ps[:, 4 + b, :].rearrange("p (h d) -> p h d", h=H),
                                     ACT.Copy, scale=back2[:, 0:1]).then_inc(wh_ready, 1)

            def project_out(t, b):
                if at_least(t, 1):
                    x2T_out(t - 1, 1 - b)
                if at_least(t, 2):
                    wh_out(t - 2, b)
                if before_end(t, 1):
                    keep_x2(t, b)

            def keep_x2(t, b):
                act.wait_ge(x2_ready, t + 1)
                nc.scalar.activation(r_x[:, t, :], x2[:, b, :], ACT.Copy).then_inc(x2_kept, 1)

            tiles(act, project_out, 2)
            x2T_out(T - 1, 0)
            keep_x2(T - 1, 0)
            wh_out(T - 2, 1)
            wh_out(T - 1, 0)

            def take_pt(n, s):
                act.wait_ge(pt_ps, n + 1)
                if later(n):
                    act.wait_ge(o_done, n - 1)
                b = 3 * (s % 2)
                nc.scalar.activation(PT[:, s % 2, :], ps[:, b:b + 3, :].rearrange("p b i -> p (b i)")[:, 0:NP],
                                     ACT.Copy).then_inc(pt_ready, 1)

            act.wait_ge(pad_ready, 2)

            def exps(hp):
                first = isinstance(hp, int)
                for s in range(2 * T):
                    n = hp * 2 * T + s
                    act.wait_ge(g_ready, n + 1)
                    if not (first and s < 2):
                        act.wait_ge(pt_ps, n - 1)
                    nc.scalar.activation(PR[s % 2][:, 0:N], G[:, s % 2, :], ACT.Exp, scale=-1.0,
                                         bias=nmax[:, s % 2:s % 2 + 1]).then_inc(p_ready, 1)
                    if not (first and s == 0):
                        take_pt(n - 1, (s - 1) % 2)
            exps(0)
            with act.Fori(1, H // 2) as hp:
                exps(hp)

            act.wait_ge(enc_a, H)

            def elu_exp(t):
                if t >= 2:
                    act.wait_ge(elu_done, t - 1)
                nc.scalar.activation(pre[:, t % 2, :], enc[:, t, :], ACT.Exp).then_inc(elu_e, 1)

            def take_encT(t):
                act.wait_ge(encT_ps, t + 1)
                nc.scalar.activation(encT[:, :, bass.ts(t, P)], ps[:, t % 2, :].rearrange("p (k i) -> p k i", k=KD),
                                     ACT.Copy).then_inc(encT_ready, 1)

            def relu1(n):
                i, w = CH[n]
                for m in range(2):
                    act.wait_ge(m1_ps, 2 * n + m + 1)
                    nc.scalar.activation(o1T[:, m, i:i + w], ps[:, 2 + m, 0:w], ACT.Relu,
                                         bias=bcol[:, m:m + 1]).then_inc(m1_ready, 1)

            def relu2(n):
                i, w = CH[n]
                act.wait_ge(m2_ps, n + 1)
                nc.scalar.activation(o2T[:, i:i + w], ps[:, 4, 0:w], ACT.Relu, bias=bcol[:, 2:3]).then_inc(m2_ready, 1)

            def relu3(n):
                i, w = CH[n]
                for m in range(2):
                    act.wait_ge(m3_ps, 2 * n + m + 1)
                    nc.scalar.activation(o3T[:, m, i:i + w], ps[:, 5 - m, 0:w], ACT.Relu,
                                         bias=bcol[:, 3 + m:4 + m]).then_inc(m3_ready, 1)

            elu_exp(0)
            elu_exp(1)
            take_pt(H * T - 1, 1)
            for t in range(2, TA):
                elu_exp(t)
            for t in range(4):
                take_encT(t)
            act.wait_ge(enc_b, H)
            elu_exp(TA)
            elu_exp(TA + 1)
            elu_exp(TA + 2)
            relu1(0)
            elu_exp(TA + 3)
            elu_exp(T - 1)
            for t in range(4, 8):
                take_encT(t)
            act.wait_ge(scale3_ready, 1)
            nc.scalar.activation(m_parts[:, 0], M32, ACT.Copy, scale=sig3[:, 0:1]).then_inc(m_hi, 1)
            relu2(0)
            relu1(1)
            relu3(0)
            nc.scalar.activation(wv_parts[:, 0], wv, ACT.Copy, scale=sig3[:, 2:3]).then_inc(wv_hi, 1)
            for t in range(8, T):
                take_encT(t)
            relu2(1)
            relu1(2)
            relu3(1)

            def x3T_high(t):
                act.wait_ge(x3T_ps, t + 1)
                nc.scalar.activation(x3T[:, 0, :, bass.ts(t, P)], ps[:, t % 2, :].rearrange("p (k i) -> p k i", k=KD),
                                     ACT.Copy, scale=X_SCALE).then_inc(x3T_hi, 1)

            def v_high(t):
                act.wait_ge(v_ps, t + 1)
                nc.scalar.activation(vv[:, 0, t, :], ps[:, V_BANK[t % 2], :], ACT.Copy, scale=kc(A_V)).then_inc(v_hi, 1)

            x3T_high(0)
            x3T_high(1)
            relu2(2)
            x3T_high(2)
            relu3(2)
            x3T_high(3)
            v_high(0)
            v_high(1)
            for t in range(4, T):
                x3T_high(t)
                v_high(t - 2)

            def g_high(t, b):
                act.wait_ge(g_read, t + 1)
                if later(t):
                    act.wait_ge(sc_ps, t - 1)
                nc.scalar.activation(g_parts[:, b, 0], g32[:, b], ACT.Copy).then_inc(g_hi, 1)

            def soft(t, b):
                act.wait_ge(s3_ready, t + 1)
                nc.scalar.activation(S3[:, b, 0:N], S3[:, b, 0:N], ACT.Exp, scale=kc(KAPPA),
                                     bias=nmax[:, b:b + 1], accum_out=rs3[:, b:b + 1]).then_inc(p3_ready, 1)

            def last(t, b, n):
                act.wait_ge(pt3_ps, t + 1)
                if later(t):
                    act.wait_ge(o3_ps, t - 1)
                nc.scalar.activation(PT3[:, b, 0, :], ps[:, 3:6, :].rearrange("p b i -> p (b i)")[:, 0:NP],
                                     ACT.Copy, scale=P_SCALE).then_inc(pt3_hi, 1)
                if before_end(t, 1):
                    soft(t + 1, 1 - b)
                if before_end(t, 3):
                    g_high(t + 3, 1 - b)

            g_high(0, 0)
            g_high(1, 1)
            v_high(T - 2)
            soft(0, 0)
            v_high(T - 1)
            g_high(2, 0)
            last_tiles(last)(act)

        @block.vector
        def _(dve):
            v = nc.vector
            ch = Chain(dve, dve_a)

            def rsqrt(ch, y, val, h, t):
                def h_of_y():
                    if y.shape[-1] == 1:
                        ch(v.scalar_tensor_tensor(out=h, in0=y, scalar=val, in1=y, op0=ALU.mult, op1=ALU.mult))
                    else:
                        ch(v.tensor_tensor(h, y, y, ALU.mult))
                        ch(v.tensor_tensor(h, h, val, ALU.mult))
                ch(v.tensor_scalar(h.bitcast(I32), val.bitcast(I32), 1, None, ALU.logical_shift_right))
                ch(v.tensor_scalar(y.bitcast(I32), h.bitcast(I32), -1.0, float(RSQRT_SEED - 2 ** 31), ALU.mult, ALU.add))
                h_of_y()
                ch(v.scalar_tensor_tensor(out=t, in0=h, scalar=-10.0 / 3.0, in1=h, op0=ALU.add, op1=ALU.mult))
                ch(v.scalar_tensor_tensor(out=y, in0=t, scalar=5.0, in1=y, op0=ALU.add, op1=ALU.mult))
                h_of_y()
                ch(v.scalar_tensor_tensor(out=y, in0=h, scalar=-3.0 * (8.0 / 3.0) ** 2, in1=y, op0=ALU.add, op1=ALU.mult))

            def x_levels(k):
                dve.wait_ge(ld_xT[k], 16)
                ch(v.tensor_scalar(xT3[:, k, :], xT3[:, k, :], c(RALPHA), 1.0, ALU.mult, ALU.min))
                v.tensor_scalar(xT3[:, k, :], xT3[:, k, :], X_LEVELS, ROUND, ALU.mult, ALU.add).then_inc(x_rounded, 1)

            dve.wait_ge(ld_sc, 16)
            ch(v.reciprocal(c(RWA), scs[:, 1:2]))
            ch(v.reciprocal(c(RALPHA), scs[:, 2:3]))
            dve.wait_ge(wsum_out, 1)
            v.tensor_scalar(c(NMEAN), ps[:, 7, 0:1], -1.0 / (D * D), None, ALU.mult).then_inc(mean_ready, 1)
            x_levels(0)
            dve.wait_ge(wsum_out, 2)
            ch(v.tensor_scalar(rv[:, 2:3], ps[:, 7, 1:2], RSQRT_GAIN ** 2 / (D * D - 1), None, ALU.mult))
            rsqrt(ch, c(RSTD), rv[:, 2:3], rv[:, 3:4], rv[:, 4:5])
            dve.wait_ge(mean_ready, 1)
            ch(v.tensor_scalar(wlev, wlev, c(NMEAN), c(RSTD), ALU.add, ALU.mult))
            ch(v.tensor_scalar(wlev, wlev, c(RWA), 1.0, ALU.mult, ALU.min))
            x_levels(1)
            ch(v.tensor_scalar(wlev, wlev, -1.0, W_LEVELS, ALU.max, ALU.mult))
            v.tensor_scalar(wlev, wlev, ROUND, ROUND, ALU.add, ALU.subtract).then_inc(wq_ready, 1)
            for k in range(2, KD):
                x_levels(k)

            ch(v.tensor_scalar(c(C_Q), scs[:, 2:3], 1.0 / X_LEVELS, None, ALU.mult))
            ch(v.tensor_scalar(c(TMP), scs[:, 1:2], 1.0 / W_LEVELS, c(C_Q), ALU.mult, ALU.mult))
            ch(v.reciprocal(rv[:, 4:5], scs[:, 3:4]))
            ch(v.tensor_scalar(c(C_Q), c(TMP), rv[:, 4:5], None, ALU.mult))

            def quantise(t):
                b = t % 2
                dve.wait_ge(sup_done, t + 1)
                if t >= 2:
                    dve.wait_ge(q_ready, t - 1)
                ch(v.tensor_scalar(pre[:, b, :], ps[:, b, :], c(C_Q), 0.0, ALU.mult, ALU.max))
                ch(v.tensor_scalar(pre[:, b, :], pre[:, b, :], 1.0, X_LEVELS, ALU.min, ALU.mult))
                v.tensor_scalar(q[:, t, :], pre[:, b, :], ROUND, ROUND, ALU.add, ALU.subtract).then_inc(q_ready, 1)

            Q_AHEAD = 4
            for t in range(Q_AHEAD):
                quantise(t)

            dve.wait_ge(asum_ready, T)
            v.tensor_reduce(amax[:, 4:5], asum[:], AX_X, ALU.max).then_inc(amax_in, 1)
            dve.wait_ge(amax_out, 1)
            ch(v.tensor_scalar(c(TMP), amax[:, 5:6], 1.0, None, ALU.add))
            ch(v.tensor_scalar(c(RSIG).bitcast(I32), c(TMP).bitcast(I32), 0x7F800000, None, ALU.bitwise_and))
            ch(v.tensor_scalar(c(RSIG), c(RSIG), 1.0 / A_TOP, None, ALU.mult))
            ch(v.reciprocal(c(SIG), c(RSIG)))
            v.tensor_scalar(c(SIGH), c(SIG), 0.5, None, ALU.mult).then_inc(sig_ready, 1)
            ch(v.reciprocal(rv[:, 5:6], scs[:, 0:1]))
            ch(v.tensor_scalar(rv[:, 6:7], rv[:, 5:6], scs[:, 0:1], 1.0 / X_LEVELS, ALU.mult, ALU.mult))
            ch(v.tensor_scalar(c(F0), rv[:, 6:7], scs[:, 3:4], c(RSIG), ALU.mult, ALU.mult))
            ch(v.tensor_scalar(c(F1), c(RSIG), 1.0 / Y_SCALE, None, ALU.mult))
            ch(v.tensor_scalar(c(CY), c(RSIG), Y_SCALE / (X_SCALE * X_SCALE), None, ALU.mult))

            for t in range(T):
                dve.wait_ge(at_hi, t + 1)
                v.scalar_tensor_tensor(out=r_at[:, 1, t, :], in0=at_raw[:, t, :], scalar=c(SIG), in1=r_at[:, 0, t, :],
                                       op0=ALU.mult, op1=ALU.subtract).then_inc(at_lo, 1)
                if t + Q_AHEAD < T:
                    quantise(t + Q_AHEAD)
            dve.wait_ge(at_lo, T)
            dve.wait_ge(q_ready, T)

            LN_CHAINED = 3 + 7

            def layer_norm(ch, t, b, dst=None):
                ch(v.bn_stats(bns[:], pre[:, b, :]))
                v.memset(junk[:], 0.0)
                ch(v.bn_aggr(mv[:], bns[:]))
                ch(v.tensor_scalar(rv[:, 0:1], mv[:, 1:2], LN_EPS, RSQRT_GAIN ** 2, ALU.add, ALU.mult))
                rsqrt(ch, rv[:, 2:3], rv[:, 0:1], rv[:, 4:5], rv[:, 6:7])
                return v.tensor_scalar(r_x[:, t, :] if dst is None else dst, pre[:, b, :], mv[:, 0:1], rv[:, 2:3],
                                       ALU.subtract, ALU.mult)

            dve.wait_ge(ld_x, 16)
            K0 = LN_CHAINED + 1

            def ln0(t, b, buf, n):
                dve.wait_ge(s_hi, t + 1)
                v.scalar_tensor_tensor(out=r_s[:, t, 1, :], in0=nat_buf[buf], scalar=c(SIGH), in1=r_s[:, t, 0, :],
                                       op0=ALU.mult, op1=ALU.subtract).then_inc(s_lo, 1)
                ch = Chain(dve, dve_ln0, t * K0)
                dve.wait_ge(aq_done, t + 1)
                v.scalar_tensor_tensor(out=pre[:, b, :], in0=ps[:, 2 + b, :], scalar=c(F0), in1=r_x[:, t, :],
                                       op0=ALU.mult, op1=ALU.add).then_inc(aq_read, 1)
                dve.wait_ge(aq_read, t + 1)
                layer_norm(ch, t, b).then_inc(x1_ready, 1)
                assert ch.n == K0 - 1, ch.n
                dve.wait_ge(x1_ready, t + 1)
                v.memset(junk[:], 0.0).then_inc(dve_ln0, 1)
            tiles4(dve, ln0)

            ch = Chain(dve, dve_d)
            dve.wait_ge(s_lo, T)
            ch(v.tensor_scalar(dtmp[:, 0], dcol[:], c(RSIG), 1e-30, ALU.mult, ALU.max))
            rsqrt(ch, dtmp[:, 1], dtmp[:, 0], dtmp[:, 2], dtmp[:, 3])
            ch(v.tensor_scalar(dtmp[:, 2], dcol[:], 0.0, X_SCALE / RSQRT_GAIN, ALU.is_gt, ALU.mult))
            ch(v.tensor_tensor(dcol[:], dtmp[:, 2], dtmp[:, 1], ALU.mult))
            ch(v.tensor_scalar(ycol[:], dcol[:], c(CY), None, ALU.mult))
            v.memset(junk[:], 0.0).then_inc(deg_ready, 1)

            def x1_lo(t, b):
                dve.wait_ge(xs_hi, t + 1)
                v.scalar_tensor_tensor(out=r_xs[:, 1, t, :], in0=r_x[:, t, :], scalar=dcol[:, bass.ts(t, 1)],
                                       in1=r_xs[:, 0, t, :], op0=ALU.mult, op1=ALU.subtract).then_inc(xs_lo, 1)
            tiles(dve, x1_lo)

            def y_low(t):
                b = t % 2
                dve.wait_ge(y_hi, t + 1)
                v.scalar_tensor_tensor(out=r_y[:, 1, t, :], in0=ps[:, 4 + b, :], scalar=ycol[:, t:t + 1],
                                       in1=r_y[:, 0, t, :], op0=ALU.mult, op1=ALU.subtract).then_inc(y_lo, 1)

            def fold_a(k):
                for a in range(2):
                    ch(v.tensor_tensor(prod, W2_st[:, k, :], a_bc[:, a], ALU.mult))
                    ch(v.tensor_reduce(wa[:, k, a * H:(a + 1) * H], prod.rearrange("p (h d) -> p h d", h=H), AX_X, ALU.add))

            ch = Chain(dve, dve_w)
            for t in range(T):
                y_low(t)
                if t == 0:
                    dve.wait_ge(ld_w2, 16)
                    dve.wait_ge(ld_a, 16)
                if t < KD:
                    fold_a(t)
                if t == KD:
                    ch(v.tensor_reduce(amax[:, 0:1], W2_st.rearrange("p k d -> p (k d)"), AX_X, ALU.max,
                                       apply_absolute_value=True))
                    ch(v.tensor_reduce(amax[:, 1:2], wa[:].rearrange("p k h -> p (k h)"), AX_X, ALU.max,
                                       apply_absolute_value=True))
                    v.memset(junk[:], 0.0).then_inc(scale2_in, 1)
                if t == KD + 1:
                    dve.wait_ge(scale2_out, 1)
                    ch(v.tensor_scalar(amax[:, 2:4], amax[:, 2:4], 1e-18, None, ALU.max))
                    ch(v.tensor_scalar(r_sig2[:].bitcast(I32), amax[:, 2:4].bitcast(I32), 0x7F800000, None,
                                       ALU.bitwise_and))
                    ch(v.tensor_scalar(r_sig2[:], r_sig2[:], 1.0 / A_TOP, None, ALU.mult))
                    ch(v.reciprocal(sig2[:], r_sig2[:]))
                    ch(v.tensor_scalar(back2[:], r_sig2[:], 1.0 / X_SCALE, None, ALU.mult))
                    v.memset(junk[:], 0.0).then_inc(scale2_ready, 1)

            ch = Chain(dve, dve_p)
            dve.wait_ge(sx_done, T)
            dve.wait_ge(w2_hi, 1)
            v.scalar_tensor_tensor(out=W2[:, 1], in0=W2_st, scalar=sig2[:, 0:1], in1=W2[:, 0],
                                   op0=ALU.mult, op1=ALU.subtract).then_inc(w2_ready, 1)
            dve.wait_ge(w2_hi, 2)
            v.scalar_tensor_tensor(out=wa_parts[:, 1], in0=wa[:], scalar=sig2[:, 1:2], in1=wa_parts[:, 0],
                                   op0=ALU.mult, op1=ALU.subtract).then_inc(wa_ready, 1)

            K1 = LN_CHAINED + 1

            def ln1(t, b):
                dve.wait_ge(ld_m[b], 16 * nth(t, b))
                v.tensor_scalar(mask[:, t, :], r_st[:, b, 0:N], 0.0, NEG, ALU.is_le, ALU.mult).then_inc(mask_ready, 1)
                ch = Chain(dve, dve_ln1, t * K1)
                dve.wait_ge(ay_done, t + 1)
                if later(t):
                    dve.wait_ge(x2_kept, t - 1)
                    dve.wait_ge(x2T_ps, t - 1)
                v.scalar_tensor_tensor(out=pre[:, b, :], in0=ps[:, 2 + b, :], scalar=c(F1), in1=r_x[:, t, :],
                                       op0=ALU.mult, op1=ALU.add).then_inc(ay_read, 1)
                dve.wait_ge(ay_read, t + 1)
                layer_norm(ch, t, b, x2[:, b, :]).then_inc(x2_ready, 1)
                assert ch.n == K1 - 1, ch.n
                dve.wait_ge(x2_ready, t + 1)
                v.memset(junk[:], 0.0).then_inc(dve_ln1, 1)
                if at_least(t, 1):
                    x2T_low(t - 1, 1 - b)
                if at_least(t, 2):
                    logits(t - 2, b)
                if at_least(t, 3):
                    take_ed(t - 3, 1 - b)

            def x2T_low(t, b):
                dve.wait_ge(x2T_hi, t + 1)
                v.scalar_tensor_tensor(out=x2T[:, b, 1], in0=ps[:, b, :].rearrange("p (k i) -> p k i", k=KD),
                                       scalar=X_SCALE, in1=x2T[:, b, 0], op0=ALU.mult,
                                       op1=ALU.subtract).then_inc(x2T_ready, 1)

            def logits(t, b):
                dve.wait_ge(e_ps, t + 1)
                if later(t):
                    dve.wait_ge(ed_ps, t - 1)
                v.tensor_scalar(ed[:, b, :], ps[:, 6 + b, H:2 * H], back2[:, 1:2], None, ALU.mult).then_inc(e_ready, 1)
                v.tensor_scalar(es[:, :, bass.ts(t, 1)], ps[:, 6 + b, 0:H].unsqueeze(2), back2[:, 1:2], 1.0 - LEAK,
                                ALU.mult, ALU.mult).then_inc(e_ready, 1)

            def take_ed(t, b):
                dve.wait_ge(ed_ps, t + 1)
                v.tensor_copy(edrow[:, bass.ts(t, P)], ps[0:H, 6 + b, P:2 * P]).then_inc(ed_ready, 1)

            tiles(dve, ln1, 2)
            x2T_low(T - 1, 0)
            logits(T - 2, 1)
            take_ed(T - 3, 0)
            logits(T - 1, 0)
            take_ed(T - 2, 1)
            take_ed(T - 1, 0)
            dve.wait_ge(ay_done, T)
            ch(v.memset(Wh[:, :, :, HD:HW], 1.0))
            v.memset(PR0[:, N:NP], 0.0).then_inc(pad_ready, 1)

            dve.wait_ge(e_ready, 2 * T)
            dve.wait_ge(mask_ready, T)
            dve.wait_ge(ed_stored, 16)
            v.memset(PR1[:, N:NP], 0.0).then_inc(pad_ready, 1)
            dve.wait_ge(pad_ready, 2)
            KG = 1 + 2 * T + 2 + 2 * 2

            def take_enc(ch, h, bank, t0, nt):
                src = ps[:, bank, 0:nt * HW].rearrange("p (t d) -> p t d", t=nt)
                ch(v.reciprocal(rsum[:, 0:nt], src[:, :, HD]))
                return v.tensor_tensor(enc[:, t0:t0 + nt, bass.ts(h, HD)], src[:, :, 0:HD],
                                       rsum[:, 0:nt].unsqueeze(2).broadcast_to([P, nt, HD]), ALU.mult)

            def scores(hp):
                first = isinstance(hp, int)
                ch = Chain(dve, dve_g, hp * KG)
                ch(v.tensor_copy(es_pair[:], es[:, bass.ts(hp, 2), :].rearrange("p h t -> p (h t)")))
                for s in range(2 * T):
                    hh, t = divmod(s, T)
                    n = hp * 2 * T + s
                    b = s % 2
                    if t == 0:
                        dve.wait_ge(ld_d[hh], 16 * (hp + 1))
                        ch(v.tensor_scalar(drow[:, hh, 1, :], drow[:, hh, 0, :], LEAK, None, ALU.mult))
                    if not (first and s < 2):
                        dve.wait_ge(p_ready, n - 1)
                    ch(v.scalar_tensor_tensor(out=G[:, b, :], in0=drow[:, hh, 0, :], scalar=es_pair[:, s:s + 1],
                                              in1=drow[:, hh, 1, :], op0=ALU.add, op1=ALU.max))
                    v.memset(junk[:], 0.0)
                    v.tensor_tensor_reduce(out=G[:, b, :], in0=G[:, b, :], in1=mask[:, t, :], scale=-1.0,
                                           scalar=BIG, op0=ALU.add, op1=ALU.min,
                                           accum_out=nmax[:, b:b + 1]).then_inc(g_ready, 1)
                    if t == T - 1:
                        dve.wait_ge(g_ready, n + 1)
                        v.memset(junk[:], 0.0).then_inc(d_used, 1)
                    if t == 9:
                        dve.wait_ge(o_done, (2 * hp + hh) * T + TA)
                        take_enc(ch, 2 * hp + hh, 6, 0, TA).then_inc(enc_a, 1)
                        dve.wait_ge(enc_a, 2 * hp + hh + 1)
                    if t == 3 and not (first and hh == 0):
                        dve.wait_ge(o_done, (2 * hp + hh) * T)
                        take_enc(ch, 2 * hp + hh - 1, 7, TA, T - TA).then_inc(enc_b, 1)
                        dve.wait_ge(enc_b, 2 * hp + hh)
                if first:
                    ch(v.nop())
                assert ch.n == KG
            scores(0)
            with dve.Fori(1, H // 2) as hp:
                scores(hp)
            ch = Chain(dve, dve_m)

            def elu(t):
                dve.wait_ge(elu_e, t + 1)
                ch(v.tensor_scalar(pre[:, t % 2, :], pre[:, t % 2, :], 1.0, -1.0, ALU.min, ALU.add))
                v.tensor_tensor(enc[:, t, :], enc[:, t, :], pre[:, t % 2, :], ALU.max).then_inc(elu_done, 1)

            dve.wait_ge(g_ready, H * T)
            dve.wait_ge(enc_a, H)
            elu(0)
            elu(1)
            for t in range(2, TA):
                elu(t)
            dve.wait_ge(o_done, H * T)
            take_enc(ch, H - 1, 7, TA, T - TA).then_inc(enc_b, 1)
            dve.wait_ge(enc_b, H)
            dve.wait_ge(fold_ready, FOLDS)
            dve.wait_ge(ld_fold, 16 * 2)
            dve.wait_ge(ld_qkv, 16)
            dve.wait_ge(ld_bv, 16)
            for n, src in ((0, M32.rearrange("p k d -> p (k d)")), (1, fold[:, 0:KD]), (2, wv.rearrange("p k d -> p (k d)"))):
                ch(v.tensor_reduce(amax[:, n:n + 1], src, AX_X, ALU.max, apply_absolute_value=True))
            v.memset(junk[:], 0.0).then_inc(bound_in, 1)
            for t in range(TA, T):
                elu(t)
            dve.wait_ge(bound_out, 1)
            ch(v.scalar_tensor_tensor(out=bound[:, 1:2], in0=bound[:, 0:1], scalar=float(D), in1=bound[:, 1:2],
                                      op0=ALU.mult, op1=ALU.add))
            ch(v.tensor_scalar(bound[:, 3:4], bound[:, 2:3], float(D), None, ALU.mult))
            ch(v.tensor_scalar(bound[:], bound[:], 1e-18, None, ALU.max))
            ch(v.tensor_scalar(r_sig3[:].bitcast(I32), bound[:].bitcast(I32), 0x7F800000, None, ALU.bitwise_and))
            ch(v.tensor_scalar(r_sig3[:], r_sig3[:], 1.0 / A_TOP, None, ALU.mult))
            ch(v.reciprocal(sig3[:], r_sig3[:]))
            v.memset(junk[:], 0.0).then_inc(scale3_ready, 1)
            for dst, src, by in ((A_G, 1, 0), (A_V, 3, 2)):
                ch(v.tensor_scalar(kc(dst), sig3[:, src:src + 1], r_sig3[:, by:by + 1], 1.0 / X_SCALE, ALU.mult, ALU.mult))
            ch(v.tensor_scalar(kc(KAPPA), r_sig3[:, 1:2], -float(D) ** -0.5 / X_SCALE, None, ALU.mult))
            ch(v.tensor_scalar(kc(NEG_K), sig3[:, 1:2], NEG3 * float(D) ** 0.5 * X_SCALE, None, ALU.mult))
            ch(v.tensor_scalar(kc(R_V), r_sig3[:, 3:4], 1.0 / P_SCALE, None, ALU.mult))
            ch(v.tensor_scalar(kc(S_R), sig3[:, 1:2], X_SCALE, None, ALU.mult))
            ch(v.tensor_scalar(w_row, w_row, kc(S_R), None, ALU.mult))
            ch(v.tensor_scalar(fold[:, KD:KD + 1], fold[:, KD:KD + 1], kc(S_R), None, ALU.mult))
            ch(v.tensor_scalar(fold[:, 0:KD], fold[:, 0:KD], sig3[:, 1:2], None, ALU.mult))
            for b in range(2):
                v.memset(S3[:, b, N:NP], 0.0).then_inc(s3_pad, 1)

            dve.wait_ge(elu_done, T)
            dve.wait_ge(ld_mlp, 16 * 5)
            dve.wait_ge(m_hi, 1)
            v.scalar_tensor_tensor(out=m_parts[:, 1], in0=M32, scalar=sig3[:, 0:1], in1=m_parts[:, 0],
                                   op0=ALU.mult, op1=ALU.subtract).then_inc(m_ready, 1)
            dve.wait_ge(wv_hi, 1)
            v.scalar_tensor_tensor(out=wv_parts[:, 1], in0=wv, scalar=sig3[:, 2:3], in1=wv_parts[:, 0],
                                   op0=ALU.mult, op1=ALU.subtract).then_inc(wv_ready, 1)

            def ln2(t):
                b = t % 2
                dve.wait_ge(m4_ps, t + 1)
                dve.wait_ge(b4_added, t + 1)
                v.tensor_tensor(pre[:, b, :], ps[:, 6 + b, :], r_x[:, t, :], ALU.add).then_inc(m4_read, 1)
                dve.wait_ge(m4_read, t + 1)
                layer_norm(ch, t, b).then_inc(x3_ready, 1)
                dve.wait_ge(x3_ready, t + 1)

            def x3T_low(t):
                dve.wait_ge(x3T_hi, t + 1)
                v.scalar_tensor_tensor(out=x3T[:, 1, :, bass.ts(t, P)],
                                       in0=ps[:, t % 2, :].rearrange("p (k i) -> p k i", k=KD), scalar=X_SCALE,
                                       in1=x3T[:, 0, :, bass.ts(t, P)], op0=ALU.mult, op1=ALU.subtract).then_inc(x3T_ready, 1)

            def v_low(t):
                dve.wait_ge(v_hi, t + 1)
                v.scalar_tensor_tensor(out=vv[:, 1, t, :], in0=ps[:, V_BANK[t % 2], :], scalar=kc(A_V), in1=vv[:, 0, t, :],
                                       op0=ALU.mult, op1=ALU.subtract).then_inc(v_lo, 1)

            for t in range(T + 3):
                if t < T:
                    ln2(t)
                if 2 <= t < T + 2:
                    x3T_low(t - 2)
                if t >= 5:
                    v_low(t - 5)

            def take_g(t, b):
                dve.wait_ge(g_ps, t + 1)
                if later(t):
                    dve.wait_ge(g_lo, t - 1)
                v.scalar_tensor_tensor(out=g32[:, b], in0=ps[:, 6, :].rearrange("p (k i) -> p k i", k=KD), scalar=kc(A_G),
                                       in1=fold[:, 0:KD].unsqueeze(2).broadcast_to([P, KD, P]), op0=ALU.mult,
                                       op1=ALU.add).then_inc(g_read, 1)

            def row_part(ch, t, b):
                col = r_col[:, bass.ts(t, 1)]
                ch(v.tensor_tensor(pre[:, b, :], r_x[:, t, :], w_row, ALU.mult))
                ch(v.tensor_reduce(col, pre[:, b, :], AX_X, ALU.add))
                ch(v.tensor_scalar(col, col, fold[:, KD:KD + 1], None, ALU.add))

            def masked(ch, t, b, n):
                dve.wait_ge(sc_ps, t + 1)
                dve.wait_ge(ld_a3[b], 16 * n)
                if later(t):
                    dve.wait_ge(pt3_ps, t - 1)
                v.scalar_tensor_tensor(out=S3[:, b, 0:N], in0=ps[:, 0:3, :].rearrange("p b i -> p (b i)")[:, 0:N],
                                       scalar=r_col[:, bass.ts(t, 1)], in1=r_st[:, b, 0:N], op0=ALU.add,
                                       op1=ALU.mult).then_inc(sc_read, 1)
                dve.wait_ge(sc_read, t + 1)
                ch(v.tensor_scalar(Z3[:, 0:N], S3[:, b, 0:N], 0.0, kc(NEG_K), ALU.is_equal, ALU.mult))
                v.memset(junk[:], 0.0)
                ch(v.tensor_tensor_reduce(out=S3[:, b, 0:N], in0=S3[:, b, 0:N], in1=Z3[:, 0:N], scale=-1.0,
                                          scalar=BIG, op0=ALU.add, op1=ALU.min, accum_out=rv[:, 7:8]))
                v.tensor_scalar(nmax[:, b:b + 1], rv[:, 7:8], kc(KAPPA), -1.0, ALU.mult, ALU.mult).then_inc(s3_ready, 1)
                dve.wait_ge(s3_ready, t + 1)

            def pt_low(t, b):
                dve.wait_ge(pt3_hi, t + 1)
                v.scalar_tensor_tensor(out=PT3[:, b, 1, :], in0=ps[:, 3:6, :].rearrange("p b i -> p (b i)")[:, 0:NP],
                                       scalar=P_SCALE, in1=PT3[:, b, 0, :], op0=ALU.mult, op1=ALU.subtract).then_inc(pt3_lo, 1)

            def read_out(ch, t, b):
                dve.wait_ge(o3_ps, t + 1)
                ch(v.reciprocal(rsum[:, 0:1], rs3[:, b:b + 1]))
                ch(v.tensor_scalar(rsum[:, 1:2], rsum[:, 0:1], kc(R_V), None, ALU.mult))
                v.scalar_tensor_tensor(out=pre[:, b, :], in0=ps[:, 7, :], scalar=rsum[:, 1:2], in1=v_row, op0=ALU.mult,
                                       op1=ALU.add).then_inc(o3_read, 1)

            def finish(ch, t, b):
                dve.wait_ge(o3_read, t + 1)
                ch(v.scalar_tensor_tensor(out=pre[:, b, :], in0=pre[:, b, :], scalar=0.0, in1=r_x[:, t, :], op0=ALU.max,
                                          op1=ALU.add))
                layer_norm(ch, t, b).then_inc(x4_ready, 1)
                dve.wait_ge(x4_ready, t + 1)

            K3 = (1 + LN_CHAINED) + 3 + 2 + 2

            def last(t, b, n):
                ch = ch3 if isinstance(t, int) else Chain(dve, dve_3, t * K3 + after_two[0] - 2 * K3)
                pt_low(t, b)
                if at_least(t, 1):
                    finish(ch, t - 1, 1 - b)
                if before_end(t, 1):
                    row_part(ch, t + 1, 1 - b)
                    masked(ch, t + 1, 1 - b, n + b)
                if before_end(t, 3):
                    take_g(t + 3, 1 - b)
                read_out(ch, t, b)
                if not isinstance(t, int):
                    assert ch.n == K3, ch.n
                elif t == 1:
                    after_two[0] = ch.n
                    ch3.n += (T - 5) * K3

            after_two = [None]

            ch3 = Chain(dve, dve_3)
            take_g(0, 0)
            take_g(1, 1)
            row_part(ch3, 0, 0)
            dve.wait_ge(s3_pad, 2)
            masked(ch3, 0, 0, 1)
            v_low(T - 2)
            v_low(T - 1)
            take_g(2, 0)
            last_tiles(last)(dve)
            finish(ch3, T - 1, 0)

        @block.tensor
        def _(pe):
            mm = nc.tensor.matmul
            pe.wait_ge(const_ready, 5)
            for n in range(2):
                pe.wait_ge(wsum_in, n + 1)
                mm(ps[:, 7, n:n + 1], ones[:], rv[:, n:n + 1], start=True, stop=True).then_inc(wsum_out, 1)
            pe.wait_ge(wq_ready, 1)
            for t in range(T):
                b = t % 2
                if t >= 2:
                    pe.wait_ge(q_ready, t - 1)
                for k in range(KD):
                    if t == 0:
                        pe.wait_ge(xq_ready, k + 1)
                    last = mm(ps[:, b, :], xT3[:, k, bass.ts(t, P)], wk3[:, k, :], start=(k == 0), stop=(k == KD - 1))
                last.then_inc(sup_done, 1)
            pe.wait_ge(q_ready, T)

            def aq(t, b):
                if later(t):
                    pe.wait_ge(aq_read, t - 1)
                for j in range(T):
                    if isinstance(t, int) and t == 0:
                        pe.wait_ge(at_lo, j + 1)
                    for part in range(2):
                        last = mm(ps[:, 2 + b, :], r_at[:, part, j, bass.ts(t, P)], q[:, j, :],
                                  start=(j == 0 and part == 0), stop=(j == T - 1 and part == 1))
                last.then_inc(aq_done, 1)
            tiles(pe, aq)

            def split_product(out_bank, left, right, wait_right=None):
                for j in range(T):
                    if wait_right:
                        wait_right(j)
                    for part, (a, bb) in enumerate(((0, 0), (0, 1), (1, 0))):
                        last = mm(out_bank, left(a, j), right[:, bb, j, :], start=(j == 0 and part == 0),
                                  stop=(j == T - 1 and part == 2))
                return last

            pe.wait_ge(ld_qk, 16 * 2)
            pe.wait_ge(ld_b, 16 * 5)
            pe.wait_ge(bqk_ready, 1)
            for n in range(FOLDS):
                if n == 4:
                    pe.wait_ge(fold_ready, 2)
                out_n = ps[:, FOLD_BANK[n], :]
                for k in range(KD):
                    st = dict(start=(k == 0), stop=(k == KD - 1))
                    if n < KD:
                        last = mm(out_n, wq_n[:, k, bass.ts(n, P)], wk_n[:, k, :], **st)
                    elif n == KD:
                        last = mm(out_n[0:1, :], bcol[:, 9 + k:10 + k], wq_n[:, k, :], **st)
                    else:
                        last = mm(out_n[:, KD:KD + 1], ones[:], bqk[:, k:k + 1], **st)
                if n == KD + 1:
                    for m in range(KD):
                        for k in range(KD):
                            last = mm(out_n[:, m:m + 1], wk_n[:, k, bass.ts(m, P)], bcol[:, 5 + k:6 + k],
                                      start=(k == 0), stop=(k == KD - 1))
                last.then_inc(fold_ps, 1)

            pe.wait_ge(s_lo, T)

            def sx(t, b):
                first = isinstance(t, int) and t == 0
                if later(t):
                    pe.wait_ge(y_lo, t - 1)
                def wait_right(j):
                    pe.wait_ge(xs_lo, j + 1)
                split_product(ps[:, 4 + b, :], lambda a, j: r_s[:, j, a, bass.ts(t, P)], r_xs,
                              wait_right if first else None).then_inc(sx_done, 1)
            tiles(pe, sx)

            pe.wait_ge(x1_ready, T)

            tr = nc.tensor.transpose

            def parts(out, left, right, ks):
                for k in ks:
                    for n, (a, bb) in enumerate(((0, 0), (0, 1), (1, 0))):
                        last = mm(out, left(a, k), right(bb, k), start=(k == ks[0] and n == 0), stop=(k == ks[-1] and n == 2))
                return last

            def ay(t, b):
                first = isinstance(t, int) and t == 0
                if later(t):
                    pe.wait_ge(ay_read, t - 1)

                def wait_right(j):
                    pe.wait_ge(y_lo, j + 1)
                split_product(ps[:, 2 + b, :], lambda a, j: r_at[:, a, j, bass.ts(t, P)], r_y,
                              wait_right if first else None).then_inc(ay_done, 1)
                if at_least(t, 1):
                    turn_x2(t - 1, 1 - b)
                if at_least(t, 2):
                    logits(t - 2, b)
                    project(t - 2, b)
                if at_least(t, 3):
                    turn_ed(t - 3, 1 - b)

            def turn_x2(t, b):
                pe.wait_ge(x2_ready, t + 1)
                if later(t):
                    pe.wait_ge(x2T_ready, t - 1)
                for k in range(KD):
                    last = tr(ps[:, b, bass.ts(k, P)], x2[:, b, bass.ts(k, P)], ident[:])
                last.then_inc(x2T_ps, 1)

            def logits(t, b):
                pe.wait_ge(x2T_ready, t + 1)
                if isinstance(t, int) and t == 0:
                    pe.wait_ge(wa_ready, 1)
                if later(t):
                    pe.wait_ge(ed_ready, t - 1)
                parts(ps[:, 6 + b, 0:2 * H], lambda a, k: x2T[:, b, a, k, :], lambda a, k: wa_parts[:, a, k, :],
                      range(KD)).then_inc(e_ps, 1)

            def project(t, b):
                if isinstance(t, int) and t == 0:
                    pe.wait_ge(w2_ready, 1)
                if later(t):
                    pe.wait_ge(wh_ready, t - 1)
                parts(ps[:, 4 + b, :], lambda a, k: x2T[:, b, a, k, :], lambda a, k: W2[:, a, k, :],
                      range(KD)).then_inc(wh_ps, 1)

            def turn_ed(t, b):
                pe.wait_ge(e_ready, 2 * t + 2)
                tr(ps[0:H, 6 + b, P:2 * P], ed[:, b, :], ident[:]).then_inc(ed_ps, 1)

            tiles(pe, ay, 2)
            turn_x2(T - 1, 0)
            logits(T - 2, 1)
            turn_ed(T - 3, 0)
            logits(T - 1, 0)
            turn_ed(T - 2, 1)
            turn_ed(T - 1, 0)
            project(T - 2, 1)
            project(T - 1, 0)
            pe.wait_ge(wh_ready, T)
            pe.wait_ge(ed_ready, T)

            def weigh(n, s, h, hh, t):
                pe.wait_ge(pt_ready, n + 1)
                if t == 0 and later(h + 1):
                    pe.wait_ge(enc_a, h)
                if t == TA and later(h + 1):
                    pe.wait_ge(enc_b, h)
                bank, c0 = (6, t * HW) if t < TA else (7, (t - TA) * HW)
                for j in range(T):
                    last = mm(ps[:, bank, c0:c0 + HW], PT[:, s % 2, bass.ts(j, P)],
                              Wh[:, j, bass.ts(h, 1), :].rearrange("p h d -> p (h d)"), start=(j == 0), stop=(j == T - 1))
                last.then_inc(o_done, 1)

            def heads(hp):
                first = isinstance(hp, int)
                for s in range(2 * T):
                    hh, t = divmod(s, T)
                    n = hp * 2 * T + s
                    pe.wait_ge(p_ready, n + 1)
                    if not (first and s < 2):
                        pe.wait_ge(pt_ready, n - 1)
                    for j in range(T):
                        last = tr(ps[:, 3 * (s % 2) + j // KD, bass.ts(j % KD, P)], PR[s % 2][:, bass.ts(j, P)], ident[:])
                    last.then_inc(pt_ps, 1)
                    if not (first and s == 0):
                        hb, tb = divmod((s - 1) % (2 * T), T)
                        h = 2 * hp + hb if s else 2 * hp - 1
                        weigh(n - 1, (s - 1) % 2, h, hb, tb)

            heads(0)
            with pe.Fori(1, H // 2) as hp:
                heads(hp)
            weigh(H * T - 1, 1, H - 1, 1, T - 1)

            pe.wait_ge(ld_mlp, 16 * 5)

            def turn_enc(t):
                pe.wait_ge(elu_done, t + 1)
                if t >= 2:
                    pe.wait_ge(encT_ready, t - 1)
                for k in range(KD):
                    last = tr(ps[:, t % 2, bass.ts(k, P)], enc[:, t, bass.ts(k, P)], ident[:])
                last.then_inc(encT_ps, 1)

            def mlp1(n):
                i, w = CH[n]
                pe.wait_ge(encT_ready, (i + w) // P)
                for m in range(2):
                    if n:
                        pe.wait_ge(m1_ready, 2 * (n - 1) + m + 1)
                    for k in range(KD):
                        last = mm(ps[:, 2 + m, 0:w], w1[:, k, bass.ts(m, P)], encT[:, k, i:i + w], start=(k == 0), stop=(k == KD - 1))
                    last.then_inc(m1_ps, 1)

            def mlp2(n):
                i, w = CH[n]
                pe.wait_ge(m1_ready, 2 * n + 2)
                if n:
                    pe.wait_ge(m3_ready, 2 * n)
                for k in range(2):
                    last = mm(ps[:, 4, 0:w], w2[:, k, :], o1T[:, k, i:i + w], start=(k == 0), stop=(k == 1))
                last.then_inc(m2_ps, 1)

            def mlp3(n):
                i, w = CH[n]
                pe.wait_ge(m2_ready, n + 1)
                for m in range(2):
                    mm(ps[:, 5 - m, 0:w], w3[:, bass.ts(m, P)], o2T[:, i:i + w], start=True, stop=True).then_inc(m3_ps, 1)

            def mlp4(t):
                pe.wait_ge(m3_ready, 2 * (t // KD + 1))
                if t >= 2:
                    pe.wait_ge(m4_read, t - 1)
                for k in range(2):
                    last = mm(ps[:, 6 + t % 2, :], o3T[:, k, bass.ts(t, P)], w4[:, k, :], start=(k == 0), stop=(k == 1))
                last.then_inc(m4_ps, 1)

            def turn_x3(t):
                pe.wait_ge(x3_ready, t + 1)
                if t >= 2:
                    pe.wait_ge(x3T_ready, t - 1)
                for k in range(KD):
                    last = tr(ps[:, t % 2, bass.ts(k, P)], r_x[:, t, bass.ts(k, P)], ident[:])
                last.then_inc(x3T_ps, 1)

            def value(t):
                pe.wait_ge(x3T_ready, t + 1)
                if t == 0:
                    pe.wait_ge(wv_ready, 1)
                if t >= 2:
                    pe.wait_ge(v_lo, t - 1)
                parts(ps[:, V_BANK[t % 2], :], lambda a, k: x3T[:, a, k, bass.ts(t, P)], lambda a, k: wv_parts[:, a, k, :],
                      range(KD)).then_inc(v_ps, 1)

            for t in range(4):
                turn_enc(t)
            mlp1(0)
            for t in range(4, 8):
                turn_enc(t)
            mlp2(0)
            mlp1(1)
            mlp3(0)
            mlp4(0)
            mlp4(1)
            for t in range(8, T):
                turn_enc(t)
            mlp2(1)
            mlp4(2)
            mlp1(2)
            mlp3(1)
            pe.wait_ge(encT_ready, T)
            mlp4(3)
            turn_x3(0)
            turn_x3(1)
            mlp2(2)
            mlp4(4)
            turn_x3(2)
            mlp3(2)
            mlp4(5)
            turn_x3(3)
            pe.wait_ge(m3_ready, 6)
            value(0)
            value(1)
            for t in range(6, T + 2):
                if t < T:
                    mlp4(t)
                turn_x3(t - 2)
                value(t - 4)

            def make_g(t):
                if at_least(t, 1):
                    pe.wait_ge(g_read, t)
                for m in range(KD):
                    last = parts(ps[:, 6, bass.ts(m, P)], lambda a, k: m_parts[:, a, k, bass.ts(m, P)],
                                 lambda a, k: x3T[:, a, k, bass.ts(t, P)], range(KD))
                last.then_inc(g_ps, 1)

            def score(t, b):
                pe.wait_ge(g_lo, t + 1)
                if at_least(t, 1):
                    pe.wait_ge(sc_read, t)
                for n, (i, w) in enumerate(CHN):
                    last = parts(ps[:, n, 0:w], lambda a, k: g_parts[:, b, a, k, :], lambda a, k: x3T[:, a, k, i:i + w],
                                 range(KD))
                last.then_inc(sc_ps, 1)

            def turn_p(t, b):
                pe.wait_ge(p3_ready, t + 1)
                if at_least(t, 1):
                    pe.wait_ge(pt3_lo, t)
                for j in range(T):
                    last = tr(ps[:, 3 + j // KD, bass.ts(j % KD, P)], S3[:, b, bass.ts(j, P)], ident[:])
                last.then_inc(pt3_ps, 1)

            def weigh_v(t, b):
                pe.wait_ge(pt3_lo, t + 1)
                if at_least(t, 1):
                    pe.wait_ge(o3_read, t)
                parts(ps[:, 7, :], lambda a, j: PT3[:, b, a, bass.ts(j, P)], lambda a, j: vv[:, a, j, :],
                      range(T)).then_inc(o3_ps, 1)

            def last_tile(t, b, n):
                turn_p(t, b)
                if before_end(t, 1):
                    score(t + 1, 1 - b)
                if before_end(t, 3):
                    make_g(t + 3)
                weigh_v(t, b)

            pe.wait_ge(m_ready, 1)
            pe.wait_ge(m4_read, T)
            make_g(0)
            make_g(1)
            pe.wait_ge(x3T_ready, T)
            score(0, 0)
            value(T - 2)
            value(T - 1)
            make_g(2)
            pe.wait_ge(v_lo, T)
            last_tiles(last_tile)(pe)


_OUT = (N, D)


def kernel(**inputs):
    import numpy as _np
    import concourse.bacc as _bacc
    from concourse import mybir as _mybir
    from concourse.bass_utils import run_bass_kernel_spmd as _run

    f = {k: _np.asarray(a) for k, a in inputs.items()}
    pad = NP - N
    lay = {
        "adjT": _np.pad(f["adj"].T, ((0, pad), (0, pad))),
        "adj": _np.pad(f["adj"], ((0, pad), (0, pad))),
        "xT": _np.pad(f["x"].T, ((0, 0), (0, pad))),
        "x": _np.pad(f["x"], ((0, pad), (0, 0))),
        "scal": _np.broadcast_to(_np.stack([f["L0_gnn_adj_scaling_factor"], f["L0_gnn_wgt_alpha"], f["L0_gnn_act_alpha"],
                                            f["L0_gnn_act_alpha2"]]), (P, 4)),
        "w0": f["L0_gnn_weight"],
        "gat_w": f["L2_gnn_W"].transpose(1, 0, 2).reshape(D, D),
        "gat_a": _np.stack([f["L2_gnn_a1"], f["L2_gnn_a2"]]).reshape(1, 2 * D),
        "w1T": f["L2_gnn_W1"].T, "w2T": f["L2_gnn_W2"].T, "w3T": f["L2_gnn_W3"].T, "w4T": f["L2_gnn_W4"].T,
        "b1": f["L2_gnn_b1"].reshape(-1, P).T, "b2": f["L2_gnn_b2"].reshape(-1, P).T, "b3": f["L2_gnn_b3"].reshape(-1, P).T,
        "b4": f["L2_gnn_b4"].reshape(1, D),
        "wq": f["L3_gnn_W_q"], "wk": f["L3_gnn_W_k"], "wvT": f["L3_gnn_W_v"].T,
        "bq": f["L3_gnn_b_q"].reshape(-1, P).T, "bk": f["L3_gnn_b_k"].reshape(-1, P).T, "bv": f["L3_gnn_b_v"].reshape(1, D),
    }
    nc = _bacc.Bacc("TRN2", target_bir_lowering=False, num_devices=1)
    arrays, args = {}, []
    for name, a in lay.items():
        a = _np.ascontiguousarray(a)
        arrays[f"in_{name}_dram"] = a
        args.append(nc.dram_tensor(f"in_{name}_dram", a.shape, _mybir.dt.from_np(a.dtype), kind="ExternalInput").ap())
    args.append(nc.dram_tensor("out_0_dram", _OUT, F32, kind="ExternalOutput").ap())
    build(nc, *args)
    r = _run(nc, [arrays], core_ids=[0])
    return r.results[0]["out_0_dram"]
```
